# Optimizing a Trainium2 kernel written in Bass

```python
import numpy as np
import jax
import jax.numpy as jnp

def _softmax(x, axis=-1):
    return jax.nn.softmax(x, axis=axis)

def _gelu(x):
    return jax.nn.gelu(x, approximate=True)

def _silu(x):
    return jax.nn.silu(x)

def _sigmoid(x):
    return jax.nn.sigmoid(x)

def _layernorm(x, axis=-1, eps=1e-05):
    m = jnp.mean(x, axis=axis, keepdims=True)
    v = jnp.var(x, axis=axis, keepdims=True)
    return (x - m) / jnp.sqrt(v + eps)

def _scatter_add(tgt, idx, src, axis=0):
    return tgt.at[idx].add(src)

def _segment_sum(src, seg, n):
    return jax.ops.segment_sum(src, seg, n)
kernel_name = 'mk_conv_attn_hybrid_d2_conv_nchw512_r2_86bd14'

def setup_inputs(seed: int=0):
    np.random.seed(seed)
    _w = jnp.asarray

    def _rec_inputs():
        import jax
        import jax.numpy as jnp
        _gk = jax.random.key(seed)
        x = 7.22e-05 + 1 * jax.random.normal(jax.random.fold_in(_gk, 1), (4, 256, 32, 32), jnp.float32)
        return x
    x = _rec_inputs()

    def _L0_conv_setup():
        import jax, jax.numpy as jnp
        import numpy as np
        NUM_GROUPS = 32
        EPS = 1e-06

        def group_norm(x, gamma, beta):
            b, c, h, w = x.shape
            g = NUM_GROUPS
            xr = x.reshape(b, g, c // g, h, w)
            mean = xr.mean(axis=(2, 3, 4), keepdims=True)
            var = xr.var(axis=(2, 3, 4), keepdims=True)
            xn = (xr - mean) * jax.lax.rsqrt(var + EPS)
            xn = xn.reshape(b, c, h, w)
            return xn * gamma[None, :, None, None] + beta[None, :, None, None]

        def conv1x1(x, w, bias):
            return jnp.einsum('oc,bchw->bohw', w, x) + bias[None, :, None, None]
        key = jax.random.key(seed)
        ks = jax.random.split(key, 11)
        c = 256
        x = jax.random.normal(ks[0], (4, c, 32, 32), dtype=jnp.float32)
        s = 1.0 / np.sqrt(c)
        params = {'norm_gamma': jnp.ones((c,), jnp.float32), 'norm_beta': jnp.zeros((c,), jnp.float32), 'wq': jax.random.normal(ks[1], (c, c), jnp.float32) * s, 'bq': jax.random.normal(ks[2], (c,), jnp.float32) * 0.01, 'wk': jax.random.normal(ks[3], (c, c), jnp.float32) * s, 'bk': jax.random.normal(ks[4], (c,), jnp.float32) * 0.01, 'wv': jax.random.normal(ks[5], (c, c), jnp.float32) * s, 'bv': jax.random.normal(ks[6], (c,), jnp.float32) * 0.01, 'wp': jax.random.normal(ks[7], (c, c), jnp.float32) * s, 'bp': jax.random.normal(ks[8], (c,), jnp.float32) * 0.01}
        return {'x': x, **params}
    _L0_conv_all = _L0_conv_setup()
    _L0_conv_in = {k: v for k, v in _L0_conv_all.items() if k in ('norm_gamma', 'norm_beta', 'wq', 'bq', 'wk', 'bk', 'wv', 'bv', 'wp', 'bp')}
    del _L0_conv_all

    def _L1_attn_setup():
        import jax, jax.numpy as jnp
        import numpy as np
        import math
        C = 1.0
        N_HEADS = 8
        EPS_BALL = 1e-05

        def _log0(y, c=C):
            n = jnp.clip(jnp.linalg.norm(y, axis=-1, keepdims=True), 1e-06, 1.0 - 1e-05)
            sc = math.sqrt(c)
            return jnp.arctanh(sc * n) * y / (sc * n)

        def _exp0(v, c=C):
            n = jnp.maximum(jnp.linalg.norm(v, axis=-1, keepdims=True), 1e-06)
            sc = math.sqrt(c)
            return jnp.tanh(sc * n) * v / (sc * n)

        def _project_to_ball(x, c=C, eps=EPS_BALL):
            max_norm = (1.0 - eps) / math.sqrt(c)
            n = jnp.linalg.norm(x, axis=-1, keepdims=True)
            return x * (max_norm / jnp.maximum(n, max_norm))

        def _hyperbolic_linear(x, w, c=C):
            t = _log0(x, c)
            o = jnp.einsum('btd,ed->bte', t, w)
            return _project_to_ball(_exp0(o, c), c)

        def _rms_norm(x, w):
            eps = jnp.finfo(x.dtype).eps
            return x * jax.lax.rsqrt(jnp.mean(x * x, axis=-1, keepdims=True) + eps) * w
        key = jax.random.key(seed)
        ks = jax.random.split(key, 9)
        B, T, D = (4, 512, 256)
        FF = 2 * D
        f32 = jnp.float32
        return {'x': jax.random.normal(ks[0], (B, T, D), f32), 'q_w': jax.random.normal(ks[1], (D, D), f32) * 0.0002, 'k_w': jax.random.normal(ks[2], (D, D), f32) * 0.0002, 'v_w': jax.random.normal(ks[3], (D, D), f32) * 0.02, 'o_w': jax.random.normal(ks[4], (D, D), f32) * 0.02, 'gate_w': jax.random.normal(ks[5], (FF, D), f32) * 0.02, 'up_w': jax.random.normal(ks[6], (FF, D), f32) * 0.02, 'down_w': jax.random.normal(ks[7], (D, FF), f32) * 0.02, 'norm1_w': jnp.ones((D,), f32), 'norm2_w': jnp.ones((D,), f32)}
    _L1_attn_all = _L1_attn_setup()
    _L1_attn_in = {k: v for k, v in _L1_attn_all.items() if k in ('q_w', 'k_w', 'v_w', 'o_w', 'gate_w', 'up_w', 'down_w', 'norm1_w', 'norm2_w')}
    del _L1_attn_all

    def _L1_ffn_setup():
        import jax, jax.numpy as jnp
        import numpy as np
        B, S, D = (8, 1024, 256)
        E, K, H = (8, 2, 1024)
        key = jax.random.key(seed)
        ks = jax.random.split(key, 6)
        scale = 0.02
        return {'x': jax.random.normal(ks[0], (B, S, D), dtype=jnp.float32), 'gate_w': jax.random.normal(ks[1], (E, D), dtype=jnp.float32) * scale, 'w1': jax.random.normal(ks[2], (E, H, D), dtype=jnp.float32) * scale, 'b1': jax.random.normal(ks[3], (E, H), dtype=jnp.float32) * scale, 'w2': jax.random.normal(ks[4], (E, D, H), dtype=jnp.float32) * scale, 'b2': jax.random.normal(ks[5], (E, D), dtype=jnp.float32) * scale}
    _L1_ffn_all = _L1_ffn_setup()
    _L1_ffn_in = {k: v for k, v in _L1_ffn_all.items() if k in ('gate_w', 'w1', 'b1', 'w2', 'b2')}
    del _L1_ffn_all
    return {'x': x, 'L0_conv_norm_gamma': _L0_conv_in['norm_gamma'], 'L0_conv_norm_beta': _L0_conv_in['norm_beta'], 'L0_conv_wq': _L0_conv_in['wq'], 'L0_conv_bq': _L0_conv_in['bq'], 'L0_conv_wk': _L0_conv_in['wk'], 'L0_conv_bk': _L0_conv_in['bk'], 'L0_conv_wv': _L0_conv_in['wv'], 'L0_conv_bv': _L0_conv_in['bv'], 'L0_conv_wp': _L0_conv_in['wp'], 'L0_conv_bp': _L0_conv_in['bp'], 'L1_attn_q_w': _L1_attn_in['q_w'], 'L1_attn_k_w': _L1_attn_in['k_w'], 'L1_attn_v_w': _L1_attn_in['v_w'], 'L1_attn_o_w': _L1_attn_in['o_w'], 'L1_attn_gate_w': _L1_attn_in['gate_w'], 'L1_attn_up_w': _L1_attn_in['up_w'], 'L1_attn_down_w': _L1_attn_in['down_w'], 'L1_attn_norm1_w': _L1_attn_in['norm1_w'], 'L1_attn_norm2_w': _L1_attn_in['norm2_w'], 'L1_ffn_gate_w': _L1_ffn_in['gate_w'], 'L1_ffn_w1': _L1_ffn_in['w1'], 'L1_ffn_b1': _L1_ffn_in['b1'], 'L1_ffn_w2': _L1_ffn_in['w2'], 'L1_ffn_b2': _L1_ffn_in['b2']}

def reference(x, L0_conv_norm_gamma, L0_conv_norm_beta, L0_conv_wq, L0_conv_bq, L0_conv_wk, L0_conv_bk, L0_conv_wv, L0_conv_bv, L0_conv_wp, L0_conv_bp, L1_attn_q_w, L1_attn_k_w, L1_attn_v_w, L1_attn_o_w, L1_attn_gate_w, L1_attn_up_w, L1_attn_down_w, L1_attn_norm1_w, L1_attn_norm2_w, L1_ffn_gate_w, L1_ffn_w1, L1_ffn_b1, L1_ffn_w2, L1_ffn_b2):
    import jax
    import jax.numpy as jnp

    def _L0_conv_ref(x, norm_gamma, norm_beta, wq, bq, wk, bk, wv, bv, wp, bp):
        import jax, jax.numpy as jnp
        import numpy as np
        NUM_GROUPS = 32
        EPS = 1e-06

        def group_norm(x, gamma, beta):
            b, c, h, w = x.shape
            g = NUM_GROUPS
            xr = x.reshape(b, g, c // g, h, w)
            mean = xr.mean(axis=(2, 3, 4), keepdims=True)
            var = xr.var(axis=(2, 3, 4), keepdims=True)
            xn = (xr - mean) * jax.lax.rsqrt(var + EPS)
            xn = xn.reshape(b, c, h, w)
            return xn * gamma[None, :, None, None] + beta[None, :, None, None]

        def conv1x1(x, w, bias):
            return jnp.einsum('oc,bchw->bohw', w, x) + bias[None, :, None, None]
        b, c, h, w = x.shape
        hn = group_norm(x, norm_gamma, norm_beta)
        q = conv1x1(hn, wq, bq).reshape(b, c, h * w)
        k = conv1x1(hn, wk, bk).reshape(b, c, h * w)
        v = conv1x1(hn, wv, bv).reshape(b, c, h * w)
        scale = jnp.asarray(c, x.dtype) ** (-0.5)
        scores = jnp.einsum('bci,bcj->bij', q, k) * scale
        attn = jax.nn.softmax(scores, axis=2)
        out = jnp.einsum('bcj,bij->bci', v, attn).reshape(b, c, h, w)
        out = conv1x1(out, wp, bp)
        return x + out

    def _L1_attn_ref(x, q_w, k_w, v_w, o_w, gate_w, up_w, down_w, norm1_w, norm2_w):
        import jax, jax.numpy as jnp
        import numpy as np
        import math
        C = 1.0
        N_HEADS = 8
        EPS_BALL = 1e-05

        def _log0(y, c=C):
            n = jnp.clip(jnp.linalg.norm(y, axis=-1, keepdims=True), 1e-06, 1.0 - 1e-05)
            sc = math.sqrt(c)
            return jnp.arctanh(sc * n) * y / (sc * n)

        def _exp0(v, c=C):
            n = jnp.maximum(jnp.linalg.norm(v, axis=-1, keepdims=True), 1e-06)
            sc = math.sqrt(c)
            return jnp.tanh(sc * n) * v / (sc * n)

        def _project_to_ball(x, c=C, eps=EPS_BALL):
            max_norm = (1.0 - eps) / math.sqrt(c)
            n = jnp.linalg.norm(x, axis=-1, keepdims=True)
            return x * (max_norm / jnp.maximum(n, max_norm))

        def _hyperbolic_linear(x, w, c=C):
            t = _log0(x, c)
            o = jnp.einsum('btd,ed->bte', t, w)
            return _project_to_ball(_exp0(o, c), c)

        def _rms_norm(x, w):
            eps = jnp.finfo(x.dtype).eps
            return x * jax.lax.rsqrt(jnp.mean(x * x, axis=-1, keepdims=True) + eps) * w
        B, T, D = x.shape
        H = N_HEADS
        hd = D // H
        h = _rms_norm(x, norm1_w)
        h_ball = _project_to_ball(h * 0.5)
        q = _hyperbolic_linear(h_ball, q_w).reshape(B, T, H, hd).transpose(0, 2, 1, 3)
        k = _hyperbolic_linear(h_ball, k_w).reshape(B, T, H, hd).transpose(0, 2, 1, 3)
        v = jnp.einsum('btd,ed->bte', h, v_w).reshape(B, T, H, hd).transpose(0, 2, 1, 3)
        q2 = jnp.sum(q * q, axis=-1)
        k2 = jnp.sum(k * k, axis=-1)
        qk = jnp.einsum('bhqd,bhkd->bhqk', q, k)
        attn = -(q2[..., :, None] + k2[..., None, :] - 2.0 * qk) / math.sqrt(hd)
        causal = jnp.tril(jnp.ones((T, T), dtype=bool))
        attn = jnp.where(causal, attn, -jnp.inf)
        attn = jax.nn.softmax(attn, axis=-1)
        out = jnp.einsum('bhqk,bhkd->bhqd', attn, v).transpose(0, 2, 1, 3).reshape(B, T, D)
        x = x + jnp.einsum('btd,ed->bte', out, o_w)
        h2 = _rms_norm(x, norm2_w)
        gate = jnp.einsum('btd,fd->btf', h2, gate_w)
        up = jnp.einsum('btd,fd->btf', h2, up_w)
        ff = jnp.einsum('btf,df->btd', jax.nn.silu(gate) * up, down_w)
        return x + ff

    def _L1_ffn_ref(x, gate_w, w1, b1, w2, b2):
        import jax, jax.numpy as jnp
        import numpy as np
        B, S, D = (8, 1024, 256)
        E, K, H = (8, 2, 1024)
        batch, seq, dim = x.shape
        x_flat = x.reshape(-1, dim)
        T = x_flat.shape[0]
        gate_logits = x_flat @ gate_w.T
        topk_vals, topk_idx = jax.lax.top_k(gate_logits, K)
        topk_w = jax.nn.softmax(topk_vals, axis=-1)
        comb = jnp.zeros((T, E), dtype=x_flat.dtype)
        comb = comb.at[jnp.arange(T)[:, None], topk_idx].add(topk_w)
        out = jnp.zeros_like(x_flat)
        for e in range(E):
            h = jax.nn.gelu(x_flat @ w1[e].T + b1[e], approximate=False)
            y = h @ w2[e].T + b2[e]
            out = out + comb[:, e:e + 1] * y
        return out.reshape(batch, seq, dim)

    def _gn(v, G=32, eps=1e-05):
        B_, C_, H_, W_ = v.shape
        g = v.reshape(B_, G, C_ // G, H_, W_)
        m = jnp.mean(g, axis=(2, 3, 4), keepdims=True)
        s = jnp.var(g, axis=(2, 3, 4), keepdims=True)
        return ((g - m) / jnp.sqrt(s + eps)).reshape(v.shape)

    def _ln_c(v, eps=1e-06):
        m = jnp.mean(v, axis=1, keepdims=True)
        s = jnp.var(v, axis=1, keepdims=True)
        return (v - m) / jnp.sqrt(s + eps)

    def _ln_t(v, eps=1e-05):
        m = jnp.mean(v, axis=-1, keepdims=True)
        s = jnp.var(v, axis=-1, keepdims=True)
        return (v - m) / jnp.sqrt(s + eps)

    def _to_tokens(v):
        B_, C_, H_, W_ = v.shape
        return v.reshape(B_, C_, H_ * W_).transpose(0, 2, 1)

    def _from_tokens(t, like):
        B_, C_, H_, W_ = like.shape
        return t.transpose(0, 2, 1).reshape(B_, C_, H_, W_)
    x = _L0_conv_ref(x, L0_conv_norm_gamma, L0_conv_norm_beta, L0_conv_wq, L0_conv_bq, L0_conv_wk, L0_conv_bk, L0_conv_wv, L0_conv_bv, L0_conv_wp, L0_conv_bp)
    t = _to_tokens(x)
    t = t + _L1_attn_ref(_ln_t(t), L1_attn_q_w, L1_attn_k_w, L1_attn_v_w, L1_attn_o_w, L1_attn_gate_w, L1_attn_up_w, L1_attn_down_w, L1_attn_norm1_w, L1_attn_norm2_w)
    t = t + _L1_ffn_ref(_ln_t(t), L1_ffn_gate_w, L1_ffn_w1, L1_ffn_b1, L1_ffn_w2, L1_ffn_b2)
    x = _from_tokens(t, x)
    return x

_drawn_inputs = setup_inputs


def setup_inputs(seed=0):
    import zlib

    import numpy as np

    out = dict(_drawn_inputs(seed))
    spreads = {'L0_conv_norm_gamma': (1.0, 0.2),
     'L0_conv_norm_beta': (0.0, 0.1),
     'L1_attn_norm1_w': (1.0, 0.6),
     'L1_attn_norm2_w': (1.0, 0.6)}
    factors = {'L0_conv_bq': 8.0,
     'L0_conv_bk': 200.0,
     'L0_conv_bv': 5.289,
     'L0_conv_bp': 5.598,
     'L1_attn_q_w': 200.0,
     'L1_attn_k_w': 200.0,
     'L1_attn_v_w': 7.19,
     'L1_attn_o_w': 6.747,
     'L1_attn_gate_w': 4.317,
     'L1_attn_up_w': 4.249,
     'L1_attn_down_w': 4.262,
     'L1_ffn_b1': 64.0,
     'L1_ffn_b2': 24.37,
     'L1_ffn_gate_w': 3.026,
     'L1_ffn_w1': 4.678,
     'L1_ffn_w2': 4.056}
    for name, (base, spread) in spreads.items():
        noise = np.random.default_rng([zlib.crc32(name.encode()), seed]).standard_normal(out[name].shape)
        drawn = base * np.exp(spread * noise) if base else spread * noise
        out[name] = jnp.asarray(drawn.astype(out[name].dtype))
    for name, factor in factors.items():
        out[name] = (out[name] * factor).astype(out[name].dtype)
    return out
```

```python
from contextlib import ExitStack

import concourse.bass as bass
from concourse import mybir

F32 = mybir.dt.float32
F32R = mybir.dt.float32r
F16 = mybir.dt.float16
U32 = mybir.dt.uint32
ALU = mybir.AluOpType
ACT = mybir.ActivationFunctionType
AX = mybir.AxisListType

P = 128
B = 4
C = 256
T = 1024
CC = C // P
GROUP = 8
QB = T // P
GQ = 4
NG = QB // GQ
GN_EPS = 1e-6
LN_EPS = 1e-5


class Scope:

    def __init__(self, nc, ctx, tag):
        self.nc, self.ctx, self.tag = nc, ctx, tag
        self.sems = []

    def sb(self, name, shape, dt=F32):
        return self.ctx.enter_context(self.nc.sbuf_tensor(f"{self.tag}_{name}", shape, dt))

    def ps(self, name, shape, dt=F32):
        return self.ctx.enter_context(self.nc.psum_tensor(f"{self.tag}_{name}", shape, dt))

    def sem(self, name):
        sem = self.ctx.enter_context(self.nc.semaphore(f"{self.tag}_{name}"))
        self.sems.append(sem)
        return sem

    def clear(self):
        with self.nc.Block() as block:

            @block.gpsimd
            def _(pool):
                for sem in self.sems:
                    pool.sem_clear(sem)


def make_constants(nc, ident, ident_h, group_mean):
    with ExitStack() as ctx:
        s = Scope(nc, ctx, "const")
        filled, selected = s.sem("filled"), s.sem("selected")
        with nc.Block() as block:

            @block.gpsimd
            def _(pool):
                pool.memset(ident[:, :], 0.0).then_inc(filled, 1)
                pool.memset(group_mean[:, :], 1.0 / GROUP).then_inc(filled, 1)
                pool.wait_ge(filled, 2)
                pool.affine_select(out=ident[:, :], in_=ident[:, :], compare_op=ALU.not_equal, fill=1.0,
                                   base=0, pattern=[[-1, P]], channel_multiplier=1).then_inc(selected, 1)
                gm = group_mean[:, :].rearrange("p (g r) -> p g r", r=GROUP)
                pool.affine_select(out=gm, in_=gm, compare_op=ALU.is_ge, fill=0.0, base=0,
                                   pattern=[[-GROUP, P // GROUP], [0, GROUP]],
                                   channel_multiplier=1).then_inc(selected, 1)
                pool.wait_ge(selected, 2)
                pool.affine_select(out=gm, in_=gm, compare_op=ALU.is_ge, fill=0.0, base=GROUP - 1,
                                   pattern=[[GROUP, P // GROUP], [0, GROUP]],
                                   channel_multiplier=-1).then_inc(selected, 1)
                pool.tensor_copy(ident_h[:, :], ident[:, :]).then_inc(selected, 1)
                pool.wait_ge(selected, 4)
        s.clear()


def prepare_weights(nc, tag, units, ident):
    with ExitStack() as ctx:
        s = Scope(nc, ctx, tag)
        widest = max(w.shape[0] // P * w.shape[1] for w, _, _ in units)
        natural = [s.sb(f"natural{i}", [P, widest]) for i in range(3)]
        turned = [s.ps(f"turned{i}", [P, 512]) for i in range(3)]
        loaded = [s.sem(f"loaded{i}") for i in range(3)]
        turned_full, unit_read, hi_done, lo_done = (s.sem(n) for n in ("turned_full", "unit_read", "hi_done", "lo_done"))
        strips = [(u, k) for u, (w, _, _) in enumerate(units) for k in range(w.shape[1] // P)]

        def view(u):
            w = units[u][0]
            return natural[u % 3][:, 0:w.shape[0] // P * w.shape[1]].rearrange("p (o i) -> p o i", i=w.shape[1])

        with nc.Block() as block:

            @block.sync
            def _(sp):
                for u, (w, _, _) in enumerate(units):
                    if u >= 3:
                        sp.wait_ge(unit_read, u - 2)
                    sp.dma_start(view(u), w.rearrange("(o p) i -> p o i", p=P)).then_inc(loaded[u % 3], 16)

            @block.tensor
            def _(pe):
                for n, (u, k) in enumerate(strips):
                    w = units[u][0]
                    if k == 0:
                        pe.wait_ge(loaded[u % 3], 16 * (u // 3 + 1))
                    if n >= 3:
                        pe.wait_ge(lo_done, n - 2)
                    for o in range(w.shape[0] // P):
                        last = pe.transpose(turned[n % 3][:, o * P:(o + 1) * P], view(u)[:, o, k * P:(k + 1) * P], ident[:, :])
                    last.then_inc(turned_full, 1)
                    if k == w.shape[1] // P - 1:
                        pe.wait_ge(turned_full, n + 1)
                        pe.sem_inc(unit_read, 1)

            @block.scalar
            def _(act):
                for n, (u, k) in enumerate(strips):
                    w, hi, _ = units[u]
                    act.wait_ge(turned_full, n + 1)
                    act.activation(hi[:, k, :], turned[n % 3][:, 0:w.shape[0]], ACT.Copy).then_inc(hi_done, 1)

            @block.vector
            def _(dve):
                for n, (u, k) in enumerate(strips):
                    w, hi, lo = units[u]
                    dve.wait_ge(hi_done, n + 1)
                    dve.tensor_tensor(lo[:, k, :], turned[n % 3][:, 0:w.shape[0]], hi[:, k, :].bitcast(F32),
                                      ALU.subtract).then_inc(lo_done, 1)
                dve.wait_ge(lo_done, len(strips))
        s.clear()


def group_norm_affine(nc, x, xs, gamma, beta, group_mean, scale, shift):
    with ExitStack() as ctx:
        s = Scope(nc, ctx, "gn")
        stats = s.sb("stats", [P, B, CC, 2, 6])
        moments = s.sb("moments", [P, B, CC, 2])
        square = s.sb("square", [P, B, CC])
        var = s.sb("var", [P, B, CC])
        std = s.sb("std", [P, B, CC])
        gb = s.sb("gb", [P, 2, CC])
        mean_ps = s.ps("mean_ps", [P, B, CC, 2])
        loaded = [s.sem(f"loaded{b}") for b in range(B)]
        gb_loaded, stats_done, chain, averaged, rooted = (s.sem(n) for n in ("gb_loaded", "stats_done", "chain", "averaged", "rooted"))
        with nc.Block() as block:

            @block.sync
            def _(sp):
                for b in range(B):
                    for c in range(CC):
                        sp.dma_start(xs[:, b, c, :], x[b, c * P:(c + 1) * P].rearrange("p h w -> p (h w)")).then_inc(loaded[b], 16)
                sp.dma_start(gb[:, 0, :], gamma.rearrange("(c p) -> p c", p=P), allow_slow_non_contiguous=True).then_inc(gb_loaded, 16)
                sp.dma_start(gb[:, 1, :], beta.rearrange("(c p) -> p c", p=P), allow_slow_non_contiguous=True).then_inc(gb_loaded, 16)

            @block.tensor
            def _(pe):
                pe.wait_ge(chain, 3)
                pe.matmul(mean_ps[:, :, :, :], group_mean[:, :], moments[:, :, :, :], start=True, stop=True).then_inc(averaged, 1)

            @block.scalar
            def _(act):
                act.wait_ge(chain, 6)
                act.activation(std[:, :, :], var[:, :, :], ACT.Sqrt).then_inc(rooted, 1)

            @block.vector
            def _(dve):
                for b in range(B):
                    dve.wait_ge(loaded[b], 16 * CC)
                    for c in range(CC):
                        for h in range(2):
                            dve.bn_stats(stats[:, b, c, h, :], xs[:, b, c, h * 512:(h + 1) * 512]).then_inc(stats_done, 1)
                    dve.wait_ge(stats_done, (b + 1) * CC * 2 + b * CC)
                    for c in range(CC):
                        dve.bn_aggr(moments[:, b, c, :], stats[:, b, c, :, :]).then_inc(stats_done, 1)
                dve.wait_ge(stats_done, 3 * B * CC)
                dve.tensor_tensor(square[:, :, :], moments[:, :, :, 0], moments[:, :, :, 0], ALU.mult).then_inc(chain, 1)
                dve.wait_ge(chain, 1)
                dve.tensor_tensor(moments[:, :, :, 1], moments[:, :, :, 1], square[:, :, :], ALU.add).then_inc(chain, 2)
                dve.wait_ge(averaged, 1)
                dve.tensor_copy(moments[:, :, :, :], mean_ps[:, :, :, :]).then_inc(chain, 1)
                dve.wait_ge(chain, 4)
                dve.tensor_tensor(square[:, :, :], moments[:, :, :, 0], moments[:, :, :, 0], ALU.mult).then_inc(chain, 1)
                dve.wait_ge(chain, 5)
                dve.scalar_tensor_tensor(var[:, :, :], moments[:, :, :, 1], GN_EPS, square[:, :, :], ALU.add, ALU.subtract).then_inc(chain, 1)
                dve.wait_ge(rooted, 1)
                dve.reciprocal(var[:, :, :], std[:, :, :]).then_inc(chain, 1)
                dve.wait_ge(chain, 7)
                dve.wait_ge(gb_loaded, 32)
                for b in range(B):
                    dve.tensor_tensor(scale[:, b, :], var[:, b, :], gb[:, 0, :], ALU.mult).then_inc(chain, 1)
                dve.wait_ge(chain, 7 + B)
                dve.tensor_tensor(square[:, :, :], moments[:, :, :, 0], scale[:, :, :], ALU.mult).then_inc(chain, 1)
                dve.wait_ge(chain, 8 + B)
                for b in range(B):
                    dve.tensor_tensor(shift[:, b, :], gb[:, 1, :], square[:, b, :], ALU.subtract).then_inc(chain, 1)
                dve.wait_ge(chain, 8 + 2 * B)
        s.clear()


def split_product(pe, out, pairs, start=True, stop=True):
    n = 3 * len(pairs)
    k = 0
    for ah, al, bh, bl in pairs:
        for a, b in ((ah, bh), (ah, bl), (al, bh)):
            last = pe.matmul(out, a, b, start=start and k == 0, stop=stop and k == n - 1)
            k += 1
    return last


def conv_attention(nc, xs, scale, shift, ident, w, bq, bk, bv, bp):
    SCALE = float(C) ** -0.5
    UNITS = 12 + 4 * NG
    SPLIT = 12 + 2 * NG
    with ExitStack() as ctx:
        s = Scope(nc, ctx, "conv")
        hn = s.sb("hn", [P, CC, T])
        hn_hi, hn_lo = s.sb("hn_hi", [P, CC, T], F32R), s.sb("hn_lo", [P, CC, T], F32R)
        q_hi, q_lo = s.sb("q_hi", [P, CC, T], F32R), s.sb("q_lo", [P, CC, T], F32R)
        k_hi, k_lo = s.sb("k_hi", [P, CC, T], F32R), s.sb("k_lo", [P, CC, T], F32R)
        v_hi, v_lo = s.sb("v_hi", [P, QB, C], F32R), s.sb("v_lo", [P, QB, C], F32R)
        probs = [s.sb(f"probs{i}", [P, T]) for i in range(2)]
        pt_hi, pt_lo = s.sb("pt_hi", [P, NG, QB, GQ * P], F32R), s.sb("pt_lo", [P, NG, QB, GQ * P], F32R)
        ao_hi, ao_lo = s.sb("ao_hi", [P, CC, GQ * P], F32R), s.sb("ao_lo", [P, CC, GQ * P], F32R)
        bias = s.sb("bias", [P, 4, CC])
        rowmax, negmax = s.sb("rowmax", [P, QB]), s.sb("negmax", [P, QB])
        rowsum, rowinv = s.sb("rowsum", [P, QB]), s.sb("rowinv", [P, QB])
        score = [s.ps(f"score{i}", [P, T]) for i in range(2)]
        turned = s.ps("turned", [P, QB, P])
        prod = [s.ps(f"prod{i}", [P, 512]) for i in range(2)]
        (bias_loaded, hn_ready, hn_act, hn_free, prod_full, unit_hi, unit_done, score_full, max_done, neg_done,
         exp_done, inv_done, probs_ready, turned_full, pt_hi_done, pt_lo_done, av_done, proj_done) = (
            s.sem(n) for n in ("bias_loaded", "hn_ready", "hn_act", "hn_free", "prod_full", "unit_hi", "unit_done",
                               "score_full", "max_done", "neg_done", "exp_done", "inv_done", "probs_ready",
                               "turned_full", "pt_hi_done", "pt_lo_done", "av_done", "proj_done"))

        proj_units = [(n, o, h) for n in ("q", "k") for o in range(CC) for h in range(2)]
        bias_of = {"q": 0, "k": 1}
        dest = {"q": (q_hi, q_lo), "k": (k_hi, k_lo)}
        U_V, U_AV = len(proj_units), 12

        def av_unit(g, c):
            return U_AV + 4 * g + c

        with nc.Block() as block:

            @block.sync
            def _(sp):
                for n, src in enumerate((bq, bk, bv, bp)):
                    sp.dma_start(bias[:, n, :], src.rearrange("(c p) -> p c", p=P), allow_slow_non_contiguous=True).then_inc(bias_loaded, 16)

            @block.tensor
            def _(pe):
                def free_bank(b, u):
                    pe.wait_ge(unit_done, b * UNITS + max(u - 1, 0))

                def qkv(b):
                    pe.wait_ge(hn_ready, (b + 1) * CC)
                    for u, (name, o, h) in enumerate(proj_units):
                        free_bank(b, u)
                        wh, wl = w[name]
                        cols, toks = slice(o * P, (o + 1) * P), slice(h * 512, (h + 1) * 512)
                        split_product(pe, prod[u % 2][:, :], [(wh[:, k, cols], wl[:, k, cols], hn_hi[:, k, toks], hn_lo[:, k, toks])
                                                              for k in range(CC)]).then_inc(prod_full, 1)
                    wh, wl = w["v"]
                    for n in range(QB // 2):
                        u = U_V + n
                        free_bank(b, u)
                        for t in (2 * n, 2 * n + 1):
                            toks = slice(t * P, (t + 1) * P)
                            last = split_product(pe, prod[u % 2][:, t % 2 * C:(t % 2 + 1) * C],
                                                 [(hn_hi[:, k, toks], hn_lo[:, k, toks], wh[:, k, :], wl[:, k, :]) for k in range(CC)])
                        last.then_inc(prod_full, 1)
                    pe.wait_ge(prod_full, b * UNITS + U_AV)
                    pe.sem_inc(hn_free, 1)

                def scores(b, i):
                    pe.wait_ge(exp_done, b * QB + max(i - 1, 0))
                    if i == 0:
                        pe.wait_ge(unit_done, b * UNITS + U_AV)
                    qs = slice(i * P, (i + 1) * P)
                    for h in range(2):
                        ks = slice(h * 512, (h + 1) * 512)
                        last = split_product(pe, score[i % 2][:, ks], [(q_hi[:, k, qs], q_lo[:, k, qs], k_hi[:, k, ks], k_lo[:, k, ks])
                                                                       for k in range(CC)])
                    last.then_inc(score_full, 1)

                def turn(b, i):
                    pe.wait_ge(probs_ready, b * QB + i + 1)
                    pe.wait_ge(pt_lo_done, b * QB + i)
                    for j in range(QB):
                        last = pe.transpose(turned[:, j, :], probs[i % 2][:, j * P:(j + 1) * P], ident[:, :])
                    last.then_inc(turned_full, 1)

                def av(b, g, c, half):
                    u = av_unit(g, c)
                    if half == 0:
                        free_bank(b, u)
                        pe.wait_ge(pt_lo_done, b * QB + (g + 1) * GQ)
                    cs = slice(c * P, (c + 1) * P)
                    js = range(half * QB // 2, (half + 1) * QB // 2)
                    last = split_product(pe, prod[u % 2][:, :], [(v_hi[:, j, cs], v_lo[:, j, cs], pt_hi[:, g, j, :], pt_lo[:, g, j, :])
                                                                 for j in js], start=half == 0, stop=half == 1)
                    if half == 1:
                        last.then_inc(prod_full, 1)

                def proj(b, g):
                    wh, wl = w["p"]
                    for o in range(CC):
                        u = av_unit(g, CC + o)
                        pe.wait_ge(unit_done, b * UNITS + av_unit(g, CC))
                        free_bank(b, u)
                        cols = slice(o * P, (o + 1) * P)
                        split_product(pe, prod[u % 2][:, :], [(wh[:, k, cols], wl[:, k, cols], ao_hi[:, k, :], ao_lo[:, k, :])
                                                              for k in range(CC)]).then_inc(prod_full, 1)

                def batch(b):
                    qkv(b)
                    scores(b, 0)
                    scores(b, 1)
                    for i in range(QB):
                        if i + 2 < QB:
                            scores(b, i + 2)
                        if i >= GQ:
                            av(b, 0, (i - GQ) // 2, (i - GQ) % 2)
                        turn(b, i)
                    proj(b, 0)
                    for q in range(4):
                        av(b, 1, q // 2, q % 2)
                    proj(b, 1)

                pe.wait_ge(bias_loaded, 64)
                batch(0)
                with pe.Fori(1, B) as b:
                    batch(b)

            def normalise(act, b):
                for c in range(CC):
                    act.activation(hn[:, c, :], xs[:, b, c, :], ACT.Identity, bias=shift[:, b, c:c + 1],
                                   scale=scale[:, b, c:c + 1]).then_inc(hn_act, 1)
                    act.wait_ge(hn_act, (2 * b * CC) + 2 * c + 1)
                    act.activation(hn_hi[:, c, :], hn[:, c, :], ACT.Copy).then_inc(hn_act, 1)

            @block.scalar
            def _(act):
                def hi(b, u, dst, bias_ap):
                    act.wait_ge(prod_full, b * UNITS + u + 1)
                    if bias_ap is None:
                        act.activation(dst, prod[u % 2][:, :], ACT.Copy).then_inc(unit_hi, 1)
                    else:
                        act.activation(dst, prod[u % 2][:, :], ACT.Identity, bias=bias_ap).then_inc(unit_hi, 1)

                def exps(b, i):
                    act.wait_ge(neg_done, b * QB + i + 1)
                    act.wait_ge(turned_full, b * QB + max(i - 1, 0))
                    act.activation(probs[i % 2][:, :], score[i % 2][:, :], ACT.Exp, bias=negmax[:, i:i + 1], scale=SCALE,
                                   accum_out=rowsum[:, i:i + 1]).then_inc(exp_done, 1)

                def pt(b, i):
                    act.wait_ge(turned_full, b * QB + i + 1)
                    act.wait_ge(av_done, b * NG)
                    act.activation(pt_hi[:, i // GQ, :, i % GQ * P:(i % GQ + 1) * P], turned[:, :, :], ACT.Copy).then_inc(pt_hi_done, 1)

                def ao(b, g, c):
                    act.wait_ge(proj_done, b * NG + g)
                    hi(b, av_unit(g, c), ao_hi[:, c, :], bias[:, 2, c:c + 1])

                def batch(b, last):
                    for u, (name, o, h) in enumerate(proj_units):
                        hi(b, u, dest[name][0][:, o, h * 512:(h + 1) * 512], bias[:, bias_of[name], o:o + 1])
                    for n in range(QB // 2):
                        hi(b, U_V + n, v_hi[:, 2 * n:2 * n + 2, :], None)
                    exps(b, 0)
                    exps(b, 1)
                    for i in range(QB):
                        if i + 2 < QB:
                            exps(b, i + 2)
                        pt(b, i)
                        if i == GQ + 1:
                            ao(b, 0, 0)
                    ao(b, 0, 1)
                    if not last:
                        act.wait_ge(hn_free, b + 1)
                        act.wait_ge(hn_ready, (b + 1) * CC)
                        normalise(act, b + 1)
                    ao(b, 1, 0)
                    ao(b, 1, 1)

                act.wait_ge(bias_loaded, 64)
                normalise(act, 0)
                batch(0, False)
                with act.Fori(1, B - 1) as b:
                    batch(b, False)
                batch(B - 1, True)

            @block.vector
            def _(dve):
                def normalise_lo(b):
                    for c in range(CC):
                        dve.wait_ge(hn_act, 2 * b * CC + 2 * c + 2)
                        dve.tensor_tensor(hn_lo[:, c, :], hn[:, c, :], hn_hi[:, c, :].bitcast(F32), ALU.subtract).then_inc(hn_ready, 1)

                def lo(b, u, n, dst, hi, bias_ap):
                    dve.wait_ge(unit_hi, b * SPLIT + n + 1)
                    if bias_ap is None:
                        dve.tensor_tensor(dst, prod[u % 2][:, :], hi.bitcast(F32), ALU.subtract).then_inc(unit_done, 1)
                    else:
                        dve.scalar_tensor_tensor(dst, prod[u % 2][:, :], bias_ap, hi.bitcast(F32), ALU.add, ALU.subtract).then_inc(unit_done, 1)

                def row_max(b, i):
                    dve.wait_ge(score_full, b * QB + i + 1)
                    dve.tensor_reduce(rowmax[:, i:i + 1], score[i % 2][:, :], AX.X, ALU.max).then_inc(max_done, 1)
                    dve.wait_ge(max_done, b * QB + i + 1)
                    dve.tensor_scalar(negmax[:, i:i + 1], rowmax[:, i:i + 1], -SCALE, None, ALU.mult).then_inc(neg_done, 1)

                def weigh(b, i):
                    dve.wait_ge(exp_done, b * QB + i + 1)
                    dve.reciprocal(rowinv[:, i:i + 1], rowsum[:, i:i + 1]).then_inc(inv_done, 1)
                    dve.wait_ge(inv_done, b * QB + i + 1)
                    dve.tensor_scalar(probs[i % 2][:, :], probs[i % 2][:, :], rowinv[:, i:i + 1], None, ALU.mult).then_inc(probs_ready, 1)

                def pt(b, i):
                    dve.wait_ge(pt_hi_done, b * QB + i + 1)
                    qs = slice(i % GQ * P, (i % GQ + 1) * P)
                    dve.tensor_tensor(pt_lo[:, i // GQ, :, qs], turned[:, :, :], pt_hi[:, i // GQ, :, qs].bitcast(F32), ALU.subtract).then_inc(pt_lo_done, 1)

                def ao(b, g, c):
                    lo(b, av_unit(g, c), 12 + 2 * g + c, ao_lo[:, c, :], ao_hi[:, c, :], bias[:, 2, c:c + 1])
                    if c == CC - 1:
                        dve.sem_inc(av_done, 1)

                def residual(b, g):
                    for o in range(CC):
                        u = av_unit(g, CC + o)
                        dve.wait_ge(prod_full, b * UNITS + u + 1)
                        xt = xs[:, b, o, g * 512:(g + 1) * 512]
                        dve.scalar_tensor_tensor(xt, prod[u % 2][:, :], bias[:, 3, o:o + 1], xt, ALU.add, ALU.add).then_inc(unit_done, 1)
                    dve.sem_inc(proj_done, 1)

                def batch(b, last):
                    for u, (name, o, h) in enumerate(proj_units):
                        hs = slice(h * 512, (h + 1) * 512)
                        lo(b, u, u, dest[name][1][:, o, hs], dest[name][0][:, o, hs], bias[:, bias_of[name], o:o + 1])
                    for n in range(QB // 2):
                        lo(b, U_V + n, U_V + n, v_lo[:, 2 * n:2 * n + 2, :], v_hi[:, 2 * n:2 * n + 2, :], None)
                    row_max(b, 0)
                    row_max(b, 1)
                    weigh(b, 0)
                    for i in range(QB):
                        if i + 2 < QB:
                            row_max(b, i + 2)
                        if i + 1 < QB:
                            weigh(b, i + 1)
                        pt(b, i)
                        if i == GQ + 1:
                            ao(b, 0, 0)
                    ao(b, 0, 1)
                    residual(b, 0)
                    if not last:
                        normalise_lo(b + 1)
                    ao(b, 1, 0)
                    ao(b, 1, 1)
                    residual(b, 1)

                dve.wait_ge(bias_loaded, 64)
                normalise_lo(0)
                batch(0, False)
                with dve.Fori(1, B - 1) as b:
                    batch(b, False)
                batch(B - 1, True)
                dve.wait_ge(unit_done, B * UNITS)


D = C
H = 8
HD = D // H
FF = 512
FC = FF // P
NT = T // P
PAIRS = NT // 2
MAX_NORM = 1.0 - 1e-5
F32_EPS = 2.0 ** -23
QK_GAIN = 64.0


def token_block(nc, x1, t2, ident, ident_h, w, norm1_w, norm2_w):
    SCALE = 2.0 / (float(HD) ** 0.5 * QK_GAIN ** 2)
    rounds = [(hg, qh) for hg in range(H // 4) for qh in range(2)]
    steps = [(r, kb) for r, (_, qh) in enumerate(rounds) for kb in range(4 * (qh + 1))]
    diagonal = [kb >= 4 * rounds[r][1] for r, kb in steps]
    NR, NS, ND = len(rounds), len(steps), sum(diagonal)

    def first_query(m):
        r, kb = steps[m]
        return max(kb * P - rounds[r][1] * 512, 0)

    with ExitStack() as ctx:
        s = Scope(nc, ctx, "block")
        xs = s.sb("xs", [P, CC, T])
        t1, u, h = s.sb("t1", [P, NT, D]), s.sb("u", [P, NT, D]), s.sb("h", [P, NT, D])
        turned_hi, turned_lo = s.sb("turned_hi", [P, CC, T], F32R), s.sb("turned_lo", [P, CC, T], F32R)
        qk = s.sb("qk", [P, NT, 2, D])
        x2 = qk[:, :, 0, :]
        v = s.sb("v", [P, NT, D])
        stack = s.sb("stack", [P, 2, 2, 2, H, 4, HD], F16)
        qkT = s.sb("qkT", [P, 2, H, T], F16)
        probs = s.sb("probs", [P, 2, 4, 512])
        ff_hi, ff_lo = s.sb("ff_hi", [P, FC, 512], F32R), s.sb("ff_lo", [P, FC, 512], F32R)
        n1, n2 = s.sb("n1", [P, D]), s.sb("n2", [P, D])
        mask = s.sb("mask", [P, P])
        ones = s.sb("ones", [P, HD])
        stats, mv = s.sb("stats", [P, NT, 6]), s.sb("mv", [P, NT, 2])
        rstd, rr, hsq, alpha = (s.sb(n, [P, NT]) for n in ("rstd", "rr", "hsq", "alpha"))
        ta, tb, tc, td = (s.sb(n, [P, 2 * NT]) for n in ("ta", "tb", "tc", "td"))
        gsq, fac = s.sb("gsq", [P, NT, 2]), s.sb("fac", [P, NT, 2])
        sq2 = s.sb("sq2", [P, 2, 2, 2, H])
        rr2 = s.sb("rr2", [P, NT])
        junk = s.sb("junk", [P, D])
        bank = s.ps("bank", [P, 8, 512])

        names = ("consts", "x_loaded", "norm_loaded", "x_full", "x_copied", "stats_done", "scal", "act_scal", "u_done", "h_done",
                 "hsq_done", "h_full", "hT_hi", "hT_lo", "qkv_full", "qk_copied", "v_copied", "gsq_done", "fac_done",
                 "scaled", "squared", "summed", "stack_hi", "stack_dup", "stack_lo", "stack_x", "stack_full", "qT_done", "kT_done",
                 "score_full", "exp_done", "masked", "av_step", "av_round", "inv_done", "attn_done", "aT_hi", "aT_lo",
                 "o_full", "x2_done", "x2sq_done", "h2_done", "h2_full", "h2T_hi", "h2T_lo", "gate_full", "silu_done", "ffprod_done",
                 "ff_hi_done", "ff_lo_done", "down_full", "down_added", "t2_done", "t2_stored", "log_done", "alpha_done", "passed")
        S = {n: s.sem(n) for n in names}

        ACT_SCAL, DVE_SCAL = 8, 24

        def attn_buf(r):
            return h[:, 2 * (r % 2):2 * (r % 2) + 2, :].rearrange("p a b -> p (a b)")

        with nc.Block() as block:

            @block.gpsimd
            def _(pool):
                pool.memset(ones[:, :], 1.0).then_inc(S["consts"], 1)
                pool.memset(mask[:, :], 1.0).then_inc(S["consts"], 1)
                for slot in range(2):
                    pool.memset(stack[:, slot, :, :, :, 3, :], 0.0).then_inc(S["consts"], 1)
                pool.wait_ge(S["consts"], 4)
                pool.affine_select(out=mask[:, :], in_=mask[:, :], compare_op=ALU.is_ge, fill=0.0, base=0,
                                   pattern=[[1, P]], channel_multiplier=-1).then_inc(S["consts"], 1)
                for slot in range(2):
                    pool.memset(stack[:, slot, :, 0, :, 3, 2:4], 1.0).then_inc(S["consts"], 1)
                    pool.memset(stack[:, slot, :, 1, :, 3, 0:2], 1.0).then_inc(S["consts"], 1)

            CONSTS = 9

            @block.sync
            def _(sp):
                for dst, src in ((n1, norm1_w), (n2, norm2_w)):
                    sp.dma_start(dst[:, :], src.rearrange("(a d) -> a d", a=1).to_broadcast((P, D))).then_inc(S["norm_loaded"], 16)
                def load(b):
                    sp.dma_start(xs[:, :, :], x1[b].rearrange("(c p) t -> p c t", p=P)).then_inc(S["x_loaded"], 16)

                def store(b):
                    sp.wait_ge(S["t2_done"], (b + 1) * PAIRS)
                    sp.dma_start(t2.rearrange("(b t p) d -> b p t d", p=P, t=NT)[b], t1[:, :, :]).then_inc(S["t2_stored"], 16)

                load(0)
                with sp.Fori(0, B - 1) as b:
                    sp.wait_ge(S["x_full"], (b + 1) * PAIRS)
                    load(b + 1)
                    store(b)
                store(B - 1)
                sp.wait_ge(S["t2_stored"], 16 * B)

            @block.tensor
            def _(pe):
                def batch(b):
                    pe.wait_ge(S["x_loaded"], (b + 1) * 16)
                    pe.wait_ge(S["t2_done"], b * PAIRS)
                    for pr in range(PAIRS):
                        for t in range(2):
                            for c in range(CC):
                                last = pe.transpose(bank[:, pr, (t * CC + c) * P:(t * CC + c + 1) * P],
                                                    xs[:, c, (2 * pr + t) * P:(2 * pr + t + 1) * P], ident[:, :])
                        last.then_inc(S["x_full"], 1)
                    for pr in range(PAIRS):
                        pe.wait_ge(S["h_done"], b * NT + 2 * pr + 2)
                        for c in range(CC):
                            for t in range(2):
                                last = pe.transpose(bank[:, 4 + pr, (c * 2 + t) * P:(c * 2 + t + 1) * P],
                                                    h[:, 2 * pr + t, c * P:(c + 1) * P], ident[:, :])
                        last.then_inc(S["h_full"], 1)
                    wh, wl = w["qkv"]
                    for t in range(NT):
                        pe.wait_ge(S["hT_lo"], b * PAIRS + (1 if t < 2 else PAIRS))
                        if t >= 4:
                            pe.wait_ge(S["gsq_done"], b * 2 * NT + 2 * (t - 3))
                            pe.wait_ge(S["v_copied"], b * NT + t - 3)
                        toks = slice(t * P, (t + 1) * P)
                        for i, cols in ((0, slice(0, 512)), (1, slice(512, 768))):
                            last = split_product(pe, bank[:, (2 * t + i) % 8, 0:cols.stop - cols.start],
                                                 [(turned_hi[:, k, toks], turned_lo[:, k, toks], wh[:, k, cols], wl[:, k, cols])
                                                  for k in range(CC)])
                            last.then_inc(S["qkv_full"], 1)
                    for n in range(2 * NT):
                        t, side = n // 2, n % 2
                        pe.wait_ge(S["stack_x"], b * PAIRS + t // 2 + 1)
                        pe.wait_ge(S["v_copied"], b * NT + NT)
                        if n >= 8:
                            pe.wait_ge(S[("qT_done", "kT_done")[side]], b * NT + t - 3)
                        out = bank[:, n % 8, :].bitcast(F16)
                        for hh in range(H):
                            last = pe.transpose(out[:, hh * P:(hh + 1) * P],
                                                stack[:, t // 2 % 2, t % 2, side, hh, :, :], ident_h[:, :])
                        last.then_inc(S["stack_full"], 1)
                    pe.wait_ge(S["qT_done"], b * NT + NT)
                    pe.wait_ge(S["kT_done"], b * NT + NT)

                    def scores(m):
                        r, kb = steps[m]
                        hg, qh = rounds[r]
                        q0 = first_query(m)
                        for p in range(2):
                            n = 2 * m + p
                            if n >= 2:
                                pe.wait_ge(S["exp_done"], b * 2 * NS + n - 1)
                            for i in range(2):
                                hh = 4 * hg + 2 * p + i
                                last = pe.matmul(bank[:, 2 * (n % 2) + i, q0:512], qkT[:, 1, hh, kb * P:(kb + 1) * P],
                                                 qkT[:, 0, hh, qh * 512 + q0:(qh + 1) * 512], start=True, stop=True)
                            last.then_inc(S["score_full"], 1)

                    def weigh(m):
                        r, kb = steps[m]
                        hg, qh = rounds[r]
                        q0 = first_query(m)
                        last_kb = 4 * (qh + 1) - 1
                        pe.wait_ge(S["exp_done"], b * 2 * NS + 2 * m + 2)
                        pe.wait_ge(S["masked"], b * ND + sum(diagonal[:m + 1]))
                        if kb == 0 and r >= 2:
                            pe.wait_ge(S["attn_done"], b * NR + r - 1)
                        num, den = bank[:, 4 + 2 * (r % 2), :], bank[:, 5 + 2 * (r % 2), :]
                        for out, own in ((num, True), (den, False)):
                            for i in range(4):
                                hh = 4 * hg + i
                                lhs = v[:, kb, hh * HD:(hh + 1) * HD] if own else ones[:, :]
                                last = pe.matmul(out[i * HD:(i + 1) * HD, q0:512], lhs, probs[:, m % 2, i, q0:512],
                                                 start=kb == 0, stop=kb == last_kb)
                        last.then_inc(S["av_step"], 1)

                    scores(0)
                    for m in range(NS):
                        if m + 1 < NS:
                            scores(m + 1)
                        weigh(m)
                    wh, wl = w["o"]
                    pe.wait_ge(S["aT_lo"], b * NR + NR)
                    for pr in range(PAIRS):
                        for t in range(2):
                            toks = slice((2 * pr + t) * P, (2 * pr + t + 1) * P)
                            last = split_product(pe, bank[:, pr, t * D:(t + 1) * D],
                                                 [(turned_hi[:, k, toks], turned_lo[:, k, toks], wh[:, k, :], wl[:, k, :]) for k in range(CC)])
                        last.then_inc(S["o_full"], 1)
                    for pr in range(PAIRS):
                        pe.wait_ge(S["h2_done"], b * NT + 2 * pr + 2)
                        for c in range(CC):
                            for t in range(2):
                                last = pe.transpose(bank[:, 4 + pr, (c * 2 + t) * P:(c * 2 + t + 1) * P],
                                                    h[:, 2 * pr + t, c * P:(c + 1) * P], ident[:, :])
                        last.then_inc(S["h2_full"], 1)
                    for g in range(2):
                        toks = slice(g * 512, (g + 1) * 512)
                        pe.wait_ge(S["h2T_lo"], b * PAIRS + PAIRS)
                        for f in range(FC):
                            n = g * FC + f
                            if n >= 4:
                                pe.wait_ge(S["ffprod_done"], b * 2 * FC + n - 3)
                                pe.wait_ge(S["t2_done"], b * PAIRS + 2)
                            for i, name in enumerate(("gate", "up")):
                                wh, wl = w[name]
                                cols = slice(f * P, (f + 1) * P)
                                last = split_product(pe, bank[:, 2 * (n % 4) + i, :],
                                                     [(wh[:, k, cols], wl[:, k, cols], turned_hi[:, k, toks], turned_lo[:, k, toks])
                                                      for k in range(CC)])
                            last.then_inc(S["gate_full"], 1)
                        wh, wl = w["down"]
                        pe.wait_ge(S["ff_lo_done"], b * 2 * FC + (g + 1) * FC)
                        for pr in (2 * g, 2 * g + 1):
                            for t in range(2):
                                own = slice((2 * pr + t) % 4 * P, ((2 * pr + t) % 4 + 1) * P)
                                last = split_product(pe, bank[:, pr, t * D:(t + 1) * D],
                                                     [(ff_hi[:, f, own], ff_lo[:, f, own], wh[:, f, :], wl[:, f, :]) for f in range(FC)])
                            last.then_inc(S["down_full"], 1)

                pe.wait_ge(S["consts"], CONSTS)
                batch(0)
                with pe.Fori(1, B) as b:
                    batch(b)

            @block.scalar
            def _(act):
                def batch(b):
                    act.wait_ge(S["t2_stored"], b * 16)
                    for pr in range(PAIRS):
                        act.wait_ge(S["x_full"], b * PAIRS + pr + 1)
                        act.activation(t1[:, 2 * pr:2 * pr + 2, :], bank[:, pr, :], ACT.Copy).then_inc(S["x_copied"], 1)
                    act.wait_ge(S["scal"], b * DVE_SCAL + 1)
                    act.activation(tb[:, 0:NT], ta[:, 0:NT], ACT.Sqrt).then_inc(S["act_scal"], 1)
                    act.wait_ge(S["scal"], b * DVE_SCAL + 5)
                    act.activation(td[:, 0:NT], tc[:, 0:NT], ACT.Sqrt).then_inc(S["act_scal"], 1)
                    for t in range(NT):
                        act.wait_ge(S["h_done"], b * NT + t + 1)
                        if t > 0:
                            act.wait_ge(S["hsq_done"], b * NT + t)
                        act.activation(junk[:, :], h[:, t, :], ACT.Square, accum_out=hsq[:, t:t + 1]).then_inc(S["hsq_done"], 1)
                    act.wait_ge(S["hsq_done"], b * NT + NT)
                    act.activation(ta[:, 0:NT], hsq[:, :], ACT.Sqrt, scale=0.25).then_inc(S["act_scal"], 1)
                    for pr in range(PAIRS):
                        act.wait_ge(S["h_full"], b * PAIRS + pr + 1)
                        act.activation(turned_hi[:, :, pr * 256:(pr + 1) * 256],
                                       bank[:, 4 + pr, :].rearrange("p (c q) -> p c q", c=CC), ACT.Copy).then_inc(S["hT_hi"], 1)
                    act.wait_ge(S["scal"], b * DVE_SCAL + 12)
                    act.activation(ta[:, 0:NT], tc[:, 0:NT], ACT.Ln).then_inc(S["act_scal"], 1)
                    act.activation(tb[:, 0:NT], td[:, 0:NT], ACT.Ln).then_inc(S["act_scal"], 1)
                    for t in range(NT):
                        act.wait_ge(S["qkv_full"], b * 2 * NT + 2 * t + 2)
                        src = bank[:, 2 * t % 8, :]
                        act.activation(qk[:, t, :, :], src, ACT.Copy).then_inc(S["qk_copied"], 1)
                        for side in range(2):
                            act.wait_ge(S["gsq_done"], b * 2 * NT + 2 * t + side)
                            act.activation(junk[:, :], src[:, side * D:(side + 1) * D], ACT.Square,
                                           accum_out=gsq[:, t, side:side + 1]).then_inc(S["gsq_done"], 1)
                    act.wait_ge(S["gsq_done"], b * 2 * NT + 2 * NT)
                    act.activation(ta[:, :], gsq[:, :, :], ACT.Sqrt).then_inc(S["act_scal"], 1)
                    act.wait_ge(S["scal"], b * DVE_SCAL + 17)
                    act.activation(tc[:, :], tb[:, :], ACT.Tanh).then_inc(S["act_scal"], 1)
                    for pr in range(PAIRS):
                        act.wait_ge(S["scaled"], b * PAIRS + pr + 1)
                        act.wait_ge(S["stack_full"], b * 2 * NT + max(pr - 1, 0) * 4)
                        act.wait_ge(S["summed"], b * PAIRS + pr)
                        act.activation(probs[:, 0, 0:2, :].rearrange("p a b -> p (a b)"), qk[:, 2 * pr:2 * pr + 2, :, :].rearrange("p a b c -> p (a b c)"),
                                       ACT.Square).then_inc(S["squared"], 1)
                        for side in range(2):
                            act.activation(stack[:, pr % 2, :, side, :, 0, :],
                                           qk[:, 2 * pr:2 * pr + 2, side, :].rearrange("p t (h d) -> p t h d", h=H), ACT.Copy).then_inc(S["stack_hi"], 1)
                        if pr > 0:
                            q_turned(b, pr - 1)
                    q_turned(b, PAIRS - 1)
                    for m in range(NS):
                        q0 = first_query(m)
                        act.wait_ge(S["av_step"], b * NS + max(m - 1, 0))
                        for p in range(2):
                            n = 2 * m + p
                            act.wait_ge(S["score_full"], b * 2 * NS + n + 1)
                            src = bank[:, 2 * (n % 2):2 * (n % 2) + 2, q0:512]
                            act.activation(probs[:, m % 2, 2 * p:2 * p + 2, q0:512], src, ACT.Exp, scale=SCALE).then_inc(S["exp_done"], 1)
                        if steps[m][1] == 2 and steps[m][0] > 0:
                            aT(b, steps[m][0] - 1)
                    aT(b, NR - 1)
                    for pr in range(PAIRS):
                        for t in (2 * pr, 2 * pr + 1):
                            act.wait_ge(S["x2_done"], b * PAIRS + pr + 1)
                            if t > 0:
                                act.wait_ge(S["x2sq_done"], b * NT + t)
                            act.activation(junk[:, :], x2[:, t, :], ACT.Square, accum_out=hsq[:, t:t + 1]).then_inc(S["x2sq_done"], 1)
                    act.wait_ge(S["scal"], b * DVE_SCAL + 22)
                    act.activation(tb[:, 0:NT], ta[:, 0:NT], ACT.Sqrt).then_inc(S["act_scal"], 1)
                    for pr in range(PAIRS):
                        act.wait_ge(S["h2_full"], b * PAIRS + pr + 1)
                        act.activation(turned_hi[:, :, pr * 256:(pr + 1) * 256],
                                       bank[:, 4 + pr, :].rearrange("p (c q) -> p c q", c=CC), ACT.Copy).then_inc(S["h2T_hi"], 1)
                    for n in range(2 * FC):
                        act.wait_ge(S["gate_full"], b * 2 * FC + n + 1)
                        act.wait_ge(S["ff_hi_done"], b * 2 * FC + n)
                        act.activation(probs[:, 0, n % 2, :], bank[:, 2 * (n % 4), :], ACT.Silu).then_inc(S["silu_done"], 1)
                        act.wait_ge(S["ffprod_done"], b * 2 * FC + n + 1)
                        act.wait_ge(S["down_full"], b * PAIRS + n // FC * 2)
                        act.activation(ff_hi[:, n % FC, :], probs[:, 1, n % 2, :], ACT.Copy).then_inc(S["ff_hi_done"], 1)

                def q_turned(b, pr):
                    for t in (2 * pr, 2 * pr + 1):
                        act.wait_ge(S["stack_full"], b * 2 * NT + 2 * t + 1)
                        act.activation(qkT[:, 0, :, t * P:(t + 1) * P],
                                       bank[:, 2 * t % 8, :].bitcast(F16).rearrange("p (h q) -> p h q", h=H), ACT.Copy).then_inc(S["qT_done"], 1)

                def aT(b, r):
                    hg, qh = rounds[r]
                    act.wait_ge(S["attn_done"], b * NR + r + 1)
                    act.activation(turned_hi[:, hg, qh * 512:(qh + 1) * 512], attn_buf(r), ACT.Copy).then_inc(S["aT_hi"], 1)

                act.wait_ge(S["consts"], CONSTS)
                batch(0)
                with act.Fori(1, B) as b:
                    batch(b)

            @block.vector
            def _(dve):
                def chain(b):
                    count[0] += 1
                    dve.wait_ge(S["scal"], b * DVE_SCAL + count[0])

                count = [0]

                def batch(b):
                    count[0] = 0
                    AS = b * ACT_SCAL
                    sc = S["scal"]
                    for pr in range(PAIRS):
                        dve.wait_ge(S["x_copied"], b * PAIRS + pr + 1)
                        for t in (2 * pr, 2 * pr + 1):
                            dve.bn_stats(stats[:, t, :], t1[:, t, :]).then_inc(S["stats_done"], 1)
                    dve.wait_ge(S["stats_done"], b * 2 * NT + NT)
                    dve.sem_inc(S["passed"], 1)
                    for t in range(NT):
                        dve.bn_aggr(mv[:, t, :], stats[:, t, :]).then_inc(S["stats_done"], 1)
                    dve.wait_ge(S["stats_done"], b * 2 * NT + 2 * NT)
                    mean, var = mv[:, :, 0], mv[:, :, 1]
                    dve.tensor_scalar(ta[:, 0:NT], var, LN_EPS, None, ALU.add).then_inc(sc, 1)
                    chain(b)
                    dve.wait_ge(S["act_scal"], AS + 1)
                    dve.reciprocal(rstd[:, :], tb[:, 0:NT]).then_inc(sc, 1)
                    chain(b)
                    dve.tensor_tensor(tc[:, 0:NT], rstd[:, :], rstd[:, :], ALU.mult).then_inc(sc, 1)
                    chain(b)
                    dve.tensor_tensor(td[:, 0:NT], tc[:, 0:NT], var, ALU.mult).then_inc(sc, 1)
                    chain(b)
                    dve.tensor_scalar(tc[:, 0:NT], td[:, 0:NT], F32_EPS, None, ALU.add).then_inc(sc, 1)
                    chain(b)
                    dve.wait_ge(S["act_scal"], AS + 2)
                    dve.reciprocal(rr[:, :], td[:, 0:NT]).then_inc(sc, 1)
                    chain(b)
                    for t in range(NT):
                        dve.tensor_scalar(u[:, t, :], t1[:, t, :], mean[:, t:t + 1], rstd[:, t:t + 1], ALU.subtract, ALU.mult).then_inc(S["u_done"], 1)
                    for t in range(NT):
                        dve.wait_ge(S["u_done"], b * NT + t + 1)
                        dve.scalar_tensor_tensor(h[:, t, :], u[:, t, :], rr[:, t:t + 1], n1[:, :], ALU.mult, ALU.mult).then_inc(S["h_done"], 1)
                    for pr in range(PAIRS):
                        dve.wait_ge(S["hT_hi"], b * PAIRS + pr + 1)
                        ts = slice(pr * 256, (pr + 1) * 256)
                        dve.tensor_tensor(turned_lo[:, :, ts], bank[:, 4 + pr, :].rearrange("p (c q) -> p c q", c=CC),
                                          turned_hi[:, :, ts].bitcast(F32), ALU.subtract).then_inc(S["hT_lo"], 1)
                    log_factor(b, AS, sc)
                    for t in range(NT):
                        dve.wait_ge(S["qkv_full"], b * 2 * NT + 2 * t + 2)
                        dve.tensor_copy(v[:, t, :], bank[:, (2 * t + 1) % 8, 0:D]).then_inc(S["v_copied"], 1)
                    dve.wait_ge(S["act_scal"], AS + 6)
                    av = alpha[:, :].rearrange("p (t a) -> p t a", a=1).to_broadcast((P, NT, 2))
                    g = ta[:, :].rearrange("p (t a) -> p t a", a=2)
                    dve.tensor_tensor(td[:, :].rearrange("p (t a) -> p t a", a=2), g, av, ALU.mult).then_inc(sc, 1)
                    chain(b)
                    dve.tensor_scalar(tb[:, :], td[:, :], 1e-6, None, ALU.max).then_inc(sc, 1)
                    chain(b)
                    dve.wait_ge(S["act_scal"], AS + 7)
                    dve.reciprocal(ta[:, :], tb[:, :]).then_inc(sc, 1)
                    chain(b)
                    dve.tensor_tensor(tb[:, :], ta[:, :], tc[:, :], ALU.mult).then_inc(sc, 1)
                    chain(b)
                    dve.tensor_tensor(tc[:, :], tb[:, :], td[:, :], ALU.mult).then_inc(sc, 1)
                    chain(b)
                    dve.tensor_scalar(td[:, :], tc[:, :], MAX_NORM, 1.0 / (MAX_NORM * QK_GAIN), ALU.max, ALU.mult).then_inc(S["fac_done"], 1)
                    dve.wait_ge(S["fac_done"], b * 4 + 1)
                    dve.reciprocal(tc[:, :], td[:, :]).then_inc(S["fac_done"], 1)
                    dve.wait_ge(S["fac_done"], b * 4 + 2)
                    dve.tensor_tensor(td[:, :], tc[:, :], tb[:, :], ALU.mult).then_inc(S["fac_done"], 1)
                    dve.wait_ge(S["fac_done"], b * 4 + 3)
                    dve.tensor_tensor(fac[:, :, :], td[:, :].rearrange("p (t a) -> p t a", a=2), av, ALU.mult).then_inc(S["fac_done"], 1)
                    dve.wait_ge(S["fac_done"], b * 4 + 4)
                    dve.wait_ge(S["qk_copied"], b * NT + NT)
                    for pr in range(PAIRS):
                        ts = slice(2 * pr, 2 * pr + 2)
                        dve.tensor_tensor(qk[:, ts, :, :].rearrange("p t s d -> p (t s) d"), qk[:, ts, :, :].rearrange("p t s d -> p (t s) d"),
                                          fac[:, ts, :].rearrange("p t s -> p (t s)").rearrange("p (n a) -> p n a", a=1).to_broadcast((P, 4, D)), ALU.mult).then_inc(S["scaled"], 1)
                        dve.wait_ge(S["squared"], b * PAIRS + pr + 1)
                        dve.tensor_reduce(sq2[:, pr % 2, :, :, :].rearrange("p t s h -> p (t s h)"),
                                          probs[:, 0, 0:2, :].rearrange("p a (n d) -> p (a n) d", d=HD), AX.X, ALU.add).then_inc(S["summed"], 1)
                        for side in range(2):
                            dve.wait_ge(S["stack_hi"], b * 2 * PAIRS + 2 * pr + side + 1)
                            st = stack[:, pr % 2, :, side, :, :, :]
                            src = qk[:, ts, side, :].rearrange("p t (h d) -> p t h d", h=H)
                            dve.tensor_tensor(st[:, :, :, 1 + side, :], src, st[:, :, :, 0, :], ALU.subtract).then_inc(S["stack_lo"], 1)
                            dve.tensor_copy(st[:, :, :, 2 - side, :], st[:, :, :, 0, :]).then_inc(S["stack_dup"], 1)
                        dve.wait_ge(S["summed"], b * PAIRS + pr + 1)
                        for side in range(2):
                            row = 2 * side
                            x = stack[:, pr % 2, :, side, :, 3, row:row + 2]
                            sq = sq2[:, pr % 2, :, side, :]
                            dve.tensor_scalar(x[:, :, :, 0], sq, -0.5, None, ALU.mult).then_inc(S["inv_done"], 1)
                        dve.wait_ge(S["inv_done"], b * INV + 2 * pr + 2)
                        dve.wait_ge(S["stack_dup"], (b * PAIRS + pr + 1) * 2)
                        dve.wait_ge(S["stack_lo"], (b * PAIRS + pr + 1) * 2)
                        for side in range(2):
                            row = 2 * side
                            x = stack[:, pr % 2, :, side, :, 3, row:row + 2]
                            sq = sq2[:, pr % 2, :, side, :]
                            last = dve.scalar_tensor_tensor(x[:, :, :, 1], sq, -0.5, x[:, :, :, 0], ALU.mult, ALU.subtract)
                            if side == 1:
                                last.then_inc(S["stack_x"], 1)
                        k_turned(b, 4 * pr + 1 - 4)
                        k_turned(b, 4 * pr + 3 - 4)
                    k_turned(b, 13)
                    k_turned(b, 15)
                    for m in range(NS):
                        r, kb = steps[m]
                        q0 = first_query(m)
                        if diagonal[m]:
                            dve.wait_ge(S["exp_done"], b * 2 * NS + 2 * m + 2)
                            pm = probs[:, m % 2, :, q0:q0 + P]
                            dve.tensor_tensor(pm, pm, mask[:, :].rearrange("p (a q) -> p a q", a=1).to_broadcast((P, 4, P)), ALU.mult).then_inc(S["masked"], 1)
                        if kb == 1 and r > 0:
                            normalise(b, r - 1)
                        if kb == 3 and r > 0:
                            low_part(b, r - 1)
                    normalise(b, NR - 1)
                    low_part(b, NR - 1)
                    for pr in range(PAIRS):
                        dve.wait_ge(S["o_full"], b * PAIRS + pr + 1)
                        ts = slice(2 * pr, 2 * pr + 2)
                        dve.tensor_tensor(x2[:, ts, :], bank[:, pr, :].rearrange("p (t d) -> p t d", t=2), u[:, ts, :], ALU.add).then_inc(S["x2_done"], 1)
                    dve.wait_ge(S["x2sq_done"], b * NT + NT)
                    dve.tensor_scalar(tc[:, 0:NT], hsq[:, :], 1.0 / D, None, ALU.mult).then_inc(sc, 1)
                    chain(b)
                    dve.tensor_scalar(ta[:, 0:NT], tc[:, 0:NT], F32_EPS, None, ALU.add).then_inc(sc, 1)
                    chain(b)
                    dve.wait_ge(S["act_scal"], AS + 8)
                    dve.reciprocal(rr2[:, :], tb[:, 0:NT]).then_inc(sc, 2)
                    dve.wait_ge(S["scal"], b * DVE_SCAL + 24)
                    for t in range(NT):
                        dve.scalar_tensor_tensor(h[:, t, :], x2[:, t, :], rr2[:, t:t + 1], n2[:, :], ALU.mult, ALU.mult).then_inc(S["h2_done"], 1)
                    for pr in range(PAIRS):
                        ts2 = slice(2 * pr, 2 * pr + 2)
                        dve.tensor_tensor(t1[:, ts2, :], t1[:, ts2, :], x2[:, ts2, :], ALU.add).then_inc(S["down_added"], 1)
                    for pr in range(PAIRS):
                        dve.wait_ge(S["h2T_hi"], b * PAIRS + pr + 1)
                        ts = slice(pr * 256, (pr + 1) * 256)
                        dve.tensor_tensor(turned_lo[:, :, ts], bank[:, 4 + pr, :].rearrange("p (c q) -> p c q", c=CC),
                                          turned_hi[:, :, ts].bitcast(F32), ALU.subtract).then_inc(S["h2T_lo"], 1)
                    for n in range(2 * FC):
                        dve.wait_ge(S["silu_done"], b * 2 * FC + n + 1)
                        dve.tensor_tensor(probs[:, 1, n % 2, :], probs[:, 0, n % 2, :], bank[:, 2 * (n % 4) + 1, :], ALU.mult).then_inc(S["ffprod_done"], 1)
                        dve.wait_ge(S["ff_hi_done"], b * 2 * FC + n + 1)
                        dve.tensor_tensor(ff_lo[:, n % FC, :], probs[:, 1, n % 2, :], ff_hi[:, n % FC, :].bitcast(F32), ALU.subtract).then_inc(S["ff_lo_done"], 1)
                        if n % FC == FC - 1:
                            for pr in (2 * (n // FC), 2 * (n // FC) + 1):
                                dve.wait_ge(S["down_full"], b * PAIRS + pr + 1)
                                dve.wait_ge(S["down_added"], b * PAIRS + pr + 1)
                                ts = slice(2 * pr, 2 * pr + 2)
                                dve.tensor_tensor(t1[:, ts, :], t1[:, ts, :], bank[:, pr, :].rearrange("p (t d) -> p t d", t=2), ALU.add).then_inc(S["t2_done"], 1)

                INV = 2 * PAIRS + NR

                def k_turned(b, n):
                    if n < 0:
                        return
                    dve.wait_ge(S["stack_full"], b * 2 * NT + n + 1)
                    dve.tensor_copy(qkT[:, 1, :, n // 2 * P:(n // 2 + 1) * P],
                                    bank[:, n % 8, :].bitcast(F16).rearrange("p (h q) -> p h q", h=H)).then_inc(S["kT_done"], 1)

                def normalise(b, r):
                    hg, qh = rounds[r]
                    m = max(i for i in range(NS) if steps[i][0] == r)
                    dve.wait_ge(S["av_step"], b * NS + m + 1)
                    inv = h[:, 4 + 2 * (r % 2):6 + 2 * (r % 2), :].rearrange("p a b -> p (a b)")
                    num, den = bank[:, 4 + 2 * (r % 2), :], bank[:, 5 + 2 * (r % 2), :]
                    dve.reciprocal(inv, den).then_inc(S["inv_done"], 1)
                    dve.wait_ge(S["inv_done"], b * INV + 2 * PAIRS + r + 1)
                    dve.tensor_tensor(attn_buf(r), num, inv, ALU.mult).then_inc(S["attn_done"], 1)

                def low_part(b, r):
                    hg, qh = rounds[r]
                    dve.wait_ge(S["aT_hi"], b * NR + r + 1)
                    ts = slice(qh * 512, (qh + 1) * 512)
                    dve.tensor_tensor(turned_lo[:, hg, ts], attn_buf(r), turned_hi[:, hg, ts].bitcast(F32), ALU.subtract).then_inc(S["aT_lo"], 1)

                def log_factor(b, AS, sc):
                    dve.wait_ge(S["act_scal"], AS + 3)
                    dve.tensor_scalar(tb[:, 0:NT], ta[:, 0:NT], MAX_NORM, None, ALU.max).then_inc(sc, 1)
                    chain(b)
                    dve.reciprocal(tc[:, 0:NT], tb[:, 0:NT]).then_inc(sc, 1)
                    chain(b)
                    dve.scalar_tensor_tensor(tb[:, 0:NT], tc[:, 0:NT], MAX_NORM, ta[:, 0:NT], ALU.mult, ALU.mult).then_inc(sc, 1)
                    dve.tensor_scalar(alpha[:, :], tc[:, 0:NT], 0.5 * MAX_NORM, None, ALU.mult).then_inc(sc, 1)
                    chain(b)
                    chain(b)
                    dve.tensor_scalar(rr2[:, :], tb[:, 0:NT], 1e-6, MAX_NORM, ALU.max, ALU.min).then_inc(sc, 1)
                    chain(b)
                    dve.tensor_scalar(tc[:, 0:NT], rr2[:, :], 1.0, None, ALU.add).then_inc(S["log_done"], 1)
                    dve.wait_ge(S["log_done"], b + 1)
                    dve.tensor_scalar(td[:, 0:NT], rr2[:, :], -1.0, 1.0, ALU.mult, ALU.add).then_inc(sc, 1)
                    chain(b)
                    dve.wait_ge(S["act_scal"], AS + 5)
                    dve.tensor_tensor(tc[:, 0:NT], ta[:, 0:NT], tb[:, 0:NT], ALU.subtract).then_inc(sc, 1)
                    chain(b)
                    dve.reciprocal(td[:, 0:NT], rr2[:, :]).then_inc(sc, 1)
                    chain(b)
                    dve.scalar_tensor_tensor(td[:, 0:NT], tc[:, 0:NT], 0.5, td[:, 0:NT], ALU.mult, ALU.mult).then_inc(sc, 1)
                    chain(b)
                    dve.tensor_tensor(alpha[:, :], alpha[:, :], td[:, 0:NT], ALU.mult).then_inc(S["alpha_done"], 1)
                    dve.wait_ge(S["alpha_done"], b + 1)

                dve.wait_ge(S["norm_loaded"], 32)
                dve.wait_ge(S["consts"], CONSTS)
                batch(0)
                with dve.Fori(1, B) as b:
                    batch(b)
                dve.wait_ge(S["t2_done"], B * PAIRS)


E_N = 8
HID = 1024
HC = HID // P
TILES = B * T // P
TOPK = 2
GT = 2
GS = GT * P
GROUPS = TILES * TOPK // GT + E_N - 1
ROW = 2 * D + 4
GAIN = 64.0
HID_GAIN = 16.0
AHEAD = 4


def route(nc, t2, rows, ident, gate_w, w1, w2, w1T, w2T, expert_of):
    PER = TILES // AHEAD
    CH = 4
    BANKS = 8
    with ExitStack() as ctx:
        s = Scope(nc, ctx, "route")
        xrow = s.sb("xrow", [P, TILES, ROW], F16)
        tok = s.sb("tok", [P, PER, D])
        natural = s.sb("natural", [P, CH, 4 * D])
        gT = s.sb("gT", [P, CC, E_N])
        xT = s.sb("xT", [P, 2, CC, P])
        stats, mv = s.sb("stats", [P, PER, 6]), s.sb("mv", [P, PER, 2])
        va, vb = s.sb("va", [P, PER]), s.sb("vb", [P, PER])
        top, idx = s.sb("top", [P, PER, 8]), s.sb("idx", [P, PER, 8], U32)
        logit = s.sb("logit", [P, PER, E_N])
        idxf = s.sb("idxf", [P, TILES, TOPK])
        oh = s.sb("oh", [P, TOPK, TILES, E_N])
        member = s.sb("member", [P, TILES, E_N])
        before = s.sb("before", [P, P])
        all_ones = s.sb("all_ones", [P, P])
        iota_e = s.sb("iota_e", [P, E_N])
        iota_t = s.sb("iota_t", [P, TILES // GT])
        iota_s = s.sb("iota_s", [1, GROUPS])
        within, total = s.sb("within", [P, TILES, E_N]), s.sb("total", [P, TILES, E_N])
        scan = s.sb("scan", [P, 2, TILES, E_N])
        cmp = s.sb("cmp", [P, E_N, TILES // GT])
        groups_e = s.sb("groups_e", [P, E_N])
        esc = s.sb("esc", [P, 2, E_N])
        posf, pos = s.sb("posf", [P, TILES]), s.sb("pos", [P, TOPK, TILES], U32)
        diff, wt = s.sb("diff", [P, TILES]), s.sb("wt", [P, TOPK, TILES])
        cmp_s, sum_s = s.sb("cmp_s", [1, GROUPS, E_N - 1]), s.sb("sum_s", [1, GROUPS])

        wbank = [s.ps(f"wbank{i}", [P, 512]) for i in range(4)]
        xbank = [s.ps(f"xbank{i}", [P, 512]) for i in range(2)]
        lbank = s.ps("lbank", [P, PER, E_N])
        pbank = s.ps("pbank", [P, 2, TILES * E_N])
        names = ("consts", "gate_loaded", "tok_loaded", "chunk0", "chunk1", "chunk2", "chunk3", "chunk_read", "w_full", "w_hi", "w_lo",
                 "stats_done", "var_done", "root_done", "rstd_done", "x_done", "x_hi", "x_lo", "xT_full", "xT_copied",
                 "logit_full", "logit_copied", "top_done", "idx_done", "plan", "counted", "exp_done", "choice_kept", "weights_set",
                 "pos_done", "scattered", "map_done", "passed")
        S = {n: s.sem(n) for n in names}
        w1_v = w1.rearrange("e (a o p) d -> e a p o d", a=2, p=P)
        w2_v = w2.rearrange("e (a p) h -> e a p h", p=P)
        t2_v = t2.rearrange("(a t p) d -> a p t d", p=P, t=PER)

        def wdest(e, n):
            c, half = n // 2, n % 2
            if c < 2:
                return tuple(w1T[:, e, part, half, c * 512:(c + 1) * 512] for part in range(2))
            return tuple(w2T[:, e, part, half * 4:(half + 1) * 4, (c - 2) * P:(c - 1) * P] for part in range(2))

        def bank_ap(n):
            b = wbank[n % 4][:, :]
            return b if n // 2 < 2 else b.rearrange("p (h q) -> p h q", h=4)

        with nc.Block() as block:

            @block.gpsimd
            def _(pool):
                pool.memset(before[:, :], 1.0).then_inc(S["consts"], 1)
                pool.memset(all_ones[:, :], 1.0).then_inc(S["consts"], 1)
                pool.iota(iota_e[:, :], pattern=[[1, E_N]], base=0, channel_multiplier=0, allow_small_or_imprecise_dtypes=True).then_inc(S["consts"], 1)
                pool.iota(iota_t[:, :], pattern=[[GS, TILES // GT]], base=0, channel_multiplier=0, allow_small_or_imprecise_dtypes=True).then_inc(S["consts"], 1)
                pool.iota(iota_s[:, :], pattern=[[1, GROUPS]], base=0, channel_multiplier=0, allow_small_or_imprecise_dtypes=True).then_inc(S["consts"], 1)
                pool.iota(xrow[:, :, 2 * D:2 * D + 2].bitcast(U32).rearrange("p t a -> p (t a)"), pattern=[[P, TILES]], base=0, channel_multiplier=1).then_inc(S["consts"], 1)
                pool.wait_ge(S["consts"], 6)
                pool.affine_select(out=before[:, :], in_=before[:, :], compare_op=ALU.is_gt, fill=0.0, base=0,
                                   pattern=[[1, P]], channel_multiplier=-1).then_inc(S["consts"], 1)
                for k in range(TOPK):
                    pool.wait_ge(S["pos_done"], k + 1)
                    pool.wait_ge(S["weights_set"], k + 1)
                    for t in range(TILES):
                        pool.indirect_dma_start(rows, bass.IndirectOffsetOnAxis(ap=pos[:, k, t:t + 1], axis=0),
                                                xrow[:, t, :].bitcast(U32), None).then_inc(S["scattered"], 16)
                pool.wait_ge(S["scattered"], TOPK * TILES * 16)

            CONSTS = 7

            @block.sync
            def _(sp):
                def chunk(e, c):
                    src = w1_v[e, c] if c < 2 else w2_v[e, c - 2]
                    dst = natural[:, c, :].rearrange("p (o d) -> p o d", d=D) if c < 2 else natural[:, c, :]
                    sp.dma_start(dst, src).then_inc(S[f"chunk{c}"], 16)

                sp.dma_start(tok[:, :, :], t2_v[0]).then_inc(S["tok_loaded"], 16)
                for k in range(CC):
                    sp.dma_start(gT[:, k, :], gate_w[:, k * P:(k + 1) * P].rearrange("e p -> p e"), allow_slow_non_contiguous=True).then_inc(S["gate_loaded"], 16)
                for c in range(CH):
                    chunk(0, c)
                with sp.Fori(0, E_N - 1) as e:
                    for c in range(CH):
                        sp.wait_ge(S["chunk_read"], e * CH + c + 1)
                        chunk(e + 1, c)

            @block.scalar
            def _(act):
                def load_tok(a):
                    act.dma_start(tok[:, :, :], t2_v[a]).then_inc(S["tok_loaded"], 16)

                def weights(e):
                    for n in range(BANKS):
                        act.wait_ge(S["w_full"], e * BANKS + n + 1)
                        act.activation(wdest(e, n)[0], bank_ap(n), ACT.Copy, scale=GAIN).then_inc(S["w_hi"], 1)

                def tokens(a):
                    act.wait_ge(S["var_done"], a + 1)
                    act.activation(vb[:, :], va[:, :], ACT.Sqrt).then_inc(S["root_done"], 1)
                    act.wait_ge(S["x_done"], (a + 1) * PER)
                    act.activation(xrow[:, bass.ds(a * PER, PER), 0:D], tok[:, :, :], ACT.Copy, scale=GAIN).then_inc(S["x_hi"], 1)
                    for i in range(PER):
                        act.wait_ge(S["xT_full"], a * PER + i + 1)
                        act.wait_ge(S["logit_full"], a * PER + max(i - 1, 0))
                        act.activation(xT[:, i % 2, :, :], xbank[i % 2][:, 0:CC * P].rearrange("p (c q) -> p c q", c=CC), ACT.Copy).then_inc(S["xT_copied"], 1)

                def turn(a):
                    tokens(a)
                    act.wait_ge(S["x_lo"], a + 1)
                    act.wait_ge(S["xT_full"], (a + 1) * PER)
                    load_tok(a + 1)
                    weights(a)

                turn(0)
                with act.Fori(1, AHEAD - 1) as a:
                    turn(a)
                tokens(AHEAD - 1)
                weights(AHEAD - 1)
                act.wait_ge(S["choice_kept"], 2 * AHEAD)
                act.activation(wt[:, 1, :], diff[:, :], ACT.Exp).then_inc(S["exp_done"], 1)
                with act.Fori(AHEAD, E_N) as e:
                    weights(e)

            @block.tensor
            def _(pe):
                def weights(e):
                    for n in range(BANKS):
                        c, half = n // 2, n % 2
                        if half == 0:
                            pe.wait_ge(S[f"chunk{c}"], 16 * (e + 1))
                        pe.wait_ge(S["w_lo"], e * BANKS + max(n - 3, 0))
                        for i in range(4):
                            src = natural[:, c, i * D + half * P:i * D + (half + 1) * P] if c < 2 else natural[:, c, (half * 4 + i) * P:(half * 4 + i + 1) * P]
                            last = pe.transpose(wbank[n % 4][:, i * P:(i + 1) * P], src, ident[:, :])
                        last.then_inc(S["w_full"], 1)
                        if half == 1:
                            pe.wait_ge(S["w_full"], e * BANKS + n + 1)
                            pe.sem_inc(S["chunk_read"], 1)

                def tokens(a):
                    for i in range(PER):
                        pe.wait_ge(S["x_done"], a * PER + i + 1)
                        pe.wait_ge(S["xT_copied"], a * PER + max(i - 1, 0))
                        for k in range(CC):
                            last = pe.transpose(xbank[i % 2][:, k * P:(k + 1) * P], tok[:, i, k * P:(k + 1) * P], ident[:, :])
                        last.then_inc(S["xT_full"], 1)
                        if i > 0:
                            logits(a, i - 1)
                    logits(a, PER - 1)

                def logits(a, i):
                    pe.wait_ge(S["xT_copied"], a * PER + i + 1)
                    if i == 0:
                        pe.wait_ge(S["logit_copied"], a)
                    for k in range(CC):
                        last = pe.matmul(lbank[:, i, :], xT[:, i % 2, k, :], gT[:, k, :], start=k == 0, stop=k == CC - 1)
                    last.then_inc(S["logit_full"], 1)

                pe.wait_ge(S["gate_loaded"], 16 * CC)
                tokens(0)
                weights(0)
                with pe.Fori(1, AHEAD) as a:
                    tokens(a)
                    weights(a)
                pe.wait_ge(S["consts"], CONSTS)
                pe.wait_ge(S["plan"], 3)
                flat = member[:, :, :].rearrange("p t e -> p (t e)")
                pe.matmul(pbank[:, 0, :], before[:, :], flat, start=True, stop=True).then_inc(S["counted"], 1)
                pe.matmul(pbank[:, 1, :], all_ones[:, :], flat, start=True, stop=True).then_inc(S["counted"], 1)
                with pe.Fori(AHEAD, E_N) as e:
                    weights(e)

            @block.vector
            def _(dve):
                def weights(e):
                    for n in range(BANKS):
                        dve.wait_ge(S["w_hi"], e * BANKS + n + 1)
                        hi, lo = wdest(e, n)
                        dve.scalar_tensor_tensor(lo, bank_ap(n), GAIN, hi, ALU.mult, ALU.subtract).then_inc(S["w_lo"], 1)

                def tokens(a):
                    dve.wait_ge(S["tok_loaded"], 16 * (a + 1))
                    for i in range(PER):
                        dve.bn_stats(stats[:, i, :], tok[:, i, :]).then_inc(S["stats_done"], 1)
                    dve.wait_ge(S["stats_done"], a * 2 * PER + PER)
                    dve.sem_inc(S["passed"], 1)
                    for i in range(PER):
                        dve.bn_aggr(mv[:, i, :], stats[:, i, :]).then_inc(S["stats_done"], 1)
                    dve.wait_ge(S["stats_done"], (a + 1) * 2 * PER)
                    dve.tensor_scalar(va[:, :], mv[:, :, 1], LN_EPS, None, ALU.add).then_inc(S["var_done"], 1)
                    dve.wait_ge(S["root_done"], a + 1)
                    dve.reciprocal(va[:, :], vb[:, :]).then_inc(S["rstd_done"], 1)
                    dve.wait_ge(S["rstd_done"], a + 1)
                    for i in range(PER):
                        dve.tensor_scalar(tok[:, i, :], tok[:, i, :], mv[:, i, 0:1], va[:, i:i + 1], ALU.subtract, ALU.mult).then_inc(S["x_done"], 1)
                    dve.wait_ge(S["x_hi"], a + 1)
                    rs = bass.ds(a * PER, PER)
                    dve.scalar_tensor_tensor(xrow[:, rs, D:2 * D], tok[:, :, :], GAIN, xrow[:, rs, 0:D], ALU.mult, ALU.subtract).then_inc(S["x_lo"], 1)
                    dve.wait_ge(S["logit_full"], (a + 1) * PER)
                    dve.tensor_copy(logit[:, :, :], lbank[:, :, :]).then_inc(S["logit_copied"], 1)
                    dve.wait_ge(S["logit_copied"], a + 1)
                    dve.sem_inc(S["passed"], 1)
                    for i in range(PER):
                        dve.max(top[:, i, :], logit[:, i, :]).then_inc(S["top_done"], 1)
                    dve.wait_ge(S["top_done"], (a + 1) * PER)
                    dve.sem_inc(S["passed"], 1)
                    for i in range(PER):
                        dve.max_index(idx[:, i, :], top[:, i, :], logit[:, i, :]).then_inc(S["idx_done"], 1)
                    dve.wait_ge(S["idx_done"], (a + 1) * PER)
                    dve.tensor_copy(idxf[:, rs, :], idx[:, :, 0:TOPK]).then_inc(S["choice_kept"], 1)
                    dve.tensor_tensor(diff[:, rs], top[:, :, 1], top[:, :, 0], ALU.subtract).then_inc(S["choice_kept"], 1)
                    dve.wait_ge(S["choice_kept"], 2 * (a + 1))

                tokens(0)
                weights(0)
                with dve.Fori(1, AHEAD) as a:
                    tokens(a)
                    weights(a)

                plan = S["plan"]
                dve.wait_ge(S["consts"], CONSTS)
                for k in range(TOPK):
                    dve.tensor_tensor(oh[:, k, :, :], idxf[:, :, k:k + 1].to_broadcast((P, TILES, E_N)),
                                      iota_e[:, :].rearrange("p (a e) -> p a e", a=1).to_broadcast((P, TILES, E_N)), ALU.is_equal).then_inc(S["map_done"], 1)
                dve.wait_ge(S["map_done"], 2)
                dve.tensor_tensor(member[:, :, :], oh[:, 0, :, :], oh[:, 1, :, :], ALU.add).then_inc(plan, 3)
                dve.wait_ge(S["exp_done"], 1)
                dve.tensor_scalar(diff[:, :], wt[:, 1, :], 1.0, None, ALU.add).then_inc(plan, 1)
                dve.wait_ge(plan, 4)
                dve.reciprocal(wt[:, 0, :], diff[:, :]).then_inc(plan, 1)
                dve.wait_ge(plan, 5)
                dve.tensor_tensor(wt[:, 1, :], wt[:, 1, :], wt[:, 0, :], ALU.mult).then_inc(plan, 1)
                wfield = xrow[:, :, 2 * D + 2:2 * D + 4].bitcast(F32)
                dve.tensor_copy(wfield[:, :, 0], wt[:, 0, :]).then_inc(S["weights_set"], 1)
                dve.wait_ge(S["counted"], 2)
                dve.tensor_copy(within[:, :, :], pbank[:, 0, :].rearrange("p (t e) -> p t e", e=E_N)).then_inc(plan, 1)
                dve.tensor_copy(total[:, :, :], pbank[:, 1, :].rearrange("p (t e) -> p t e", e=E_N)).then_inc(plan, 1)
                dve.wait_ge(plan, 8)
                dve.tensor_copy(scan[:, 0, :, :], total[:, :, :]).then_inc(plan, 1)
                n, step, at = 9, 1, 0
                while step < TILES:
                    dve.wait_ge(plan, n)
                    dve.tensor_copy(scan[:, 1 - at, 0:step, :], scan[:, at, 0:step, :]).then_inc(plan, 1)
                    dve.tensor_tensor(scan[:, 1 - at, step:TILES, :], scan[:, at, step:TILES, :], scan[:, at, 0:TILES - step, :], ALU.add).then_inc(plan, 1)
                    n, step, at = n + 2, step * 2, 1 - at
                dve.wait_ge(plan, n)
                dve.tensor_tensor(cmp[:, :, :], scan[:, at, TILES - 1, :].rearrange("p (e a) -> p e a", a=1).to_broadcast((P, E_N, TILES // GT)),
                                  iota_t[:, :].rearrange("p (a t) -> p a t", a=1).to_broadcast((P, E_N, TILES // GT)), ALU.is_gt).then_inc(plan, 1)
                dve.tensor_tensor(scan[:, 1 - at, :, :], scan[:, at, :, :], total[:, :, :], ALU.subtract).then_inc(plan, 1)
                at = 1 - at
                n += 2
                dve.wait_ge(plan, n)
                dve.tensor_reduce(groups_e[:, :], cmp[:, :, :], AX.X, ALU.add).then_inc(plan, 1)
                dve.tensor_tensor(within[:, :, :], within[:, :, :], scan[:, at, :, :], ALU.add).then_inc(plan, 1)
                n += 2
                dve.wait_ge(plan, n)
                dve.tensor_copy(esc[:, 0, :], groups_e[:, :]).then_inc(plan, 1)
                n, step, ea = n + 1, 1, 0
                while step < E_N:
                    dve.wait_ge(plan, n)
                    dve.tensor_copy(esc[:, 1 - ea, 0:step], esc[:, ea, 0:step]).then_inc(plan, 1)
                    dve.tensor_tensor(esc[:, 1 - ea, step:E_N], esc[:, ea, step:E_N], esc[:, ea, 0:E_N - step], ALU.add).then_inc(plan, 1)
                    n, step, ea = n + 2, step * 2, 1 - ea
                dve.wait_ge(plan, n)
                ends = esc[0:1, ea, 0:E_N - 1]
                dve.tensor_tensor(cmp_s[:, :, :], iota_s[:, :].rearrange("p (s a) -> p s a", a=1).to_broadcast((1, GROUPS, E_N - 1)),
                                  ends.rearrange("p (a e) -> p a e", a=1).to_broadcast((1, GROUPS, E_N - 1)), ALU.is_ge).then_inc(plan, 1)
                dve.tensor_tensor(esc[:, 1 - ea, :], esc[:, ea, :], groups_e[:, :], ALU.subtract).then_inc(plan, 1)
                n += 2
                dve.wait_ge(plan, n)
                dve.tensor_reduce(sum_s[:, :], cmp_s[:, :, :], AX.X, ALU.add).then_inc(plan, 1)
                dve.scalar_tensor_tensor(within[:, :, :], esc[:, 1 - ea, :].rearrange("p (a e) -> p a e", a=1).to_broadcast((P, TILES, E_N)), float(GS),
                                         within[:, :, :], ALU.mult, ALU.add).then_inc(plan, 1)
                n += 2
                dve.wait_ge(plan, n)
                dve.tensor_copy(expert_of[:, :], sum_s[:, :]).then_inc(plan, 1)
                n += 1
                for k in range(TOPK):
                    dve.tensor_tensor(oh[:, k, :, :], oh[:, k, :, :], within[:, :, :], ALU.mult).then_inc(plan, 1)
                    n += 1
                    dve.wait_ge(plan, n)
                    dve.tensor_reduce(posf[:, :], oh[:, k, :, :], AX.X, ALU.add).then_inc(plan, 1)
                    n += 1
                    dve.wait_ge(plan, n)
                    dve.tensor_copy(pos[:, k, :], posf[:, :]).then_inc(S["pos_done"], 1)
                    dve.wait_ge(S["pos_done"], k + 1)
                with dve.Fori(AHEAD, E_N) as e:
                    weights(e)
                dve.wait_ge(S["scattered"], TILES * 16)
                dve.tensor_copy(wfield[:, :, 0], wt[:, 1, :]).then_inc(S["weights_set"], 1)
                dve.wait_ge(S["weights_set"], 2)


def experts(nc, acc, rows, ident_h, b1, b2, w1T, w2T, expert_of):
    with ExitStack() as ctx:
        s = Scope(nc, ctx, "moe")
        b1T, b2r = s.sb("b1T", [P, E_N, HC]), s.sb("b2r", [P, E_N, D])
        xin = [s.sb(f"xin{i}", [P, GT, ROW], F16) for i in range(2)]
        meta = [s.sb(f"meta{i}", [P, GT, 2]) for i in range(4)]
        xT = [s.sb(f"xT{i}", [P, 2, CC, GS], F16) for i in range(2)]
        hid = [s.sb(f"hid{i}", [P, HC, GS]) for i in range(2)]
        hid_hi = [s.sb(f"hid_hi{i}", [P, HC, GS], F16) for i in range(2)]
        hid_lo = [s.sb(f"hid_lo{i}", [P, HC, GS], F16) for i in range(2)]
        y = [s.sb(f"y{i}", [P, GT, D]) for i in range(2)]
        ysum = [s.sb(f"ysum{i}", [P, GT, D]) for i in range(2)]
        turned = s.ps("turned", [P, 2 * CC, GS], F16)
        hbank = s.ps("hbank", [P, HC, GS])
        ybank = [s.ps(f"ybank{i}", [P, GT, D]) for i in range(2)]
        names = ("bias_loaded", "in0", "in1", "turned_full", "xT_done", "h_full", "gelu_done", "hi_done", "lo_done", "y_full",
                 "meta_done", "ysum_done", "y_done", "added", "passed")
        S = {n: s.sem(n) for n in names}
        rows_v = rows.rearrange("(n t p) r -> n p t r", p=P, t=GT)

        def all_tiles(eng, step):
            for j in range(3):
                step(j, j)
            with eng.Fori(0, (GROUPS - 3) // 4) as i:
                for r in range(4):
                    step(i * 4 + (3 + r), (3 + r) % 4)

        assert (GROUPS - 3) % 4 == 0

        def early(j, n):
            return isinstance(j, int) and j < n

        with nc.Block() as block:

            @block.sync
            def _(sp):
                sp.dma_start(b1T[:, :, :], b1.rearrange("e (c p) -> p e c", p=P), allow_slow_non_contiguous=True).then_inc(S["bias_loaded"], 16)
                sp.dma_start(b2r[:, :, :], b2.rearrange("(a e) d -> a e d", a=1).to_broadcast((P, E_N, D))).then_inc(S["bias_loaded"], 16)

                def step(j, r):
                    if not early(j, 2):
                        sp.wait_ge(S["turned_full"], j - 1)
                        sp.wait_ge(S["meta_done"], j - 1)
                    sp.dma_start(xin[r % 2][:, :, :].bitcast(U32), rows_v[j]).then_inc(S[f"in{r % 2}"], 16)

                all_tiles(sp, step)

            @block.gpsimd
            def _(pool):
                def step(j, r):
                    pool.wait_ge(S["y_done"], j + 1)
                    if not early(j, 1):
                        pool.wait_ge(S["added"], j * (16 * GT))
                    pool.sem_inc(S["passed"], 1)
                    for t in range(GT):
                        pool.indirect_dma_start(acc, bass.IndirectOffsetOnAxis(ap=meta[r][:, t, 0:1].bitcast(U32), axis=0),
                                                y[r % 2][:, t, :], None, compute_op=ALU.add).then_inc(S["added"], 16)

                all_tiles(pool, step)
                pool.wait_ge(S["added"], GROUPS * 16 * GT)

            @block.tensor
            def _(pe):
                def expert(j):
                    return pe.value_load(expert_of[0:1, bass.ds(j, 1)], min_val=0, max_val=E_N - 1)

                def turn(j, r):
                    q = r % 2
                    pe.wait_ge(S[f"in{q}"], (j - q) * 8 + 16)
                    if not early(j, 1):
                        pe.wait_ge(S["xT_done"], j)
                    for part in range(2):
                        for k in range(CC):
                            for t in range(GT):
                                last = pe.transpose(turned[:, part * CC + k, t * P:(t + 1) * P],
                                                    xin[q][:, t, part * D + k * P:part * D + (k + 1) * P], ident_h[:, :])
                    last.then_inc(S["turned_full"], 1)

                def up(j, r):
                    q, e = r % 2, expert(j)
                    pe.wait_ge(S["xT_done"], j + 1)
                    for c in range(HC):
                        if c % 2 == 0 and not early(j, 1):
                            pe.wait_ge(S["gelu_done"], j * HC - (HC - 2 - c))
                        n = 0
                        for wp, xp in ((0, 0), (0, 1), (1, 0)):
                            for k in range(CC):
                                last = pe.matmul(hbank[:, c, :], w1T[:, e, wp, k, c * P:(c + 1) * P], xT[q][:, xp, k, :],
                                                 start=n == 0, stop=n == 5)
                                n += 1
                        if c % 2 == 1:
                            last.then_inc(S["h_full"], 1)

                def down(j, r):
                    q, e = r % 2, expert(j)
                    pe.wait_ge(S["lo_done"], j + 1)
                    if not early(j, 2):
                        pe.wait_ge(S["ysum_done"], j - 1)
                    for t in range(GT):
                        n = 0
                        for c in range(HC):
                            for hp, wp in ((0, 0), (0, 1), (1, 0)):
                                last = pe.matmul(ybank[q][:, t, :], (hid_hi, hid_lo)[hp][q][:, c, t * P:(t + 1) * P], w2T[:, e, wp, c, :],
                                                 start=n == 0, stop=n == 3 * HC - 1)
                                n += 1
                    last.then_inc(S["y_full"], 1)

                def step(j, r):
                    turn(j + 1, (r + 1) % 4)
                    up(j, r)
                    if not early(j, 1):
                        down(j - 1, (r - 1) % 4)

                turn(0, 0)
                for j in range(3):
                    step(j, j)
                with pe.Fori(0, (GROUPS - 3) // 4 - 1) as i:
                    for r in range(4):
                        step(i * 4 + (3 + r), (3 + r) % 4)
                for j in range(GROUPS - 4, GROUPS - 1):
                    step(j, j % 4)
                up(GROUPS - 1, (GROUPS - 1) % 4)
                down(GROUPS - 2, (GROUPS - 2) % 4)
                down(GROUPS - 1, (GROUPS - 1) % 4)

            @block.scalar
            def _(act):
                act.wait_ge(S["bias_loaded"], 32)

                def step(j, r):
                    q = r % 2
                    e = act.value_load(expert_of[0:1, bass.ds(j, 1)], min_val=0, max_val=E_N - 1)
                    if not early(j, 2):
                        act.wait_ge(S["lo_done"], j - 1)
                    for c in range(HC):
                        act.wait_ge(S["h_full"], j * (HC // 2) + (c // 2 + 1))
                        act.activation(hid[q][:, c, :], hbank[:, c, :], ACT.Gelu, bias=b1T[:, e, c:c + 1],
                                       scale=1.0 / (GAIN * GAIN)).then_inc(S["gelu_done"], 1)

                all_tiles(act, step)

            @block.vector
            def _(dve):
                dve.wait_ge(S["bias_loaded"], 32)

                def tokens(j, r):
                    q = r % 2
                    dve.wait_ge(S["turned_full"], j + 1)
                    dve.tensor_copy(xT[q][:, :, :, :], turned[:, :, :].rearrange("p (a c) q -> p a c q", a=2)).then_inc(S["xT_done"], 1)
                    if not early(j, 4):
                        dve.wait_ge(S["added"], (j - 3) * (16 * GT))
                    dve.tensor_copy(meta[r][:, :, :], xin[q][:, :, 2 * D:2 * D + 4].bitcast(F32)).then_inc(S["meta_done"], 1)

                def split(j, r):
                    q = r % 2
                    dve.wait_ge(S["gelu_done"], (j + 1) * HC)
                    dve.tensor_scalar(hid_hi[q][:, :, :], hid[q][:, :, :], HID_GAIN, None, ALU.mult).then_inc(S["hi_done"], 1)
                    dve.wait_ge(S["hi_done"], j + 1)
                    dve.scalar_tensor_tensor(hid_lo[q][:, :, :], hid[q][:, :, :], HID_GAIN, hid_hi[q][:, :, :], ALU.mult, ALU.subtract).then_inc(S["lo_done"], 1)

                def out(j, r):
                    q = r % 2
                    e = dve.value_load(expert_of[0:1, bass.ds(j, 1)], min_val=0, max_val=E_N - 1)
                    dve.wait_ge(S["y_full"], j + 1)
                    dve.scalar_tensor_tensor(ysum[q][:, :, :], ybank[q][:, :, :], 1.0 / (GAIN * HID_GAIN),
                                             b2r[:, bass.ds(e, 1), :].to_broadcast((P, GT, D)), ALU.mult, ALU.add).then_inc(S["ysum_done"], 1)
                    dve.wait_ge(S["ysum_done"], j + 1)
                    if not early(j, 2):
                        dve.wait_ge(S["added"], (j - 1) * (16 * GT))
                    for t in range(GT):
                        last = dve.tensor_scalar(y[q][:, t, :], ysum[q][:, t, :], meta[r][:, t, 1:2], None, ALU.mult)
                    last.then_inc(S["y_done"], 1)

                def step(j, r):
                    tokens(j + 1, (r + 1) % 4)
                    if not early(j, 2):
                        out(j - 2, (r - 2) % 4)
                    split(j, r)

                tokens(0, 0)
                for j in range(3):
                    step(j, j)
                with dve.Fori(0, (GROUPS - 3) // 4 - 1) as i:
                    for r in range(4):
                        step(i * 4 + (3 + r), (3 + r) % 4)
                for j in range(GROUPS - 4, GROUPS - 1):
                    step(j, j % 4)
                out(GROUPS - 3, (GROUPS - 3) % 4)
                split(GROUPS - 1, (GROUPS - 1) % 4)
                out(GROUPS - 2, (GROUPS - 2) % 4)
                out(GROUPS - 1, (GROUPS - 1) % 4)
                dve.wait_ge(S["y_done"], GROUPS)


def write_out(nc, acc, out, ident):
    PER = T // P
    with ExitStack() as ctx:
        s = Scope(nc, ctx, "out")
        tok = [s.sb(f"tok{i}", [P, PER, D]) for i in range(2)]
        res = [s.sb(f"res{i}", [P, CC, T]) for i in range(2)]
        bank = [s.ps(f"bank{i}", [P, 512]) for i in range(4)]
        loaded = [s.sem(f"loaded{i}") for i in range(2)]
        stored = [s.sem(f"stored{i}") for i in range(2)]
        full, copied, copied_act = (s.sem(n) for n in ("full", "copied", "copied_act"))
        src = acc[0:B * T, :].rearrange("(b t p) d -> b p t d", p=P, t=PER)
        UN = 2 * CC
        with nc.Block() as block:

            @block.sync
            def _(sp):
                for b in range(B):
                    if b >= 2:
                        sp.wait_ge(full, (b - 1) * UN)
                    sp.dma_start(tok[b % 2][:, :, :], src[b]).then_inc(loaded[b % 2], 16)

            @block.tensor
            def _(pe):
                for b in range(B):
                    pe.wait_ge(loaded[b % 2], 16 * (b // 2 + 1))
                    for n in range(UN):
                        c, h = n // 2, n % 2
                        if b:
                            pe.wait_ge((copied, copied_act)[n % 2], (b - 1) * 2 + n // 2 + 1)
                        for i in range(4):
                            last = pe.transpose(bank[n][:, i * P:(i + 1) * P], tok[b % 2][:, h * 4 + i, c * P:(c + 1) * P], ident[:, :])
                        last.then_inc(full, 1)

            def copies(eng, copy, sem, parity):
                for b in range(B):
                    if b >= 2:
                        eng.wait_ge(stored[b % 2], 16 * CC * (b // 2))
                    for n in range(parity, UN, 2):
                        c, h = n // 2, n % 2
                        eng.wait_ge(full, b * UN + n + 1)
                        copy(res[b % 2][:, c, h * 512:(h + 1) * 512], bank[n][:, :]).then_inc(sem, 1)

            @block.vector
            def _(dve):
                copies(dve, dve.tensor_copy, copied, 0)

            @block.scalar
            def _(act):
                copies(act, lambda o, i: act.activation(o, i, ACT.Copy), copied_act, 1)

            @block.gpsimd
            def _(pool):
                for b in range(B):
                    for c in range(CC):
                        pool.wait_ge(copied, b * CC + c + 1)
                        pool.wait_ge(copied_act, b * CC + c + 1)
                        pool.dma_start(out[b, c * P:(c + 1) * P].rearrange("p h w -> p (h w)"), res[b % 2][:, c, :]).then_inc(stored[b % 2], 16)
                for i in range(2):
                    pool.wait_ge(stored[i], 16 * CC * B // 2)


def fill_rows(nc, rows, blank, filled):
    with ExitStack() as ctx:
        s = Scope(nc, ctx, "fill")
        zeroed, numbered = s.sem("zeroed"), s.sem("numbered")
        with nc.Block() as block:

            @block.gpsimd
            def _(pool):
                pool.memset(blank[:, :, :], 0.0).then_inc(zeroed, 1)
                pool.wait_ge(zeroed, 1)
                pool.iota(blank[:, :, 2 * D:2 * D + 2].bitcast(U32), pattern=[[P, GT], [0, 1]], base=B * T, channel_multiplier=1).then_inc(numbered, 1)

            @block.sync
            def _(sp):
                sp.wait_ge(numbered, 1)
                for t in range(GT):
                    sp.dma_start(rows.rearrange("(n t p) r -> t p n r", p=P, t=GT)[t],
                                 blank[:, t:t + 1, :].bitcast(U32).to_broadcast((P, GROUPS, ROW // 2))).then_inc(filled, 16)
        s.clear()


def build(nc, x, p, out):
    x1 = nc.dram_tensor("x1_scratch", (B, C, T), F32).ap()
    acc = nc.dram_tensor("acc_scratch", (B * T + GT * P, D), F32).ap()
    rows = nc.dram_tensor("rows_scratch", (GROUPS * GS, ROW // 2), U32).ap()
    with ExitStack() as whole:
        s = Scope(nc, whole, "all")
        ident, ident_h = s.sb("ident", [P, P]), s.sb("ident_h", [P, P], F16)
        with ExitStack() as ctx:
            s = Scope(nc, ctx, "l0")
            group_mean = s.sb("group_mean", [P, P])
            filled = s.sem("filled")
            make_constants(nc, ident, ident_h, group_mean)
            fill_rows(nc, rows, s.sb("blank", [P, GT, ROW], F16), filled)
            xs = s.sb("xs", [P, B, CC, T])
            scale, shift = s.sb("scale", [P, B, CC]), s.sb("shift", [P, B, CC])
            w = {n: (s.sb(f"w{n}_hi", [P, CC, C], F32R), s.sb(f"w{n}_lo", [P, CC, C], F32R)) for n in "qkvp"}
            prepare_weights(nc, "w0", [(p[f"L0_conv_w{n}"], *w[n]) for n in "qkvp"], ident)
            group_norm_affine(nc, x, xs, p["L0_conv_norm_gamma"], p["L0_conv_norm_beta"], group_mean, scale, shift)
            conv_attention(nc, xs, scale, shift, ident, w, *(p[f"L0_conv_b{n}"] for n in "qkvp"))
            stored = s.sem("stored")
            with nc.Block() as block:

                @block.sync
                def _(sp):
                    for b in range(B):
                        sp.dma_start(x1[b].rearrange("(c p) t -> p c t", p=P), xs[:, b, :, :]).then_inc(stored, 16)
                    sp.wait_ge(stored, 16 * B)
                    sp.wait_ge(filled, 16 * GT)

        with ExitStack() as ctx:
            s = Scope(nc, ctx, "l1")
            qkv = [s.sb(f"qkv{i}", [P, CC, 3 * D], F32R) for i in range(2)]
            units = [(p[f"L1_attn_{n}_w"], *(t[:, :, i * D:(i + 1) * D] for t in qkv)) for i, n in enumerate("qkv")]
            w = {"qkv": qkv}
            for n, k, f in (("o", CC, D), ("gate", CC, FF), ("up", CC, FF), ("down", FC, D)):
                w[n] = [s.sb(f"{n}{i}", [P, k, f], F32R) for i in range(2)]
                units.append((p[f"L1_attn_{n}_w"], *w[n]))
            prepare_weights(nc, "w1", units, ident)
            token_block(nc, x1, acc[0:B * T, :], ident, ident_h, w, p["L1_attn_norm1_w"], p["L1_attn_norm2_w"])

        with ExitStack() as ctx:
            s = Scope(nc, ctx, "l2")
            w1T, w2T = s.sb("w1T", [P, E_N, 2, CC, HID], F16), s.sb("w2T", [P, E_N, 2, HC, D], F16)
            expert_of = s.sb("expert_of", [1, GROUPS], mybir.dt.int32)
            route(nc, acc[0:B * T, :], rows, ident, p["L1_ffn_gate_w"], p["L1_ffn_w1"], p["L1_ffn_w2"], w1T, w2T, expert_of)
            experts(nc, acc, rows, ident_h, p["L1_ffn_b1"], p["L1_ffn_b2"], w1T, w2T, expert_of)
        write_out(nc, acc, out, ident)


_INS = ["x"] + [f"L0_conv_{n}" for n in ("norm_gamma", "norm_beta", "wq", "bq", "wk", "bk", "wv", "bv", "wp", "bp")] \
    + [f"L1_attn_{n}" for n in ("q_w", "k_w", "v_w", "o_w", "gate_w", "up_w", "down_w", "norm1_w", "norm2_w")] \
    + [f"L1_ffn_{n}" for n in ("gate_w", "w1", "b1", "w2", "b2")]


def kernel(**inputs):
    import numpy as np
    from concourse import bacc
    from concourse.bass_utils import run_bass_kernel_spmd

    nc = bacc.Bacc("TRN2", target_bir_lowering=False, num_devices=1)
    arrays, args = {}, {}
    for name in _INS:
        a = np.ascontiguousarray(inputs[name])
        arrays[f"in_{name}"] = a
        args[name] = nc.dram_tensor(f"in_{name}", a.shape, mybir.dt.from_np(a.dtype), kind="ExternalInput").ap()
    out = nc.dram_tensor("out", inputs["x"].shape, F32, kind="ExternalOutput").ap()
    build(nc, args["x"], args, out)
    r = run_bass_kernel_spmd(nc, [arrays], core_ids=[0])
    return r.results[0]["out"]
```

```python
from contextlib import ExitStack

import concourse.bass as bass
from concourse import mybir

F32 = mybir.dt.float32
F32R = mybir.dt.float32r
F16 = mybir.dt.float16
U32 = mybir.dt.uint32
ALU = mybir.AluOpType
ACT = mybir.ActivationFunctionType
AX = mybir.AxisListType

P = 128
B = 4
C = 256
T = 1024
CC = C // P
GROUP = 8
QB = T // P
GQ = 4
NG = QB // GQ
GN_EPS = 1e-6
LN_EPS = 1e-5


class Scope:

    def __init__(self, nc, ctx, tag):
        self.nc, self.ctx, self.tag = nc, ctx, tag
        self.sems = []

    def sb(self, name, shape, dt=F32):
        return self.ctx.enter_context(self.nc.sbuf_tensor(f"{self.tag}_{name}", shape, dt))

    def ps(self, name, shape, dt=F32):
        return self.ctx.enter_context(self.nc.psum_tensor(f"{self.tag}_{name}", shape, dt))

    def sem(self, name):
        sem = self.ctx.enter_context(self.nc.semaphore(f"{self.tag}_{name}"))
        self.sems.append(sem)
        return sem

    def clear(self):
        with self.nc.Block() as block:

            @block.gpsimd
            def _(pool):
                for sem in self.sems:
                    pool.sem_clear(sem)


def make_constants(nc, ident, ident_h, group_mean):
    with ExitStack() as ctx:
        s = Scope(nc, ctx, "const")
        filled, selected = s.sem("filled"), s.sem("selected")
        with nc.Block() as block:

            @block.gpsimd
            def _(pool):
                pool.memset(ident[:, :], 0.0).then_inc(filled, 1)
                pool.memset(group_mean[:, :], 1.0 / GROUP).then_inc(filled, 1)
                pool.wait_ge(filled, 2)
                pool.affine_select(out=ident[:, :], in_=ident[:, :], compare_op=ALU.not_equal, fill=1.0,
                                   base=0, pattern=[[-1, P]], channel_multiplier=1).then_inc(selected, 1)
                gm = group_mean[:, :].rearrange("p (g r) -> p g r", r=GROUP)
                pool.affine_select(out=gm, in_=gm, compare_op=ALU.is_ge, fill=0.0, base=0,
                                   pattern=[[-GROUP, P // GROUP], [0, GROUP]],
                                   channel_multiplier=1).then_inc(selected, 1)
                pool.wait_ge(selected, 2)
                pool.affine_select(out=gm, in_=gm, compare_op=ALU.is_ge, fill=0.0, base=GROUP - 1,
                                   pattern=[[GROUP, P // GROUP], [0, GROUP]],
                                   channel_multiplier=-1).then_inc(selected, 1)
                pool.tensor_copy(ident_h[:, :], ident[:, :]).then_inc(selected, 1)
                pool.wait_ge(selected, 4)
        s.clear()


def prepare_weights(nc, tag, units, ident):
    with ExitStack() as ctx:
        s = Scope(nc, ctx, tag)
        widest = max(w.shape[0] // P * w.shape[1] for w, _, _ in units)
        natural = [s.sb(f"natural{i}", [P, widest]) for i in range(3)]
        turned = [s.ps(f"turned{i}", [P, 512]) for i in range(3)]
        loaded = [s.sem(f"loaded{i}") for i in range(3)]
        turned_full, unit_read, hi_done, lo_done = (s.sem(n) for n in ("turned_full", "unit_read", "hi_done", "lo_done"))
        strips = [(u, k) for u, (w, _, _) in enumerate(units) for k in range(w.shape[1] // P)]

        def view(u):
            w = units[u][0]
            return natural[u % 3][:, 0:w.shape[0] // P * w.shape[1]].rearrange("p (o i) -> p o i", i=w.shape[1])

        with nc.Block() as block:

            @block.sync
            def _(sp):
                for u, (w, _, _) in enumerate(units):
                    if u >= 3:
                        sp.wait_ge(unit_read, u - 2)
                    sp.dma_start(view(u), w.rearrange("(o p) i -> p o i", p=P)).then_inc(loaded[u % 3], 16)

            @block.tensor
            def _(pe):
                for n, (u, k) in enumerate(strips):
                    w = units[u][0]
                    if k == 0:
                        pe.wait_ge(loaded[u % 3], 16 * (u // 3 + 1))
                    if n >= 3:
                        pe.wait_ge(lo_done, n - 2)
                    for o in range(w.shape[0] // P):
                        last = pe.transpose(turned[n % 3][:, o * P:(o + 1) * P], view(u)[:, o, k * P:(k + 1) * P], ident[:, :])
                    last.then_inc(turned_full, 1)
                    if k == w.shape[1] // P - 1:
                        pe.wait_ge(turned_full, n + 1)
                        pe.sem_inc(unit_read, 1)

            @block.scalar
            def _(act):
                for n, (u, k) in enumerate(strips):
                    w, hi, _ = units[u]
                    act.wait_ge(turned_full, n + 1)
                    act.activation(hi[:, k, :], turned[n % 3][:, 0:w.shape[0]], ACT.Copy).then_inc(hi_done, 1)

            @block.vector
            def _(dve):
                for n, (u, k) in enumerate(strips):
                    w, hi, lo = units[u]
                    dve.wait_ge(hi_done, n + 1)
                    dve.tensor_tensor(lo[:, k, :], turned[n % 3][:, 0:w.shape[0]], hi[:, k, :].bitcast(F32),
                                      ALU.subtract).then_inc(lo_done, 1)
                dve.wait_ge(lo_done, len(strips))
        s.clear()


def group_norm_affine(nc, x, xs, gamma, beta, group_mean, scale, shift):
    with ExitStack() as ctx:
        s = Scope(nc, ctx, "gn")
        stats = s.sb("stats", [P, B, CC, 2, 6])
        moments = s.sb("moments", [P, B, CC, 2])
        square = s.sb("square", [P, B, CC])
        var = s.sb("var", [P, B, CC])
        std = s.sb("std", [P, B, CC])
        gb = s.sb("gb", [P, 2, CC])
        mean_ps = s.ps("mean_ps", [P, B, CC, 2])
        loaded = [s.sem(f"loaded{b}") for b in range(B)]
        gb_loaded, stats_done, chain, averaged, rooted = (s.sem(n) for n in ("gb_loaded", "stats_done", "chain", "averaged", "rooted"))
        with nc.Block() as block:

            @block.sync
            def _(sp):
                for b in range(B):
                    for c in range(CC):
                        sp.dma_start(xs[:, b, c, :], x[b, c * P:(c + 1) * P].rearrange("p h w -> p (h w)")).then_inc(loaded[b], 16)
                sp.dma_start(gb[:, 0, :], gamma.rearrange("(c p) -> p c", p=P), allow_slow_non_contiguous=True).then_inc(gb_loaded, 16)
                sp.dma_start(gb[:, 1, :], beta.rearrange("(c p) -> p c", p=P), allow_slow_non_contiguous=True).then_inc(gb_loaded, 16)

            @block.tensor
            def _(pe):
                pe.wait_ge(chain, 3)
                pe.matmul(mean_ps[:, :, :, :], group_mean[:, :], moments[:, :, :, :], start=True, stop=True).then_inc(averaged, 1)

            @block.scalar
            def _(act):
                act.wait_ge(chain, 6)
                act.activation(std[:, :, :], var[:, :, :], ACT.Sqrt).then_inc(rooted, 1)

            @block.vector
            def _(dve):
                for b in range(B):
                    dve.wait_ge(loaded[b], 16 * CC)
                    for c in range(CC):
                        for h in range(2):
                            dve.bn_stats(stats[:, b, c, h, :], xs[:, b, c, h * 512:(h + 1) * 512]).then_inc(stats_done, 1)
                    dve.wait_ge(stats_done, (b + 1) * CC * 2 + b * CC)
                    for c in range(CC):
                        dve.bn_aggr(moments[:, b, c, :], stats[:, b, c, :, :]).then_inc(stats_done, 1)
                dve.wait_ge(stats_done, 3 * B * CC)
                dve.tensor_tensor(square[:, :, :], moments[:, :, :, 0], moments[:, :, :, 0], ALU.mult).then_inc(chain, 1)
                dve.wait_ge(chain, 1)
                dve.tensor_tensor(moments[:, :, :, 1], moments[:, :, :, 1], square[:, :, :], ALU.add).then_inc(chain, 2)
                dve.wait_ge(averaged, 1)
                dve.tensor_copy(moments[:, :, :, :], mean_ps[:, :, :, :]).then_inc(chain, 1)
                dve.wait_ge(chain, 4)
                dve.tensor_tensor(square[:, :, :], moments[:, :, :, 0], moments[:, :, :, 0], ALU.mult).then_inc(chain, 1)
                dve.wait_ge(chain, 5)
                dve.scalar_tensor_tensor(var[:, :, :], moments[:, :, :, 1], GN_EPS, square[:, :, :], ALU.add, ALU.subtract).then_inc(chain, 1)
                dve.wait_ge(rooted, 1)
                dve.reciprocal(var[:, :, :], std[:, :, :]).then_inc(chain, 1)
                dve.wait_ge(chain, 7)
                dve.wait_ge(gb_loaded, 32)
                for b in range(B):
                    dve.tensor_tensor(scale[:, b, :], var[:, b, :], gb[:, 0, :], ALU.mult).then_inc(chain, 1)
                dve.wait_ge(chain, 7 + B)
                dve.tensor_tensor(square[:, :, :], moments[:, :, :, 0], scale[:, :, :], ALU.mult).then_inc(chain, 1)
                dve.wait_ge(chain, 8 + B)
                for b in range(B):
                    dve.tensor_tensor(shift[:, b, :], gb[:, 1, :], square[:, b, :], ALU.subtract).then_inc(chain, 1)
                dve.wait_ge(chain, 8 + 2 * B)
        s.clear()


def split_product(pe, out, pairs, start=True, stop=True):
    n = 3 * len(pairs)
    k = 0
    for ah, al, bh, bl in pairs:
        for a, b in ((ah, bh), (ah, bl), (al, bh)):
            last = pe.matmul(out, a, b, start=start and k == 0, stop=stop and k == n - 1)
            k += 1
    return last


def conv_attention(nc, xs, x1, scale, shift, ident, w, bq, bk, bv, bp):
    SCALE = float(C) ** -0.5
    UNITS = 12 + 4 * NG
    SPLIT = 12 + 2 * NG
    with ExitStack() as ctx:
        s = Scope(nc, ctx, "conv")
        hn = s.sb("hn", [P, CC, T])
        hn_hi, hn_lo = s.sb("hn_hi", [P, CC, T], F32R), s.sb("hn_lo", [P, CC, T], F32R)
        q_hi, q_lo = s.sb("q_hi", [P, CC, T], F32R), s.sb("q_lo", [P, CC, T], F32R)
        k_hi, k_lo = s.sb("k_hi", [P, CC, T], F32R), s.sb("k_lo", [P, CC, T], F32R)
        v_hi, v_lo = s.sb("v_hi", [P, QB, C], F32R), s.sb("v_lo", [P, QB, C], F32R)
        probs = [s.sb(f"probs{i}", [P, T]) for i in range(2)]
        pt_hi, pt_lo = s.sb("pt_hi", [P, NG, QB, GQ * P], F32R), s.sb("pt_lo", [P, NG, QB, GQ * P], F32R)
        ao_hi, ao_lo = s.sb("ao_hi", [P, CC, GQ * P], F32R), s.sb("ao_lo", [P, CC, GQ * P], F32R)
        bias = s.sb("bias", [P, 4, CC])
        rowmax, negmax = s.sb("rowmax", [P, QB]), s.sb("negmax", [P, QB])
        rowsum, rowinv = s.sb("rowsum", [P, QB]), s.sb("rowinv", [P, QB])
        score = [s.ps(f"score{i}", [P, T]) for i in range(2)]
        turned = s.ps("turned", [P, QB, P])
        prod = [s.ps(f"prod{i}", [P, 512]) for i in range(2)]
        (bias_loaded, hn_ready, hn_act, hn_free, prod_full, unit_hi, unit_done, score_full, max_done, neg_done,
         exp_done, inv_done, probs_ready, turned_full, pt_hi_done, pt_lo_done, av_done, proj_done) = (
            s.sem(n) for n in ("bias_loaded", "hn_ready", "hn_act", "hn_free", "prod_full", "unit_hi", "unit_done",
                               "score_full", "max_done", "neg_done", "exp_done", "inv_done", "probs_ready",
                               "turned_full", "pt_hi_done", "pt_lo_done", "av_done", "proj_done"))
        stored = s.sem("stored")

        proj_units = [(n, o, h) for n in ("q", "k") for o in range(CC) for h in range(2)]
        bias_of = {"q": 0, "k": 1}
        dest = {"q": (q_hi, q_lo), "k": (k_hi, k_lo)}
        U_V, U_AV = len(proj_units), 12

        def av_unit(g, c):
            return U_AV + 4 * g + c

        with nc.Block() as block:

            @block.sync
            def _(sp):
                for n, src in enumerate((bq, bk, bv, bp)):
                    sp.dma_start(bias[:, n, :], src.rearrange("(c p) -> p c", p=P), allow_slow_non_contiguous=True).then_inc(bias_loaded, 16)
                with sp.Fori(0, B) as b:
                    sp.wait_ge(unit_done, (b + 1) * UNITS)
                    sp.dma_start(x1[b].rearrange("(c p) t -> p c t", p=P), xs[:, b, :, :]).then_inc(stored, 16)
                sp.wait_ge(stored, 16 * B)

            @block.tensor
            def _(pe):
                def free_bank(b, u):
                    pe.wait_ge(unit_done, b * UNITS + max(u - 1, 0))

                def qkv(b):
                    pe.wait_ge(hn_ready, (b + 1) * CC)
                    for u, (name, o, h) in enumerate(proj_units):
                        free_bank(b, u)
                        wh, wl = w[name]
                        cols, toks = slice(o * P, (o + 1) * P), slice(h * 512, (h + 1) * 512)
                        split_product(pe, prod[u % 2][:, :], [(wh[:, k, cols], wl[:, k, cols], hn_hi[:, k, toks], hn_lo[:, k, toks])
                                                              for k in range(CC)]).then_inc(prod_full, 1)
                    wh, wl = w["v"]
                    for n in range(QB // 2):
                        u = U_V + n
                        free_bank(b, u)
                        for t in (2 * n, 2 * n + 1):
                            toks = slice(t * P, (t + 1) * P)
                            last = split_product(pe, prod[u % 2][:, t % 2 * C:(t % 2 + 1) * C],
                                                 [(hn_hi[:, k, toks], hn_lo[:, k, toks], wh[:, k, :], wl[:, k, :]) for k in range(CC)])
                        last.then_inc(prod_full, 1)
                    pe.wait_ge(prod_full, b * UNITS + U_AV)
                    pe.sem_inc(hn_free, 1)

                def scores(b, i):
                    pe.wait_ge(exp_done, b * QB + max(i - 1, 0))
                    if i == 0:
                        pe.wait_ge(unit_done, b * UNITS + U_AV)
                    qs = slice(i * P, (i + 1) * P)
                    for h in range(2):
                        ks = slice(h * 512, (h + 1) * 512)
                        last = split_product(pe, score[i % 2][:, ks], [(q_hi[:, k, qs], q_lo[:, k, qs], k_hi[:, k, ks], k_lo[:, k, ks])
                                                                       for k in range(CC)])
                    last.then_inc(score_full, 1)

                def turn(b, i):
                    pe.wait_ge(probs_ready, b * QB + i + 1)
                    pe.wait_ge(pt_lo_done, b * QB + i)
                    for j in range(QB):
                        last = pe.transpose(turned[:, j, :], probs[i % 2][:, j * P:(j + 1) * P], ident[:, :])
                    last.then_inc(turned_full, 1)

                def av(b, g, c, half):
                    u = av_unit(g, c)
                    if half == 0:
                        free_bank(b, u)
                        pe.wait_ge(pt_lo_done, b * QB + (g + 1) * GQ)
                    cs = slice(c * P, (c + 1) * P)
                    js = range(half * QB // 2, (half + 1) * QB // 2)
                    last = split_product(pe, prod[u % 2][:, :], [(v_hi[:, j, cs], v_lo[:, j, cs], pt_hi[:, g, j, :], pt_lo[:, g, j, :])
                                                                 for j in js], start=half == 0, stop=half == 1)
                    if half == 1:
                        last.then_inc(prod_full, 1)

                def proj(b, g):
                    wh, wl = w["p"]
                    for o in range(CC):
                        u = av_unit(g, CC + o)
                        pe.wait_ge(unit_done, b * UNITS + av_unit(g, CC))
                        free_bank(b, u)
                        cols = slice(o * P, (o + 1) * P)
                        split_product(pe, prod[u % 2][:, :], [(wh[:, k, cols], wl[:, k, cols], ao_hi[:, k, :], ao_lo[:, k, :])
                                                              for k in range(CC)]).then_inc(prod_full, 1)

                def batch(b):
                    qkv(b)
                    scores(b, 0)
                    scores(b, 1)
                    for i in range(QB):
                        if i + 2 < QB:
                            scores(b, i + 2)
                        if i >= GQ:
                            av(b, 0, (i - GQ) // 2, (i - GQ) % 2)
                        turn(b, i)
                    proj(b, 0)
                    for q in range(4):
                        av(b, 1, q // 2, q % 2)
                    proj(b, 1)

                pe.wait_ge(bias_loaded, 64)
                batch(0)
                with pe.Fori(1, B) as b:
                    batch(b)

            def normalise(act, b):
                for c in range(CC):
                    act.activation(hn[:, c, :], xs[:, b, c, :], ACT.Identity, bias=shift[:, b, c:c + 1],
                                   scale=scale[:, b, c:c + 1]).then_inc(hn_act, 1)
                    act.wait_ge(hn_act, (2 * b * CC) + 2 * c + 1)
                    act.activation(hn_hi[:, c, :], hn[:, c, :], ACT.Copy).then_inc(hn_act, 1)

            @block.scalar
            def _(act):
                def hi(b, u, dst, bias_ap):
                    act.wait_ge(prod_full, b * UNITS + u + 1)
                    if bias_ap is None:
                        act.activation(dst, prod[u % 2][:, :], ACT.Copy).then_inc(unit_hi, 1)
                    else:
                        act.activation(dst, prod[u % 2][:, :], ACT.Identity, bias=bias_ap).then_inc(unit_hi, 1)

                def exps(b, i):
                    act.wait_ge(neg_done, b * QB + i + 1)
                    act.wait_ge(turned_full, b * QB + max(i - 1, 0))
                    act.activation(probs[i % 2][:, :], score[i % 2][:, :], ACT.Exp, bias=negmax[:, i:i + 1], scale=SCALE,
                                   accum_out=rowsum[:, i:i + 1]).then_inc(exp_done, 1)

                def pt(b, i):
                    act.wait_ge(turned_full, b * QB + i + 1)
                    act.wait_ge(av_done, b * NG)
                    act.activation(pt_hi[:, i // GQ, :, i % GQ * P:(i % GQ + 1) * P], turned[:, :, :], ACT.Copy).then_inc(pt_hi_done, 1)

                def ao(b, g, c):
                    act.wait_ge(proj_done, b * NG + g)
                    hi(b, av_unit(g, c), ao_hi[:, c, :], bias[:, 2, c:c + 1])

                def batch(b, last):
                    for u, (name, o, h) in enumerate(proj_units):
                        hi(b, u, dest[name][0][:, o, h * 512:(h + 1) * 512], bias[:, bias_of[name], o:o + 1])
                    for n in range(QB // 2):
                        hi(b, U_V + n, v_hi[:, 2 * n:2 * n + 2, :], None)
                    exps(b, 0)
                    exps(b, 1)
                    for i in range(QB):
                        if i + 2 < QB:
                            exps(b, i + 2)
                        pt(b, i)
                        if i == GQ + 1:
                            ao(b, 0, 0)
                    ao(b, 0, 1)
                    if not last:
                        act.wait_ge(hn_free, b + 1)
                        act.wait_ge(hn_ready, (b + 1) * CC)
                        normalise(act, b + 1)
                    ao(b, 1, 0)
                    ao(b, 1, 1)

                act.wait_ge(bias_loaded, 64)
                normalise(act, 0)
                batch(0, False)
                with act.Fori(1, B - 1) as b:
                    batch(b, False)
                batch(B - 1, True)

            @block.vector
            def _(dve):
                def normalise_lo(b):
                    for c in range(CC):
                        dve.wait_ge(hn_act, 2 * b * CC + 2 * c + 2)
                        dve.tensor_tensor(hn_lo[:, c, :], hn[:, c, :], hn_hi[:, c, :].bitcast(F32), ALU.subtract).then_inc(hn_ready, 1)

                def lo(b, u, n, dst, hi, bias_ap):
                    dve.wait_ge(unit_hi, b * SPLIT + n + 1)
                    if bias_ap is None:
                        dve.tensor_tensor(dst, prod[u % 2][:, :], hi.bitcast(F32), ALU.subtract).then_inc(unit_done, 1)
                    else:
                        dve.scalar_tensor_tensor(dst, prod[u % 2][:, :], bias_ap, hi.bitcast(F32), ALU.add, ALU.subtract).then_inc(unit_done, 1)

                def row_max(b, i):
                    dve.wait_ge(score_full, b * QB + i + 1)
                    dve.tensor_reduce(rowmax[:, i:i + 1], score[i % 2][:, :], AX.X, ALU.max).then_inc(max_done, 1)
                    dve.wait_ge(max_done, b * QB + i + 1)
                    dve.tensor_scalar(negmax[:, i:i + 1], rowmax[:, i:i + 1], -SCALE, None, ALU.mult).then_inc(neg_done, 1)

                def weigh(b, i):
                    dve.wait_ge(exp_done, b * QB + i + 1)
                    dve.reciprocal(rowinv[:, i:i + 1], rowsum[:, i:i + 1]).then_inc(inv_done, 1)
                    dve.wait_ge(inv_done, b * QB + i + 1)
                    dve.tensor_scalar(probs[i % 2][:, :], probs[i % 2][:, :], rowinv[:, i:i + 1], None, ALU.mult).then_inc(probs_ready, 1)

                def pt(b, i):
                    dve.wait_ge(pt_hi_done, b * QB + i + 1)
                    qs = slice(i % GQ * P, (i % GQ + 1) * P)
                    dve.tensor_tensor(pt_lo[:, i // GQ, :, qs], turned[:, :, :], pt_hi[:, i // GQ, :, qs].bitcast(F32), ALU.subtract).then_inc(pt_lo_done, 1)

                def ao(b, g, c):
                    lo(b, av_unit(g, c), 12 + 2 * g + c, ao_lo[:, c, :], ao_hi[:, c, :], bias[:, 2, c:c + 1])
                    if c == CC - 1:
                        dve.sem_inc(av_done, 1)

                def residual(b, g):
                    for o in range(CC):
                        u = av_unit(g, CC + o)
                        dve.wait_ge(prod_full, b * UNITS + u + 1)
                        xt = xs[:, b, o, g * 512:(g + 1) * 512]
                        dve.scalar_tensor_tensor(xt, prod[u % 2][:, :], bias[:, 3, o:o + 1], xt, ALU.add, ALU.add).then_inc(unit_done, 1)
                    dve.sem_inc(proj_done, 1)

                def batch(b, last):
                    for u, (name, o, h) in enumerate(proj_units):
                        hs = slice(h * 512, (h + 1) * 512)
                        lo(b, u, u, dest[name][1][:, o, hs], dest[name][0][:, o, hs], bias[:, bias_of[name], o:o + 1])
                    for n in range(QB // 2):
                        lo(b, U_V + n, U_V + n, v_lo[:, 2 * n:2 * n + 2, :], v_hi[:, 2 * n:2 * n + 2, :], None)
                    row_max(b, 0)
                    row_max(b, 1)
                    weigh(b, 0)
                    for i in range(QB):
                        if i + 2 < QB:
                            row_max(b, i + 2)
                        if i + 1 < QB:
                            weigh(b, i + 1)
                        pt(b, i)
                        if i == GQ + 1:
                            ao(b, 0, 0)
                    ao(b, 0, 1)
                    residual(b, 0)
                    if not last:
                        normalise_lo(b + 1)
                    ao(b, 1, 0)
                    ao(b, 1, 1)
                    residual(b, 1)

                dve.wait_ge(bias_loaded, 64)
                normalise_lo(0)
                batch(0, False)
                with dve.Fori(1, B - 1) as b:
                    batch(b, False)
                batch(B - 1, True)
                dve.wait_ge(unit_done, B * UNITS)


D = C
H = 8
HD = D // H
FF = 512
FC = FF // P
NT = T // P
PAIRS = NT // 2
MAX_NORM = 1.0 - 1e-5
F32_EPS = 2.0 ** -23
QK_GAIN = 64.0


def token_block(nc, x1, t2, ident, ident_h, w, norm1_w, norm2_w):
    SCALE = 2.0 / (float(HD) ** 0.5 * QK_GAIN ** 2)
    rounds = [(hg, qh) for qh in range(2) for hg in range(H // 4)]
    steps = [(r, kb) for r, (_, qh) in enumerate(rounds) for kb in range(4 * (qh + 1))]
    diagonal = [kb >= 4 * rounds[r][1] for r, kb in steps]
    NR, NS, ND = len(rounds), len(steps), sum(diagonal)
    O_STEP, X_STEP, ROOT_STEP = steps.index((NR - 2, 4)), steps.index((NR - 1, 2)), NS - 2

    def first_query(m):
        r, kb = steps[m]
        return max(kb * P - rounds[r][1] * 512, 0)

    with ExitStack() as ctx:
        s = Scope(nc, ctx, "block")
        xin = [s.sb(f"xin{i}", [P, CC, 2 * P]) for i in range(2)]
        t1, u, h = s.sb("t1", [P, NT, D]), s.sb("u", [P, NT, D]), s.sb("h", [P, NT, D])
        res = s.sb("res", [P, NT, D])
        hT = [s.sb(f"hT{i}", [P, CC, 2 * P], F32R) for i in range(2)]
        turned_hi, turned_lo = s.sb("turned_hi", [P, CC, T], F32R), s.sb("turned_lo", [P, CC, T], F32R)
        qk = s.sb("qk", [P, NT, 2, D])
        x2, h2 = qk[:, :, 0, :], qk[:, :, 1, :]
        v = s.sb("v", [P, NT, D])
        stack = s.sb("stack", [P, 2, 2, 2, H, 4, HD], F16)
        qkT = s.sb("qkT", [P, 2, H, T], F16)
        probs = s.sb("probs", [P, 2, 4, 512])
        ff_hi, ff_lo = s.sb("ff_hi", [P, FC, 512], F32R), s.sb("ff_lo", [P, FC, 512], F32R)
        n1, n2 = s.sb("n1", [P, D]), s.sb("n2", [P, D])
        mask = s.sb("mask", [P, P])
        ones = s.sb("ones", [P, HD])
        stats, mv = s.sb("stats", [P, NT, 6]), s.sb("mv", [P, NT, 2])
        roots = s.sb("roots", [P, 2, NT])
        mean_sq, late_root = s.sb("mean_sq", [P, NT]), s.sb("late_root", [P, NT])
        rstd, rr = roots[:, 0, :], roots[:, 1, :]
        hsq, alpha, hsq2 = (s.sb(n, [P, NT]) for n in ("hsq", "alpha", "hsq2"))
        ta, tb, tc, td = (s.sb(n, [P, 2 * NT]) for n in ("ta", "tb", "tc", "td"))
        gsq, fac = s.sb("gsq", [P, NT, 2]), s.sb("fac", [P, NT, 2])
        sq2 = s.sb("sq2", [P, 2, 2, 2, H])
        rr2, ball = s.sb("rr2", [P, NT]), s.sb("ball", [P, NT])
        junk, junk_qk = s.sb("junk", [P, D]), s.sb("junk_qk", [P, D])
        squares = [probs[:, i, 2:4, :] for i in range(2)]
        bank = s.ps("bank", [P, 8, 512])

        names = ("consts", "xin0", "xin1", "norm_loaded", "x_full", "x_copied", "stats_done", "front_scal", "front_act", "late_scal", "late_act", "res_done", "u_done", "h_done",
                 "hsq_done", "h_full", "hT_hi", "hT_lo", "qkv_full", "qk_copied", "v_copied", "gsq_done", "fac_done",
                 "scaled", "squared", "summed", "stack_hi", "stack_dup", "stack_lo", "stack_x", "stack_full", "qT_done", "kT_done",
                 "score_full", "exp_done", "masked", "av_step", "av_round", "inv_done", "attn_done", "aT_hi", "aT_lo",
                 "o_full", "x2_done", "x2sq_done", "h2_done", "h2_full", "h2T_hi", "h2T_lo", "gate_full", "silu_done", "ffprod_done",
                 "ff_hi_done", "ff_lo_done", "down_full", "o_added", "t2_done", "t2_stored", "log_done", "alpha_done", "passed")
        S = {n: s.sem(n) for n in names}

        FRONT_DVE, FRONT_ACT, LATE_DVE = 19, 6, 4

        def stack_bank(n):
            return 6 + n % 2 if n < 8 else n % 4

        def o_bank(pr):
            return 6 + pr if pr < 2 else 2 + pr

        def h2_bank(pr):
            return 2 + pr

        def attn_buf(r):
            return h[:, 2 * (r % 2):2 * (r % 2) + 2, :].rearrange("p a b -> p (a b)")

        with nc.Block() as block:

            @block.gpsimd
            def _(pool):
                pool.memset(ones[:, :], 1.0).then_inc(S["consts"], 1)
                pool.memset(mask[:, :], 1.0).then_inc(S["consts"], 1)
                for slot in range(2):
                    pool.memset(stack[:, slot, :, :, :, 3, :], 0.0).then_inc(S["consts"], 1)
                pool.wait_ge(S["consts"], 4)
                pool.affine_select(out=mask[:, :], in_=mask[:, :], compare_op=ALU.is_ge, fill=0.0, base=0,
                                   pattern=[[1, P]], channel_multiplier=-1).then_inc(S["consts"], 1)
                for slot in range(2):
                    pool.memset(stack[:, slot, 0, :, :, 3, 2:4], 1.0).then_inc(S["consts"], 1)
                    pool.memset(stack[:, slot, 1, :, :, 3, 0:2], 1.0).then_inc(S["consts"], 1)

                def second_high(b):
                    for pr in range(PAIRS):
                        pool.wait_ge(S["stack_hi"], b * 3 * PAIRS + (3 * pr + 1))
                        pool.sem_inc(S["passed"], 1)
                        st = stack[:, pr % 2, 0, :, :, :, :]
                        pool.tensor_copy(st[:, :, :, 2, :], st[:, :, :, 0, :]).then_inc(S["stack_dup"], 1)

                second_high(0)
                with pool.Fori(1, B) as b:
                    second_high(b)

            CONSTS = 9

            @block.sync
            def _(sp):
                for dst, src in ((n1, norm1_w), (n2, norm2_w)):
                    sp.dma_start(dst[:, :], src.rearrange("(a d) -> a d", a=1).to_broadcast((P, D))).then_inc(S["norm_loaded"], 16)

                def load(b, pr):
                    if not isinstance(b, int) or b or pr > 1:
                        sp.wait_ge(S["x_full"], b * PAIRS + (pr - 1))
                    sp.dma_start(xin[pr % 2][:, :, :], x1[b].rearrange("(c p) (n q) -> n p c q", p=P, q=2 * P)[pr]).then_inc(S[f"xin{pr % 2}"], 16)

                def store(b):
                    sp.wait_ge(S["t2_done"], (b + 1) * PAIRS)
                    sp.dma_start(t2.rearrange("(b t p) d -> b p t d", p=P, t=NT)[b], res[:, :, :]).then_inc(S["t2_stored"], 16)

                for pr in range(PAIRS):
                    load(0, pr)
                with sp.Fori(1, B) as b:
                    for pr in range(PAIRS):
                        load(b, pr)
                    store(b - 1)
                store(B - 1)
                sp.wait_ge(S["t2_stored"], 16 * B)

            @block.tensor
            def _(pe):
                def x_turned(b, pr):
                    pe.wait_ge(S[f"xin{pr % 2}"], 16 * (b * (PAIRS // 2) + (pr // 2 + 1)))
                    if not isinstance(b, int) or b > 0:
                        pe.wait_ge(S["attn_done"], (b - 1) * NR + (NR - 1))
                    if pr >= 2:
                        pe.wait_ge(S["x_copied"], b * PAIRS + (pr - 1))
                    for t in range(2):
                        for c in range(CC):
                            last = pe.transpose(bank[:, 4 + pr % 2, (t * CC + c) * P:(t * CC + c + 1) * P],
                                                xin[pr % 2][:, c, t * P:(t + 1) * P], ident[:, :])
                    last.then_inc(S["x_full"], 1)

                def h_turned(b, pr):
                    pe.wait_ge(S["h_done"], b * NT + (2 * pr + 2))
                    if pr == 0:
                        pe.wait_ge(S["attn_done"], b * NR)
                    else:
                        pe.wait_ge(S["v_copied"], b * NT + 2 * pr)
                    for c in range(CC):
                        for t in range(2):
                            last = pe.transpose(bank[:, 7, (c * 2 + t) * P:(c * 2 + t + 1) * P],
                                                h[:, 2 * pr + t, c * P:(c + 1) * P], ident[:, :])
                    last.then_inc(S["h_full"], 1)

                def qkv(b, t):
                    wh, wl = w["qkv"]
                    pe.wait_ge(S["hT_lo"], b * PAIRS + (t // 2 + 1))
                    pe.wait_ge(S["qk_copied"], b * NT + t)
                    toks = slice(t % 2 * P, (t % 2 + 1) * P)
                    for i, cols in ((0, slice(0, 512)), (1, slice(512, 768))):
                        if i == 1:
                            pe.wait_ge(S["v_copied"], b * NT + t)
                        last = split_product(pe, bank[:, 6 + i, 0:cols.stop - cols.start],
                                             [(hT[0][:, k, toks], hT[1][:, k, toks], wh[:, k, cols], wl[:, k, cols])
                                              for k in range(CC)])
                        last.then_inc(S["qkv_full"], 1)

                def stacks(b, pr):
                    for n in range(4 * pr, 4 * pr + 4):
                        t, side = n // 2, n % 2
                        pe.wait_ge(S["stack_x"], b * PAIRS + (pr + 1))
                        pe.wait_ge(S["stack_dup"], b * PAIRS + (pr + 1))
                        if n == 8:
                            pe.wait_ge(S["ffprod_done"], b * 2 * FC)
                        if n < 2:
                            pe.wait_ge(S["qk_copied"], (b + 1) * NT)
                            pe.wait_ge(S["v_copied"], (b + 1) * NT)
                        elif n < 8 or n >= 12:
                            pe.wait_ge(S[("qT_done", "kT_done")[side]], b * NT + (t if n < 8 else t - 1))
                        out = bank[:, stack_bank(n), :].bitcast(F16)
                        for hh in range(H):
                            last = pe.transpose(out[:, hh * P:(hh + 1) * P],
                                                stack[:, pr % 2, side, t % 2, hh, :, :], ident_h[:, :])
                        last.then_inc(S["stack_full"], 1)

                def attention(b, nb):
                    pe.wait_ge(S["qT_done"], b * NT + NT)
                    pe.wait_ge(S["kT_done"], b * NT + NT)

                    def scores(m):
                        r, kb = steps[m]
                        hg, qh = rounds[r]
                        q0 = first_query(m)
                        for p in range(2):
                            n = 2 * m + p
                            if n >= 2:
                                pe.wait_ge(S["exp_done"], b * 2 * NS + n - 1)
                            for i in range(2):
                                hh = 4 * hg + 2 * p + i
                                last = pe.matmul(bank[:, 2 * (n % 2) + i, q0:512], qkT[:, 1, hh, kb * P:(kb + 1) * P],
                                                 qkT[:, 0, hh, qh * 512 + q0:(qh + 1) * 512], start=True, stop=True)
                            last.then_inc(S["score_full"], 1)

                    def weigh(m):
                        r, kb = steps[m]
                        hg, qh = rounds[r]
                        q0 = first_query(m)
                        last_kb = 4 * (qh + 1) - 1
                        pe.wait_ge(S["exp_done"], b * 2 * NS + 2 * m + 2)
                        pe.wait_ge(S["masked"], b * ND + sum(diagonal[:m + 1]))
                        if m == 0:
                            pe.wait_ge(S["t2_done"], b * PAIRS)
                        if kb == 0 and r >= 2:
                            pe.wait_ge(S["attn_done"], b * NR + (r - 1))
                        if kb == 0 and r == NR - 1:
                            pe.wait_ge(S["o_added"], b * PAIRS + 2)
                        num, den = bank[:, 4 + 2 * (r % 2), :], bank[:, 5 + 2 * (r % 2), :]
                        for out, own in ((num, True), (den, False)):
                            for i in range(4):
                                hh = 4 * hg + i
                                lhs = v[:, kb, hh * HD:(hh + 1) * HD] if own else ones[:, :]
                                last = pe.matmul(out[i * HD:(i + 1) * HD, q0:512], lhs, probs[:, m % 2, i, q0:512],
                                                 start=kb == 0, stop=kb == last_kb)
                        last.then_inc(S["av_step"], 1)

                    scores(0)
                    for m in range(NS):
                        if m + 1 < NS:
                            scores(m + 1)
                        if m == X_STEP and nb is not None:
                            x_turned(nb, 0)
                            x_turned(nb, 1)
                        weigh(m)
                        if m == O_STEP:
                            output(b, 0)
                            output(b, 1)
                        if m == X_STEP + 1 and nb is not None:
                            x_turned(nb, 2)
                            x_turned(nb, 3)

                def output(b, pr, nb=None):
                    wh, wl = w["o"]
                    pe.wait_ge(S["aT_lo"], b * NR + (2 if pr < 2 else NR))
                    if pr < 2:
                        pe.wait_ge(S["attn_done"], b * NR + 2)
                    elif nb is not None:
                        pe.wait_ge(S["x_copied"], (nb + 1) * PAIRS)
                    for t in range(2):
                        toks = slice((2 * pr + t) * P, (2 * pr + t + 1) * P)
                        last = split_product(pe, bank[:, o_bank(pr), t * D:(t + 1) * D],
                                             [(turned_hi[:, k, toks], turned_lo[:, k, toks], wh[:, k, :], wl[:, k, :]) for k in range(CC)])
                    last.then_inc(S["o_full"], 1)

                def h2_turned(b, pr):
                    pe.wait_ge(S["h2_done"], b * NT + (2 * pr + 2))
                    for c in range(CC):
                        for t in range(2):
                            last = pe.transpose(bank[:, h2_bank(pr), (c * 2 + t) * P:(c * 2 + t + 1) * P],
                                                h2[:, 2 * pr + t, c * P:(c + 1) * P], ident[:, :])
                    last.then_inc(S["h2_full"], 1)

                def gate(b, n):
                    toks, cols = slice(n // FC * 512, (n // FC + 1) * 512), slice(n % FC * P, (n % FC + 1) * P)
                    pe.wait_ge(S["h2T_lo"], b * PAIRS + (2 if n < FC else PAIRS))
                    if n >= 2:
                        pe.wait_ge(S["ffprod_done"], b * 2 * FC + (n - 1))
                    for i in range(2):
                        wh, wl = w[("gate", "up")[i]]
                        last = split_product(pe, bank[:, 2 * (n % 2) + i, :],
                                             [(wh[:, k, cols], wl[:, k, cols], turned_hi[:, k, toks], turned_lo[:, k, toks])
                                              for k in range(CC)])
                    last.then_inc(S["gate_full"], 1)

                def down(b, pr):
                    wh, wl = w["down"]
                    g = pr // 2
                    pe.wait_ge(S["ff_lo_done"], b * 2 * FC + (g + 1) * FC)
                    if g == 1:
                        pe.wait_ge(S["t2_done"], b * PAIRS + (pr - 1))
                    else:
                        pe.wait_ge(S["h2T_lo"], (b + 1) * PAIRS)
                    for t in range(2):
                        own = slice((2 * pr + t) % 4 * P, ((2 * pr + t) % 4 + 1) * P)
                        last = split_product(pe, bank[:, 4 + pr % 2, t * D:(t + 1) * D],
                                             [(ff_hi[:, f, own], ff_lo[:, f, own], wh[:, f, :], wl[:, f, :]) for f in range(FC)])
                    last.then_inc(S["down_full"], 1)

                def first_front():
                    for pr in range(PAIRS):
                        x_turned(0, pr)
                    for pr in range(PAIRS):
                        h_turned(0, pr)
                        qkv(0, 2 * pr)
                        qkv(0, 2 * pr + 1)
                    for pr in range(PAIRS):
                        stacks(0, pr)

                def late(b, nb):
                    h2_turned(b, 0)
                    h2_turned(b, 1)
                    gate(b, 0)
                    output(b, 2, nb)
                    output(b, 3, nb)
                    gate(b, 1)
                    h_turned(nb, 0)
                    gate(b, 2)
                    qkv(nb, 0)
                    qkv(nb, 1)
                    h_turned(nb, 1)
                    h2_turned(b, 2)
                    h2_turned(b, 3)
                    qkv(nb, 2)
                    qkv(nb, 3)
                    h_turned(nb, 2)
                    gate(b, 3)
                    qkv(nb, 4)
                    qkv(nb, 5)
                    h_turned(nb, 3)
                    down(b, 0)
                    qkv(nb, 6)
                    qkv(nb, 7)
                    down(b, 1)
                    gate(b, 4)
                    gate(b, 5)
                    stacks(nb, 0)
                    gate(b, 6)
                    stacks(nb, 1)
                    gate(b, 7)
                    stacks(nb, 2)
                    down(b, 2)
                    stacks(nb, 3)
                    down(b, 3)

                def last_late(b):
                    h2_turned(b, 0)
                    h2_turned(b, 1)
                    gate(b, 0)
                    output(b, 2)
                    output(b, 3)
                    gate(b, 1)
                    gate(b, 2)
                    h2_turned(b, 2)
                    h2_turned(b, 3)
                    gate(b, 3)
                    gate(b, 4)
                    down(b, 0)
                    down(b, 1)
                    for n in range(5, 8):
                        gate(b, n)
                    down(b, 2)
                    down(b, 3)

                pe.wait_ge(S["consts"], CONSTS)
                first_front()
                attention(0, 1)
                late(0, 1)
                with pe.Fori(1, B - 1) as b:
                    attention(b, b + 1)
                    late(b, b + 1)
                attention(B - 1, None)
                last_late(B - 1)

            @block.scalar
            def _(act):
                def x_copy(b, pr):
                    act.wait_ge(S["x_full"], b * PAIRS + (pr + 1))
                    act.wait_ge(S["res_done"], b * PAIRS)
                    act.activation(t1[:, 2 * pr:2 * pr + 2, :], bank[:, 4 + pr % 2, :], ACT.Copy).then_inc(S["x_copied"], 1)

                def norm_roots(b):
                    act.wait_ge(S["front_scal"], b * FRONT_DVE + 4)
                    act.activation(tb[:, :], ta[:, :], ACT.Sqrt).then_inc(S["front_act"], 1)

                def lengths(b, ts):
                    for t in ts:
                        act.wait_ge(S["h_done"], b * NT + (t + 1))
                        act.wait_ge(S["hsq_done"], b * NT + t)
                        act.activation(junk[:, :], h[:, t, :], ACT.Square, accum_out=hsq[:, t:t + 1]).then_inc(S["hsq_done"], 1)

                def length_roots(b):
                    act.wait_ge(S["hsq_done"], (b + 1) * NT)
                    act.activation(ta[:, 0:NT], hsq[:, :], ACT.Sqrt, scale=0.25).then_inc(S["front_act"], 1)

                def h_high(b, pr):
                    act.wait_ge(S["h_full"], b * PAIRS + (pr + 1))
                    act.wait_ge(S["qkv_full"], b * 2 * NT + 4 * pr)
                    act.activation(hT[0][:, :, :], bank[:, 7, :].rearrange("p (c q) -> p c q", c=CC), ACT.Copy).then_inc(S["hT_hi"], 1)

                def logs(b):
                    act.wait_ge(S["front_scal"], b * FRONT_DVE + 11)
                    act.activation(ta[:, 0:NT], tc[:, 0:NT], ACT.Ln).then_inc(S["front_act"], 1)
                    act.activation(tb[:, 0:NT], td[:, 0:NT], ACT.Ln).then_inc(S["front_act"], 1)

                def qk_copy(b, t):
                    act.wait_ge(S["qkv_full"], b * 2 * NT + (2 * t + 1))
                    act.activation(qk[:, t, :, :], bank[:, 6, :], ACT.Copy).then_inc(S["qk_copied"], 1)
                    act.wait_ge(S["qk_copied"], b * NT + (t + 1))
                    for side in range(2):
                        act.wait_ge(S["gsq_done"], b * 2 * NT + (2 * t + side))
                        act.activation(junk_qk[:, :], qk[:, t, side, :], ACT.Square,
                                       accum_out=gsq[:, t, side:side + 1]).then_inc(S["gsq_done"], 1)

                def qk_roots(b):
                    act.wait_ge(S["gsq_done"], (b + 1) * 2 * NT)
                    act.wait_ge(S["alpha_done"], b + 1)
                    act.activation(ta[:, :], gsq[:, :, :], ACT.Sqrt).then_inc(S["front_act"], 1)

                def tanhs(b):
                    act.wait_ge(S["front_scal"], b * FRONT_DVE + 16)
                    act.activation(tc[:, :], tb[:, :], ACT.Tanh).then_inc(S["front_act"], 1)

                def stack_high(b, pr):
                    act.wait_ge(S["scaled"], b * PAIRS + (pr + 1))
                    act.wait_ge(S["stack_full"], b * 2 * NT + max(pr - 1, 0) * 4)
                    act.wait_ge(S["summed"], b * PAIRS + max(pr - 1, 0))
                    act.activation(squares[pr % 2].rearrange("p a b -> p (a b)"), qk[:, 2 * pr:2 * pr + 2, :, :].rearrange("p a b c -> p (a b c)"),
                                   ACT.Square).then_inc(S["squared"], 1)
                    act.activation(stack[:, pr % 2, 0, :, :, 0, :],
                                   qk[:, 2 * pr:2 * pr + 2, 0, :].rearrange("p t (h d) -> p t h d", h=H), ACT.Copy).then_inc(S["stack_hi"], 1)
                    for t in range(2):
                        act.activation(stack[:, pr % 2, 1, t, :, 0:2, :],
                                       qk[:, 2 * pr + t, 1, :].rearrange("p (h g d) -> p h g d", h=H, g=1).to_broadcast((P, H, 2, HD)),
                                       ACT.Copy).then_inc(S["stack_hi"], 1)

                def attention(b, nb):
                    for m in range(NS):
                        q0 = first_query(m)
                        act.wait_ge(S["av_step"], b * NS + max(m - 1, 0))
                        for p in range(2):
                            n = 2 * m + p
                            act.wait_ge(S["score_full"], b * 2 * NS + n + 1)
                            src = bank[:, 2 * (n % 2):2 * (n % 2) + 2, q0:512]
                            act.activation(probs[:, m % 2, 2 * p:2 * p + 2, q0:512], src, ACT.Exp, scale=SCALE).then_inc(S["exp_done"], 1)
                        if steps[m][1] == 2 and steps[m][0] > 0:
                            aT(b, steps[m][0] - 1)
                        if nb is not None and m in (X_STEP + 1, X_STEP + 2):
                            for pr in (2 * (m - X_STEP) - 2, 2 * (m - X_STEP) - 1):
                                x_copy(nb, pr)
                        if m in (O_STEP + 3, O_STEP + 4):
                            late_squares(b, m - O_STEP - 3)
                        if m == ROOT_STEP:
                            late_roots(b, 0)
                            if nb is not None:
                                norm_roots(nb)

                def late_squares(b, pr):
                    for t in (2 * pr, 2 * pr + 1):
                        act.wait_ge(S["x2_done"], b * PAIRS + (pr + 1))
                        act.wait_ge(S["x2sq_done"], b * NT + t)
                        act.activation(junk[:, :], x2[:, t, :], ACT.Square, accum_out=hsq2[:, t:t + 1]).then_inc(S["x2sq_done"], 1)

                def late_roots(b, half):
                    act.wait_ge(S["late_scal"], b * LATE_DVE + (2 * half + 1))
                    ts = slice(half * NT // 2, (half + 1) * NT // 2)
                    act.activation(late_root[:, ts], mean_sq[:, ts], ACT.Sqrt).then_inc(S["late_act"], 1)

                def h2_high(b, pr):
                    act.wait_ge(S["h2_full"], b * PAIRS + (pr + 1))
                    act.activation(turned_hi[:, :, pr * 256:(pr + 1) * 256],
                                   bank[:, h2_bank(pr), :].rearrange("p (c q) -> p c q", c=CC), ACT.Copy).then_inc(S["h2T_hi"], 1)

                def silu(b, n):
                    act.wait_ge(S["gate_full"], b * 2 * FC + (n + 1))
                    if n >= 2:
                        act.wait_ge(S["ffprod_done"], b * 2 * FC + (n - 1))
                    act.activation(probs[:, 0, n % 2, :], bank[:, 2 * (n % 2), :], ACT.Silu).then_inc(S["silu_done"], 1)

                def ff_high(b, n):
                    act.wait_ge(S["ffprod_done"], b * 2 * FC + (n + 1))
                    act.wait_ge(S["down_full"], b * PAIRS + n // FC * 2)
                    act.activation(ff_hi[:, n % FC, :], probs[:, 1, n % 2, :], ACT.Copy).then_inc(S["ff_hi_done"], 1)

                def q_turned(b, pr):
                    for t in (2 * pr, 2 * pr + 1):
                        act.wait_ge(S["stack_full"], b * 2 * NT + 2 * t + 1)
                        act.activation(qkT[:, 0, :, t * P:(t + 1) * P],
                                       bank[:, stack_bank(2 * t), :].bitcast(F16).rearrange("p (h q) -> p h q", h=H), ACT.Copy).then_inc(S["qT_done"], 1)

                def aT(b, r):
                    hg, qh = rounds[r]
                    act.wait_ge(S["attn_done"], b * NR + r + 1)
                    act.activation(turned_hi[:, hg, qh * 512:(qh + 1) * 512], attn_buf(r), ACT.Copy).then_inc(S["aT_hi"], 1)

                def first_front():
                    for pr in range(PAIRS):
                        x_copy(0, pr)
                    norm_roots(0)
                    h_high(0, 0)
                    lengths(0, range(NT))
                    length_roots(0)
                    logs(0)
                    for pr in range(PAIRS):
                        qk_copy(0, 2 * pr)
                        qk_copy(0, 2 * pr + 1)
                        if pr < PAIRS - 1:
                            h_high(0, pr + 1)
                    qk_roots(0)
                    tanhs(0)
                    for pr in range(PAIRS):
                        stack_high(0, pr)
                        if pr > 0:
                            q_turned(0, pr - 1)
                    q_turned(0, PAIRS - 1)

                def late(b, nb):
                    h2_high(b, 0)
                    h2_high(b, 1)
                    aT(b, NR - 1)
                    silu(b, 0)
                    late_squares(b, 2)
                    late_squares(b, 3)
                    late_roots(b, 1)
                    h_high(nb, 0)
                    silu(b, 1)
                    ff_high(b, 0)
                    qk_copy(nb, 0)
                    qk_copy(nb, 1)
                    h_high(nb, 1)
                    h2_high(b, 2)
                    h2_high(b, 3)
                    ff_high(b, 1)
                    silu(b, 2)
                    lengths(nb, range(0, 4))
                    qk_copy(nb, 2)
                    qk_copy(nb, 3)
                    ff_high(b, 2)
                    h_high(nb, 2)
                    lengths(nb, range(4, NT))
                    length_roots(nb)
                    silu(b, 3)
                    qk_copy(nb, 4)
                    qk_copy(nb, 5)
                    ff_high(b, 3)
                    h_high(nb, 3)
                    logs(nb)
                    qk_copy(nb, 6)
                    qk_copy(nb, 7)
                    qk_roots(nb)
                    silu(b, 4)
                    tanhs(nb)
                    ff_high(b, 4)
                    silu(b, 5)
                    stack_high(nb, 0)
                    ff_high(b, 5)
                    stack_high(nb, 1)
                    q_turned(nb, 0)
                    silu(b, 6)
                    ff_high(b, 6)
                    stack_high(nb, 2)
                    q_turned(nb, 1)
                    silu(b, 7)
                    ff_high(b, 7)
                    stack_high(nb, 3)
                    q_turned(nb, 2)
                    q_turned(nb, 3)

                def last_late(b):
                    h2_high(b, 0)
                    h2_high(b, 1)
                    aT(b, NR - 1)
                    silu(b, 0)
                    late_squares(b, 2)
                    late_squares(b, 3)
                    late_roots(b, 1)
                    for n in range(2 * FC):
                        if n < 2 * FC - 1:
                            silu(b, n + 1)
                        ff_high(b, n)
                        if n == 1:
                            h2_high(b, 2)
                            h2_high(b, 3)

                act.wait_ge(S["consts"], CONSTS)
                first_front()
                attention(0, 1)
                late(0, 1)
                with act.Fori(1, B - 1) as b:
                    attention(b, b + 1)
                    late(b, b + 1)
                attention(B - 1, None)
                last_late(B - 1)

            @block.vector
            def _(dve):
                FS, LS = S["front_scal"], S["late_scal"]
                count = [0]

                def chain(b):
                    count[0] += 1
                    dve.wait_ge(FS, b * FRONT_DVE + count[0])

                def statistics(b):
                    count[0] = 0
                    for pr in range(PAIRS):
                        dve.wait_ge(S["x_copied"], b * PAIRS + (pr + 1))
                        for t in (2 * pr, 2 * pr + 1):
                            dve.bn_stats(stats[:, t, :], t1[:, t, :]).then_inc(S["stats_done"], 1)
                    dve.wait_ge(S["stats_done"], b * 2 * NT + NT)
                    dve.sem_inc(S["passed"], 1)
                    for t in range(NT):
                        dve.bn_aggr(mv[:, t, :], stats[:, t, :]).then_inc(S["stats_done"], 1)
                    dve.wait_ge(S["stats_done"], (b + 1) * 2 * NT)
                    var = mv[:, :, 1]
                    dve.tensor_scalar(ta[:, 0:NT], var, LN_EPS, None, ALU.add).then_inc(FS, 1)
                    chain(b)
                    dve.reciprocal(tc[:, 0:NT], ta[:, 0:NT]).then_inc(FS, 1)
                    chain(b)
                    dve.tensor_tensor(td[:, 0:NT], tc[:, 0:NT], var, ALU.mult).then_inc(FS, 1)
                    chain(b)
                    dve.tensor_scalar(ta[:, NT:2 * NT], td[:, 0:NT], F32_EPS, None, ALU.add).then_inc(FS, 1)
                    chain(b)

                def norm_factors(b):
                    dve.wait_ge(S["front_act"], b * FRONT_ACT + 1)
                    dve.reciprocal(roots[:, :, :], tb[:, :].rearrange("p (a t) -> p a t", a=2)).then_inc(FS, 1)
                    chain(b)

                def normalised(b, ts):
                    for t in ts:
                        dve.tensor_scalar(u[:, t, :], t1[:, t, :], mv[:, t, 0:1], rstd[:, t:t + 1], ALU.subtract, ALU.mult).then_inc(S["u_done"], 1)
                    for t in ts:
                        h_tile(b, t)

                def h_tile(b, t):
                    dve.wait_ge(S["u_done"], b * NT + (t + 1))
                    dve.scalar_tensor_tensor(h[:, t, :], u[:, t, :], rr[:, t:t + 1], n1[:, :], ALU.mult, ALU.mult).then_inc(S["h_done"], 1)

                def h_low(b, pr):
                    dve.wait_ge(S["hT_hi"], b * PAIRS + (pr + 1))
                    dve.tensor_tensor(hT[1][:, :, :], bank[:, 7, :].rearrange("p (c q) -> p c q", c=CC),
                                      hT[0][:, :, :].bitcast(F32), ALU.subtract).then_inc(S["hT_lo"], 1)

                def v_copy(b, t):
                    dve.wait_ge(S["qkv_full"], b * 2 * NT + (2 * t + 2))
                    dve.tensor_copy(v[:, t, :], bank[:, 7, 0:D]).then_inc(S["v_copied"], 1)

                def onto_ball(b):
                    dve.wait_ge(S["front_act"], b * FRONT_ACT + 2)
                    dve.tensor_scalar(tb[:, 0:NT], ta[:, 0:NT], MAX_NORM, None, ALU.max).then_inc(FS, 1)
                    chain(b)
                    dve.reciprocal(tc[:, 0:NT], tb[:, 0:NT]).then_inc(FS, 1)
                    chain(b)
                    dve.scalar_tensor_tensor(tb[:, 0:NT], tc[:, 0:NT], MAX_NORM, ta[:, 0:NT], ALU.mult, ALU.mult).then_inc(FS, 1)
                    dve.tensor_scalar(alpha[:, :], tc[:, 0:NT], 0.5 * MAX_NORM, None, ALU.mult).then_inc(FS, 1)
                    chain(b)
                    chain(b)
                    dve.tensor_scalar(ball[:, :], tb[:, 0:NT], 1e-6, MAX_NORM, ALU.max, ALU.min).then_inc(FS, 1)
                    chain(b)
                    dve.tensor_scalar(tc[:, 0:NT], ball[:, :], 1.0, None, ALU.add).then_inc(S["log_done"], 1)
                    dve.wait_ge(S["log_done"], b + 1)
                    dve.tensor_scalar(td[:, 0:NT], ball[:, :], -1.0, 1.0, ALU.mult, ALU.add).then_inc(FS, 1)
                    chain(b)

                def log_factor(b):
                    dve.wait_ge(S["front_act"], b * FRONT_ACT + 4)
                    dve.tensor_tensor(tc[:, 0:NT], ta[:, 0:NT], tb[:, 0:NT], ALU.subtract).then_inc(FS, 1)
                    chain(b)
                    dve.reciprocal(td[:, 0:NT], ball[:, :]).then_inc(FS, 1)
                    chain(b)
                    dve.scalar_tensor_tensor(td[:, 0:NT], tc[:, 0:NT], 0.5, td[:, 0:NT], ALU.mult, ALU.mult).then_inc(FS, 1)
                    chain(b)
                    dve.tensor_tensor(alpha[:, :], alpha[:, :], td[:, 0:NT], ALU.mult).then_inc(S["alpha_done"], 1)
                    dve.wait_ge(S["alpha_done"], b + 1)

                alphas = alpha[:, :].rearrange("p (t a) -> p t a", a=1).to_broadcast((P, NT, 2))

                def tangent_length(b):
                    dve.wait_ge(S["front_act"], b * FRONT_ACT + 5)
                    dve.tensor_tensor(td[:, :].rearrange("p (t a) -> p t a", a=2), ta[:, :].rearrange("p (t a) -> p t a", a=2), alphas, ALU.mult).then_inc(FS, 1)
                    chain(b)
                    dve.tensor_scalar(tb[:, :], td[:, :], 1e-6, None, ALU.max).then_inc(FS, 1)
                    chain(b)

                def factors(b):
                    dve.wait_ge(S["front_act"], b * FRONT_ACT + 6)
                    dve.reciprocal(ta[:, :], tb[:, :]).then_inc(FS, 1)
                    chain(b)
                    dve.tensor_tensor(tb[:, :], ta[:, :], tc[:, :], ALU.mult).then_inc(FS, 1)
                    chain(b)
                    dve.tensor_tensor(tc[:, :], tb[:, :], td[:, :], ALU.mult).then_inc(FS, 1)
                    chain(b)
                    assert count[0] == FRONT_DVE
                    dve.tensor_scalar(td[:, :], tc[:, :], MAX_NORM, 1.0 / (MAX_NORM * QK_GAIN), ALU.max, ALU.mult).then_inc(S["fac_done"], 1)
                    dve.wait_ge(S["fac_done"], b * 4 + 1)
                    dve.reciprocal(tc[:, :], td[:, :]).then_inc(S["fac_done"], 1)
                    dve.wait_ge(S["fac_done"], b * 4 + 2)
                    dve.tensor_tensor(td[:, :], tc[:, :], tb[:, :], ALU.mult).then_inc(S["fac_done"], 1)
                    dve.wait_ge(S["fac_done"], b * 4 + 3)
                    dve.tensor_tensor(fac[:, :, :], td[:, :].rearrange("p (t a) -> p t a", a=2), alphas, ALU.mult).then_inc(S["fac_done"], 1)
                    dve.wait_ge(S["fac_done"], b * 4 + 4)
                    dve.wait_ge(S["gsq_done"], (b + 1) * 2 * NT)

                def scale_qk(b, pr):
                    ts = slice(2 * pr, 2 * pr + 2)
                    dve.tensor_tensor(qk[:, ts, :, :].rearrange("p t s d -> p (t s) d"), qk[:, ts, :, :].rearrange("p t s d -> p (t s) d"),
                                      fac[:, ts, :].rearrange("p t s -> p (t s)").rearrange("p (n a) -> p n a", a=1).to_broadcast((P, 4, D)), ALU.mult).then_inc(S["scaled"], 1)

                def stack_low(b, pr):
                    ts = slice(2 * pr, 2 * pr + 2)
                    dve.wait_ge(S["squared"], b * PAIRS + (pr + 1))
                    dve.tensor_reduce(sq2[:, pr % 2, :, :, :].rearrange("p t s h -> p (t s h)"),
                                      squares[pr % 2].rearrange("p a (n d) -> p (a n) d", d=HD), AX.X, ALU.add).then_inc(S["summed"], 1)
                    for side in range(2):
                        dve.wait_ge(S["stack_hi"], b * 3 * PAIRS + (3 * pr + 1 + 2 * side))
                        st = stack[:, pr % 2, side, :, :, :, :]
                        src = qk[:, ts, side, :].rearrange("p t (h d) -> p t h d", h=H)
                        dve.tensor_tensor(st[:, :, :, 1 + side, :], src, st[:, :, :, 0, :], ALU.subtract).then_inc(S["stack_lo"], 1)
                    dve.wait_ge(S["summed"], b * PAIRS + (pr + 1))
                    for side in range(2):
                        row = 2 * side
                        x = stack[:, pr % 2, side, :, :, 3, row:row + 2]
                        sq = sq2[:, pr % 2, :, side, :]
                        dve.tensor_scalar(x[:, :, :, 0], sq, -0.5, None, ALU.mult).then_inc(S["inv_done"], 1)
                    dve.wait_ge(S["inv_done"], b * INV + (2 * pr + 2))
                    dve.wait_ge(S["stack_lo"], b * 2 * PAIRS + 2 * (pr + 1))
                    for side in range(2):
                        row = 2 * side
                        x = stack[:, pr % 2, side, :, :, 3, row:row + 2]
                        sq = sq2[:, pr % 2, :, side, :]
                        last = dve.scalar_tensor_tensor(x[:, :, :, 1], sq, -0.5, x[:, :, :, 0], ALU.mult, ALU.subtract)
                        if side == 1:
                            last.then_inc(S["stack_x"], 1)

                def attention(b, nb):
                    for m in range(NS):
                        r, kb = steps[m]
                        q0 = first_query(m)
                        if diagonal[m]:
                            dve.wait_ge(S["exp_done"], b * 2 * NS + 2 * m + 2)
                            pm = probs[:, m % 2, :, q0:q0 + P]
                            dve.tensor_tensor(pm, pm, mask[:, :].rearrange("p (a q) -> p a q", a=1).to_broadcast((P, 4, P)), ALU.mult).then_inc(S["masked"], 1)
                        if kb == 1 and r > 0:
                            normalise(b, r - 1)
                        if kb == 3 and r > 0:
                            low_part(b, r - 1)
                        if (r, kb) == (2, 0):
                            input_sum(b)
                        if m in (O_STEP + 1, O_STEP + 2):
                            output_sum(b, m - O_STEP - 1)
                        if m == X_STEP - 1:
                            mean_square(b, 0)
                        if nb is not None and m == X_STEP + 3:
                            statistics(nb)
                        if m == ROOT_STEP + 1:
                            if nb is not None:
                                norm_factors(nb)
                            second_norm(b, 0)

                def last_round(b):
                    normalise(b, NR - 1)
                    low_part(b, NR - 1)

                def input_sum(b):
                    dve.wait_ge(S["t2_stored"], b * 16)
                    for pr in range(PAIRS):
                        ts = slice(2 * pr, 2 * pr + 2)
                        dve.tensor_tensor(res[:, ts, :], t1[:, ts, :], u[:, ts, :], ALU.add).then_inc(S["res_done"], 1)

                def output_sum(b, pr):
                    dve.wait_ge(S["o_full"], b * PAIRS + (pr + 1))
                    dve.wait_ge(S["res_done"], (b + 1) * PAIRS)
                    ts = slice(2 * pr, 2 * pr + 2)
                    out = bank[:, o_bank(pr), :].rearrange("p (t d) -> p t d", t=2)
                    dve.tensor_tensor(x2[:, ts, :], out, u[:, ts, :], ALU.add).then_inc(S["x2_done"], 1)
                    dve.tensor_tensor(res[:, ts, :], res[:, ts, :], out, ALU.add).then_inc(S["o_added"], 1)

                def mean_square(b, half):
                    dve.wait_ge(S["x2sq_done"], b * NT + (half + 1) * NT // 2)
                    ts = slice(half * NT // 2, (half + 1) * NT // 2)
                    dve.tensor_scalar(mean_sq[:, ts], hsq2[:, ts], 1.0 / D, F32_EPS, ALU.mult, ALU.add).then_inc(LS, 1)

                def second_norm(b, half):
                    dve.wait_ge(S["late_act"], b * 2 + (half + 1))
                    ts = slice(half * NT // 2, (half + 1) * NT // 2)
                    dve.reciprocal(rr2[:, ts], late_root[:, ts]).then_inc(LS, 1)
                    dve.wait_ge(LS, b * LATE_DVE + (2 * half + 2))
                    for t in range(half * NT // 2, (half + 1) * NT // 2):
                        dve.scalar_tensor_tensor(h2[:, t, :], x2[:, t, :], rr2[:, t:t + 1], n2[:, :], ALU.mult, ALU.mult).then_inc(S["h2_done"], 1)

                def h2_low(b, pr):
                    dve.wait_ge(S["h2T_hi"], b * PAIRS + (pr + 1))
                    ts = slice(pr * 256, (pr + 1) * 256)
                    dve.tensor_tensor(turned_lo[:, :, ts], bank[:, h2_bank(pr), :].rearrange("p (c q) -> p c q", c=CC),
                                      turned_hi[:, :, ts].bitcast(F32), ALU.subtract).then_inc(S["h2T_lo"], 1)

                def ff_product(b, n):
                    dve.wait_ge(S["silu_done"], b * 2 * FC + (n + 1))
                    if n >= 2:
                        dve.wait_ge(S["ff_lo_done"], b * 2 * FC + (n - 1))
                    dve.tensor_tensor(probs[:, 1, n % 2, :], probs[:, 0, n % 2, :], bank[:, 2 * (n % 2) + 1, :], ALU.mult).then_inc(S["ffprod_done"], 1)

                def ff_low(b, n):
                    dve.wait_ge(S["ff_hi_done"], b * 2 * FC + (n + 1))
                    dve.tensor_tensor(ff_lo[:, n % FC, :], probs[:, 1, n % 2, :], ff_hi[:, n % FC, :].bitcast(F32), ALU.subtract).then_inc(S["ff_lo_done"], 1)

                def add(b, pr):
                    dve.wait_ge(S["down_full"], b * PAIRS + (pr + 1))
                    dve.wait_ge(S["o_added"], b * PAIRS + (pr + 1))
                    ts = slice(2 * pr, 2 * pr + 2)
                    dve.tensor_tensor(res[:, ts, :], res[:, ts, :], bank[:, 4 + pr % 2, :].rearrange("p (t d) -> p t d", t=2), ALU.add).then_inc(S["t2_done"], 1)

                INV = 2 * PAIRS + NR

                def k_turned(b, n):
                    if n < 0:
                        return
                    dve.wait_ge(S["stack_full"], b * 2 * NT + n + 1)
                    dve.tensor_copy(qkT[:, 1, :, n // 2 * P:(n // 2 + 1) * P],
                                    bank[:, stack_bank(n), :].bitcast(F16).rearrange("p (h q) -> p h q", h=H)).then_inc(S["kT_done"], 1)

                def normalise(b, r):
                    hg, qh = rounds[r]
                    m = max(i for i in range(NS) if steps[i][0] == r)
                    dve.wait_ge(S["av_step"], b * NS + m + 1)
                    inv = h[:, 4 + 2 * (r % 2):6 + 2 * (r % 2), :].rearrange("p a b -> p (a b)")
                    num, den = bank[:, 4 + 2 * (r % 2), :], bank[:, 5 + 2 * (r % 2), :]
                    dve.reciprocal(inv, den).then_inc(S["inv_done"], 1)
                    dve.wait_ge(S["inv_done"], b * INV + 2 * PAIRS + r + 1)
                    dve.tensor_tensor(attn_buf(r), num, inv, ALU.mult).then_inc(S["attn_done"], 1)

                def low_part(b, r):
                    hg, qh = rounds[r]
                    dve.wait_ge(S["aT_hi"], b * NR + r + 1)
                    ts = slice(qh * 512, (qh + 1) * 512)
                    dve.tensor_tensor(turned_lo[:, hg, ts], attn_buf(r), turned_hi[:, hg, ts].bitcast(F32), ALU.subtract).then_inc(S["aT_lo"], 1)

                def first_front():
                    statistics(0)
                    norm_factors(0)
                    normalised(0, range(NT))
                    h_low(0, 0)
                    onto_ball(0)
                    for pr in range(PAIRS):
                        v_copy(0, 2 * pr)
                        v_copy(0, 2 * pr + 1)
                        if pr < PAIRS - 1:
                            h_low(0, pr + 1)
                    log_factor(0)
                    tangent_length(0)
                    factors(0)
                    scale_qk(0, 0)
                    for pr in range(PAIRS):
                        if pr < PAIRS - 1:
                            scale_qk(0, pr + 1)
                        stack_low(0, pr)
                        k_turned(0, 4 * pr + 1 - 4)
                        k_turned(0, 4 * pr + 3 - 4)
                    k_turned(0, 13)
                    k_turned(0, 15)

                def late(b, nb):
                    h2_low(b, 0)
                    h2_low(b, 1)
                    last_round(b)
                    normalised(nb, range(0, 4))
                    output_sum(b, 2)
                    output_sum(b, 3)
                    mean_square(b, 1)
                    ff_product(b, 0)
                    second_norm(b, 1)
                    h_low(nb, 0)
                    ff_low(b, 0)
                    ff_product(b, 1)
                    v_copy(nb, 0)
                    v_copy(nb, 1)
                    h_low(nb, 1)
                    h2_low(b, 2)
                    h2_low(b, 3)
                    normalised(nb, range(4, NT))
                    ff_low(b, 1)
                    ff_product(b, 2)
                    v_copy(nb, 2)
                    v_copy(nb, 3)
                    h_low(nb, 2)
                    ff_low(b, 2)
                    onto_ball(nb)
                    ff_product(b, 3)
                    v_copy(nb, 4)
                    v_copy(nb, 5)
                    ff_low(b, 3)
                    h_low(nb, 3)
                    add(b, 0)
                    v_copy(nb, 6)
                    v_copy(nb, 7)
                    log_factor(nb)
                    add(b, 1)
                    tangent_length(nb)
                    ff_product(b, 4)
                    factors(nb)
                    ff_low(b, 4)
                    scale_qk(nb, 0)
                    ff_product(b, 5)
                    scale_qk(nb, 1)
                    ff_low(b, 5)
                    stack_low(nb, 0)
                    scale_qk(nb, 2)
                    k_turned(nb, 1)
                    k_turned(nb, 3)
                    stack_low(nb, 1)
                    ff_product(b, 6)
                    ff_low(b, 6)
                    scale_qk(nb, 3)
                    k_turned(nb, 5)
                    k_turned(nb, 7)
                    stack_low(nb, 2)
                    ff_product(b, 7)
                    ff_low(b, 7)
                    k_turned(nb, 9)
                    k_turned(nb, 11)
                    stack_low(nb, 3)
                    add(b, 2)
                    k_turned(nb, 13)
                    k_turned(nb, 15)
                    add(b, 3)

                def last_late(b):
                    h2_low(b, 0)
                    h2_low(b, 1)
                    last_round(b)
                    output_sum(b, 2)
                    output_sum(b, 3)
                    mean_square(b, 1)
                    ff_product(b, 0)
                    second_norm(b, 1)
                    for n in range(2 * FC):
                        if n < 2 * FC - 1:
                            if n == FC:
                                add(b, 0)
                                add(b, 1)
                            ff_product(b, n + 1)
                        ff_low(b, n)
                        if n == 1:
                            h2_low(b, 2)
                            h2_low(b, 3)
                    add(b, 2)
                    add(b, 3)

                dve.wait_ge(S["norm_loaded"], 32)
                dve.wait_ge(S["consts"], CONSTS)
                first_front()
                attention(0, 1)
                late(0, 1)
                with dve.Fori(1, B - 1) as b:
                    attention(b, b + 1)
                    late(b, b + 1)
                attention(B - 1, None)
                last_late(B - 1)
                dve.wait_ge(S["t2_done"], B * PAIRS)


E_N = 8
HID = 1024
HC = HID // P
TILES = B * T // P
TOPK = 2
GT = 2
GS = GT * P
GROUPS = TILES * TOPK // GT + E_N - 1
ROW = 2 * D + 4
GAIN = 64.0
HID_GAIN = 16.0
TURNS = 4
AHEAD = 2


def route(nc, t2, rows, ident, gate_w, w1, w2, w1T, w2T, expert_of):
    PER = TILES // TURNS
    CH = 4
    BANKS = 8
    each = AHEAD * BANKS // TURNS
    own = {i * PER // each: [divmod(a * each + i, BANKS) for a in range(TURNS)] for i in range(each)}
    with ExitStack() as ctx:
        s = Scope(nc, ctx, "route")
        xrow = s.sb("xrow", [P, TILES, ROW], F16)
        tok = [s.sb(f"tok{i}", [P, PER, D]) for i in range(2)]
        natural = s.sb("natural", [P, CH, 4 * D])
        gT = s.sb("gT", [P, CC, E_N])
        xT = s.sb("xT", [P, 2, CC, P])
        stats, mv = s.sb("stats", [P, PER, 6]), s.sb("mv", [P, PER, 2])
        va, vb = s.sb("va", [P, PER]), s.sb("vb", [P, PER])
        top, idx = s.sb("top", [P, PER, 8]), s.sb("idx", [P, PER, 8], U32)
        logit = s.sb("logit", [P, PER, E_N])
        idxf = s.sb("idxf", [P, TILES, TOPK])
        oh = s.sb("oh", [P, TOPK, TILES, E_N])
        member = s.sb("member", [P, TILES, E_N])
        before = s.sb("before", [P, P])
        all_ones = s.sb("all_ones", [P, P])
        iota_e = s.sb("iota_e", [P, E_N])
        iota_t = s.sb("iota_t", [P, TILES // GT])
        iota_s = s.sb("iota_s", [1, GROUPS])
        within, total = s.sb("within", [P, TILES, E_N]), s.sb("total", [P, TILES, E_N])
        scan = s.sb("scan", [P, 2, TILES, E_N])
        cmp = s.sb("cmp", [P, E_N, TILES // GT])
        groups_e = s.sb("groups_e", [P, E_N])
        esc = s.sb("esc", [P, 2, E_N])
        posf, pos = s.sb("posf", [P, TILES]), s.sb("pos", [P, TOPK, TILES], U32)
        diff, wt = s.sb("diff", [P, TILES]), s.sb("wt", [P, TOPK, TILES])
        cmp_s, sum_s = s.sb("cmp_s", [1, GROUPS, E_N - 1]), s.sb("sum_s", [1, GROUPS])

        wbank = [s.ps(f"wbank{i}", [P, 512]) for i in range(4)]
        xbank = [s.ps(f"xbank{i}", [P, 512]) for i in range(2)]
        lbank = s.ps("lbank", [P, PER, E_N])
        pbank = s.ps("pbank", [P, 2, TILES * E_N])
        names = ("consts", "gate_loaded", "tok0", "tok1", "chunk0", "chunk1", "chunk2", "chunk3", "w_full", "w_hi", "w_lo",
                 "stats_done", "var_done", "root_done", "rstd_done", "x_done", "x_hi", "x_lo", "xT_full", "xT_copied",
                 "logit_full", "logit_copied", "top_done", "idx_done", "plan", "counted", "exp_done", "choice_kept", "weights_set",
                 "pos_done", "scattered", "map_done", "passed")
        S = {n: s.sem(n) for n in names}
        w1_v = w1.rearrange("e (a o p) d -> e a p o d", a=2, p=P)
        w2_v = w2.rearrange("e (a p) h -> e a p h", p=P)
        t2_v = t2.rearrange("(a t p) d -> a p t d", p=P, t=PER)

        def wdest(e, n):
            c, half = n // 2, n % 2
            if c < 2:
                return tuple(w1T[:, e, part, half, c * 512:(c + 1) * 512] for part in range(2))
            return tuple(w2T[:, e, part, half * 4:(half + 1) * 4, (c - 2) * P:(c - 1) * P] for part in range(2))

        def bank_ap(n):
            b = wbank[n % 4][:, :]
            return b if n // 2 < 2 else b.rearrange("p (h q) -> p h q", h=4)

        with nc.Block() as block:

            @block.gpsimd
            def _(pool):
                def load(a):
                    pool.dma_start(tok[a % 2][:, :, :], t2_v[a]).then_inc(S[f"tok{a % 2}"], 16)

                load(0)
                load(1)
                pool.memset(before[:, :], 1.0).then_inc(S["consts"], 1)
                pool.memset(all_ones[:, :], 1.0).then_inc(S["consts"], 1)
                pool.iota(iota_e[:, :], pattern=[[1, E_N]], base=0, channel_multiplier=0, allow_small_or_imprecise_dtypes=True).then_inc(S["consts"], 1)
                pool.iota(iota_t[:, :], pattern=[[GS, TILES // GT]], base=0, channel_multiplier=0, allow_small_or_imprecise_dtypes=True).then_inc(S["consts"], 1)
                pool.iota(iota_s[:, :], pattern=[[1, GROUPS]], base=0, channel_multiplier=0, allow_small_or_imprecise_dtypes=True).then_inc(S["consts"], 1)
                pool.iota(xrow[:, :, 2 * D:2 * D + 2].bitcast(U32).rearrange("p t a -> p (t a)"), pattern=[[P, TILES]], base=0, channel_multiplier=1).then_inc(S["consts"], 1)
                pool.wait_ge(S["consts"], 6)
                pool.affine_select(out=before[:, :], in_=before[:, :], compare_op=ALU.is_gt, fill=0.0, base=0,
                                   pattern=[[1, P]], channel_multiplier=-1).then_inc(S["consts"], 1)
                for a in range(2, TURNS):
                    pool.wait_ge(S["x_lo"], a - 1)
                    pool.wait_ge(S["xT_full"], (a - 1) * PER)
                    load(a)
                for k in range(TOPK):
                    pool.wait_ge(S["pos_done"], k + 1)
                    if k:
                        pool.wait_ge(S["scattered"], k * TILES * 16)
                        pool.tensor_copy(xrow[:, :, 2 * D + 2:2 * D + 4].bitcast(F32)[:, :, 0], wt[:, k, :]).then_inc(S["weights_set"], 1)
                    pool.wait_ge(S["weights_set"], k + 1)
                    for t in range(TILES):
                        pool.indirect_dma_start(rows, bass.IndirectOffsetOnAxis(ap=pos[:, k, t:t + 1], axis=0),
                                                xrow[:, t, :].bitcast(U32), None).then_inc(S["scattered"], 16)
                pool.wait_ge(S["scattered"], TOPK * TILES * 16)

            CONSTS = 7

            @block.sync
            def _(sp):
                def chunk(e, c):
                    src = w1_v[e, c] if c < 2 else w2_v[e, c - 2]
                    dst = natural[:, c, :].rearrange("p (o d) -> p o d", d=D) if c < 2 else natural[:, c, :]
                    sp.dma_start(dst, src).then_inc(S[f"chunk{c}"], 16)

                for k in range(CC):
                    sp.dma_start(gT[:, k, :], gate_w[:, k * P:(k + 1) * P].rearrange("e p -> p e"), allow_slow_non_contiguous=True).then_inc(S["gate_loaded"], 16)
                for c in range(CH):
                    chunk(0, c)
                with sp.Fori(0, E_N - 1) as e:
                    for c in range(CH):
                        sp.wait_ge(S["w_full"], e * BANKS + (2 * c + 2))
                        chunk(e + 1, c)

            @block.scalar
            def _(act):
                def weight(e, n):
                    act.wait_ge(S["w_full"], e * BANKS + n + 1)
                    act.activation(wdest(e, n)[0], bank_ap(n), ACT.Copy, scale=GAIN).then_inc(S["w_hi"], 1)

                def root(a):
                    act.wait_ge(S["var_done"], a + 1)
                    act.activation(vb[:, :], va[:, :], ACT.Sqrt).then_inc(S["root_done"], 1)

                root(0)
                for a in range(TURNS):
                    for i in range(PER):
                        act.wait_ge(S["xT_full"], a * PER + i + 1)
                        if a or i > 1:
                            act.wait_ge(S["logit_full"], a * PER + i - 1)
                        act.activation(xT[:, i % 2, :, :], xbank[i % 2][:, 0:CC * P].rearrange("p (c q) -> p c q", c=CC), ACT.Copy).then_inc(S["xT_copied"], 1)
                        if i == 0:
                            act.wait_ge(S["x_done"], (a + 1) * PER)
                            act.activation(xrow[:, a * PER:(a + 1) * PER, 0:D], tok[a % 2][:, :, :], ACT.Copy, scale=GAIN).then_inc(S["x_hi"], 1)
                        if i in own:
                            weight(*own[i][a])
                        if i == 4 and a + 1 < TURNS:
                            root(a + 1)
                act.wait_ge(S["choice_kept"], 2 * TURNS)
                act.activation(wt[:, 1, :], diff[:, :], ACT.Exp).then_inc(S["exp_done"], 1)
                with act.Fori(AHEAD, E_N) as e:
                    for n in range(BANKS):
                        weight(e, n)

            @block.tensor
            def _(pe):
                def weight(e, n):
                    c, half = n // 2, n % 2
                    if half == 0:
                        pe.wait_ge(S[f"chunk{c}"], 16 * (e + 1))
                    if n > 3 or not isinstance(e, int) or e > 0:
                        pe.wait_ge(S["w_lo"], e * BANKS + (n - 3))
                    for i in range(4):
                        src = natural[:, c, i * D + half * P:i * D + (half + 1) * P] if c < 2 else natural[:, c, (half * 4 + i) * P:(half * 4 + i + 1) * P]
                        last = pe.transpose(wbank[n % 4][:, i * P:(i + 1) * P], src, ident[:, :])
                    last.then_inc(S["w_full"], 1)

                def logits(a, i):
                    pe.wait_ge(S["xT_copied"], a * PER + i + 1)
                    if i == 0 and a:
                        pe.wait_ge(S["logit_copied"], a)
                    for k in range(CC):
                        last = pe.matmul(lbank[:, i, :], xT[:, i % 2, k, :], gT[:, k, :], start=k == 0, stop=k == CC - 1)
                    last.then_inc(S["logit_full"], 1)

                pe.wait_ge(S["gate_loaded"], 16 * CC)
                for a in range(TURNS):
                    for i in range(PER):
                        pe.wait_ge(S["x_done"], a * PER + i + 1)
                        if a or i > 1:
                            pe.wait_ge(S["xT_copied"], a * PER + i - 1)
                        for k in range(CC):
                            last = pe.transpose(xbank[i % 2][:, k * P:(k + 1) * P], tok[a % 2][:, i, k * P:(k + 1) * P], ident[:, :])
                        last.then_inc(S["xT_full"], 1)
                        if i in own:
                            weight(*own[i][a])
                        if i:
                            logits(a, i - 1)
                    logits(a, PER - 1)
                pe.wait_ge(S["consts"], CONSTS)
                pe.wait_ge(S["plan"], 3)
                flat = member[:, :, :].rearrange("p t e -> p (t e)")
                pe.matmul(pbank[:, 0, :], before[:, :], flat, start=True, stop=True).then_inc(S["counted"], 1)
                pe.matmul(pbank[:, 1, :], all_ones[:, :], flat, start=True, stop=True).then_inc(S["counted"], 1)
                with pe.Fori(AHEAD, E_N) as e:
                    for n in range(BANKS):
                        weight(e, n)

            @block.vector
            def _(dve):
                def weight(e, n):
                    dve.wait_ge(S["w_hi"], e * BANKS + n + 1)
                    hi, lo = wdest(e, n)
                    dve.scalar_tensor_tensor(lo, bank_ap(n), GAIN, hi, ALU.mult, ALU.subtract).then_inc(S["w_lo"], 1)

                def variance(a):
                    dve.wait_ge(S[f"tok{a % 2}"], 16 * (a // 2 + 1))
                    for i in range(PER):
                        dve.bn_stats(stats[:, i, :], tok[a % 2][:, i, :]).then_inc(S["stats_done"], 1)
                    dve.wait_ge(S["stats_done"], a * 2 * PER + PER)
                    for i in range(PER):
                        dve.bn_aggr(mv[:, i, :], stats[:, i, :]).then_inc(S["stats_done"], 1)
                    dve.wait_ge(S["stats_done"], (a + 1) * 2 * PER)
                    dve.tensor_scalar(va[:, :], mv[:, :, 1], LN_EPS, None, ALU.add).then_inc(S["var_done"], 1)

                def normalise(a):
                    dve.wait_ge(S["root_done"], a + 1)
                    dve.reciprocal(va[:, :], vb[:, :]).then_inc(S["rstd_done"], 1)
                    dve.wait_ge(S["rstd_done"], a + 1)
                    for i in range(PER):
                        dve.tensor_scalar(tok[a % 2][:, i, :], tok[a % 2][:, i, :], mv[:, i, 0:1], va[:, i:i + 1], ALU.subtract, ALU.mult).then_inc(S["x_done"], 1)

                def low_parts(a):
                    dve.wait_ge(S["x_hi"], a + 1)
                    rs = slice(a * PER, (a + 1) * PER)
                    dve.scalar_tensor_tensor(xrow[:, rs, D:2 * D], tok[a % 2][:, :, :], GAIN, xrow[:, rs, 0:D], ALU.mult, ALU.subtract).then_inc(S["x_lo"], 1)

                def choose(a):
                    dve.wait_ge(S["logit_full"], (a + 1) * PER)
                    dve.tensor_copy(logit[:, :, :], lbank[:, :, :]).then_inc(S["logit_copied"], 1)
                    dve.wait_ge(S["logit_copied"], a + 1)
                    for i in range(PER):
                        dve.max(top[:, i, :], logit[:, i, :]).then_inc(S["top_done"], 1)
                    dve.wait_ge(S["top_done"], (a + 1) * PER)
                    for i in range(PER):
                        dve.max_index(idx[:, i, :], top[:, i, :], logit[:, i, :]).then_inc(S["idx_done"], 1)
                    dve.wait_ge(S["idx_done"], (a + 1) * PER)
                    rs = slice(a * PER, (a + 1) * PER)
                    dve.tensor_copy(idxf[:, rs, :], idx[:, :, 0:TOPK]).then_inc(S["choice_kept"], 1)
                    dve.tensor_tensor(diff[:, rs], top[:, :, 1], top[:, :, 0], ALU.subtract).then_inc(S["choice_kept"], 1)
                    dve.wait_ge(S["choice_kept"], 2 * (a + 1))

                variance(0)
                normalise(0)
                for a in range(TURNS):
                    for i in range(PER):
                        if i in own:
                            weight(*own[i][a])
                        if i == 0:
                            low_parts(a)
                        if i == 3 and a + 1 < TURNS:
                            variance(a + 1)
                    if a + 1 < TURNS:
                        normalise(a + 1)
                    choose(a)

                plan = S["plan"]
                dve.wait_ge(S["consts"], CONSTS)
                for k in range(TOPK):
                    dve.tensor_tensor(oh[:, k, :, :], idxf[:, :, k:k + 1].to_broadcast((P, TILES, E_N)),
                                      iota_e[:, :].rearrange("p (a e) -> p a e", a=1).to_broadcast((P, TILES, E_N)), ALU.is_equal).then_inc(S["map_done"], 1)
                dve.wait_ge(S["map_done"], 2)
                dve.tensor_tensor(member[:, :, :], oh[:, 0, :, :], oh[:, 1, :, :], ALU.add).then_inc(plan, 3)
                dve.wait_ge(S["exp_done"], 1)
                dve.tensor_scalar(diff[:, :], wt[:, 1, :], 1.0, None, ALU.add).then_inc(plan, 1)
                dve.wait_ge(plan, 4)
                dve.reciprocal(wt[:, 0, :], diff[:, :]).then_inc(plan, 1)
                dve.wait_ge(plan, 5)
                dve.tensor_tensor(wt[:, 1, :], wt[:, 1, :], wt[:, 0, :], ALU.mult).then_inc(plan, 1)
                wfield = xrow[:, :, 2 * D + 2:2 * D + 4].bitcast(F32)
                dve.tensor_copy(wfield[:, :, 0], wt[:, 0, :]).then_inc(S["weights_set"], 1)
                dve.wait_ge(S["counted"], 2)
                dve.tensor_copy(within[:, :, :], pbank[:, 0, :].rearrange("p (t e) -> p t e", e=E_N)).then_inc(plan, 1)
                dve.tensor_copy(total[:, :, :], pbank[:, 1, :].rearrange("p (t e) -> p t e", e=E_N)).then_inc(plan, 1)
                dve.wait_ge(plan, 8)
                dve.tensor_copy(scan[:, 0, :, :], total[:, :, :]).then_inc(plan, 1)
                n, step, at = 9, 1, 0
                while step < TILES:
                    dve.wait_ge(plan, n)
                    dve.tensor_copy(scan[:, 1 - at, 0:step, :], scan[:, at, 0:step, :]).then_inc(plan, 1)
                    dve.tensor_tensor(scan[:, 1 - at, step:TILES, :], scan[:, at, step:TILES, :], scan[:, at, 0:TILES - step, :], ALU.add).then_inc(plan, 1)
                    n, step, at = n + 2, step * 2, 1 - at
                dve.wait_ge(plan, n)
                dve.tensor_tensor(cmp[:, :, :], scan[:, at, TILES - 1, :].rearrange("p (e a) -> p e a", a=1).to_broadcast((P, E_N, TILES // GT)),
                                  iota_t[:, :].rearrange("p (a t) -> p a t", a=1).to_broadcast((P, E_N, TILES // GT)), ALU.is_gt).then_inc(plan, 1)
                dve.tensor_tensor(scan[:, 1 - at, :, :], scan[:, at, :, :], total[:, :, :], ALU.subtract).then_inc(plan, 1)
                at = 1 - at
                n += 2
                dve.wait_ge(plan, n)
                dve.tensor_reduce(groups_e[:, :], cmp[:, :, :], AX.X, ALU.add).then_inc(plan, 1)
                dve.tensor_tensor(within[:, :, :], within[:, :, :], scan[:, at, :, :], ALU.add).then_inc(plan, 1)
                n += 2
                dve.wait_ge(plan, n)
                dve.tensor_copy(esc[:, 0, :], groups_e[:, :]).then_inc(plan, 1)
                n, step, ea = n + 1, 1, 0
                while step < E_N:
                    dve.wait_ge(plan, n)
                    dve.tensor_copy(esc[:, 1 - ea, 0:step], esc[:, ea, 0:step]).then_inc(plan, 1)
                    dve.tensor_tensor(esc[:, 1 - ea, step:E_N], esc[:, ea, step:E_N], esc[:, ea, 0:E_N - step], ALU.add).then_inc(plan, 1)
                    n, step, ea = n + 2, step * 2, 1 - ea
                dve.wait_ge(plan, n)
                ends = esc[0:1, ea, 0:E_N - 1]
                dve.tensor_tensor(cmp_s[:, :, :], iota_s[:, :].rearrange("p (s a) -> p s a", a=1).to_broadcast((1, GROUPS, E_N - 1)),
                                  ends.rearrange("p (a e) -> p a e", a=1).to_broadcast((1, GROUPS, E_N - 1)), ALU.is_ge).then_inc(plan, 1)
                dve.tensor_tensor(esc[:, 1 - ea, :], esc[:, ea, :], groups_e[:, :], ALU.subtract).then_inc(plan, 1)
                n += 2
                dve.wait_ge(plan, n)
                dve.tensor_reduce(sum_s[:, :], cmp_s[:, :, :], AX.X, ALU.add).then_inc(plan, 1)
                dve.scalar_tensor_tensor(within[:, :, :], esc[:, 1 - ea, :].rearrange("p (a e) -> p a e", a=1).to_broadcast((P, TILES, E_N)), float(GS),
                                         within[:, :, :], ALU.mult, ALU.add).then_inc(plan, 1)
                n += 2
                dve.wait_ge(plan, n)
                dve.tensor_copy(expert_of[:, :], sum_s[:, :]).then_inc(plan, 1)
                n += 1
                for k in range(TOPK):
                    dve.tensor_tensor(oh[:, k, :, :], oh[:, k, :, :], within[:, :, :], ALU.mult).then_inc(plan, 1)
                    n += 1
                    dve.wait_ge(plan, n)
                    dve.tensor_reduce(posf[:, :], oh[:, k, :, :], AX.X, ALU.add).then_inc(plan, 1)
                    n += 1
                    dve.wait_ge(plan, n)
                    dve.tensor_copy(pos[:, k, :], posf[:, :]).then_inc(S["pos_done"], 1)
                    dve.wait_ge(S["pos_done"], k + 1)
                with dve.Fori(AHEAD, E_N) as e:
                    for n in range(BANKS):
                        weight(e, n)


def experts(nc, acc, rows, ident_h, b1, b2, w1T, w2T, expert_of):
    with ExitStack() as ctx:
        s = Scope(nc, ctx, "moe")
        b1T, b2r = s.sb("b1T", [P, E_N, HC]), s.sb("b2r", [P, E_N, D])
        xin = [s.sb(f"xin{i}", [P, GT, ROW], F16) for i in range(2)]
        meta = [s.sb(f"meta{i}", [P, GT, 2]) for i in range(4)]
        xT = [s.sb(f"xT{i}", [P, 2, CC, GS], F16) for i in range(2)]
        hid = [s.sb(f"hid{i}", [P, HC, GS]) for i in range(2)]
        hid_hi = [s.sb(f"hid_hi{i}", [P, HC, GS], F16) for i in range(2)]
        hid_lo = [s.sb(f"hid_lo{i}", [P, HC, GS], F16) for i in range(2)]
        y = [s.sb(f"y{i}", [P, GT, D]) for i in range(2)]
        ysum = [s.sb(f"ysum{i}", [P, GT, D]) for i in range(2)]
        turned = s.ps("turned", [P, 2 * CC, GS], F16)
        hbank = s.ps("hbank", [P, HC, GS])
        ybank = [s.ps(f"ybank{i}", [P, GT, D]) for i in range(2)]
        names = ("bias_loaded", "in0", "in1", "turned_full", "xT_done", "h_full", "gelu_done", "hi_done", "lo_done", "y_full",
                 "meta_done", "ysum_done", "y_done", "added", "passed")
        S = {n: s.sem(n) for n in names}
        rows_v = rows.rearrange("(n t p) r -> n p t r", p=P, t=GT)

        def all_tiles(eng, step):
            for j in range(3):
                step(j, j)
            with eng.Fori(0, (GROUPS - 3) // 4) as i:
                for r in range(4):
                    step(i * 4 + (3 + r), (3 + r) % 4)

        assert (GROUPS - 3) % 4 == 0

        def early(j, n):
            return isinstance(j, int) and j < n

        with nc.Block() as block:

            @block.sync
            def _(sp):
                sp.dma_start(b1T[:, :, :], b1.rearrange("e (c p) -> p e c", p=P), allow_slow_non_contiguous=True).then_inc(S["bias_loaded"], 16)
                sp.dma_start(b2r[:, :, :], b2.rearrange("(a e) d -> a e d", a=1).to_broadcast((P, E_N, D))).then_inc(S["bias_loaded"], 16)

                def step(j, r):
                    if not early(j, 2):
                        sp.wait_ge(S["turned_full"], j - 1)
                        sp.wait_ge(S["meta_done"], j - 1)
                    sp.dma_start(xin[r % 2][:, :, :].bitcast(U32), rows_v[j]).then_inc(S[f"in{r % 2}"], 16)

                all_tiles(sp, step)

            @block.gpsimd
            def _(pool):
                def step(j, r):
                    pool.wait_ge(S["y_done"], j + 1)
                    if not early(j, 1):
                        pool.wait_ge(S["added"], j * (16 * GT))
                    pool.sem_inc(S["passed"], 1)
                    for t in range(GT):
                        pool.indirect_dma_start(acc, bass.IndirectOffsetOnAxis(ap=meta[r][:, t, 0:1].bitcast(U32), axis=0),
                                                y[r % 2][:, t, :], None, compute_op=ALU.add).then_inc(S["added"], 16)

                all_tiles(pool, step)
                pool.wait_ge(S["added"], GROUPS * 16 * GT)

            @block.tensor
            def _(pe):
                def expert(j):
                    return pe.value_load(expert_of[0:1, bass.ds(j, 1)], min_val=0, max_val=E_N - 1)

                def turn(j, r):
                    q = r % 2
                    pe.wait_ge(S[f"in{q}"], (j - q) * 8 + 16)
                    if not early(j, 1):
                        pe.wait_ge(S["xT_done"], j)
                    for part in range(2):
                        for k in range(CC):
                            for t in range(GT):
                                last = pe.transpose(turned[:, part * CC + k, t * P:(t + 1) * P],
                                                    xin[q][:, t, part * D + k * P:part * D + (k + 1) * P], ident_h[:, :])
                    last.then_inc(S["turned_full"], 1)

                def up(j, r):
                    q, e = r % 2, expert(j)
                    pe.wait_ge(S["xT_done"], j + 1)
                    for c in range(HC):
                        if c % 2 == 0 and not early(j, 1):
                            pe.wait_ge(S["gelu_done"], j * HC - (HC - 2 - c))
                        n = 0
                        for wp, xp in ((0, 0), (0, 1), (1, 0)):
                            for k in range(CC):
                                last = pe.matmul(hbank[:, c, :], w1T[:, e, wp, k, c * P:(c + 1) * P], xT[q][:, xp, k, :],
                                                 start=n == 0, stop=n == 5)
                                n += 1
                        if c % 2 == 1:
                            last.then_inc(S["h_full"], 1)

                def down(j, r):
                    q, e = r % 2, expert(j)
                    pe.wait_ge(S["lo_done"], j + 1)
                    if not early(j, 2):
                        pe.wait_ge(S["ysum_done"], j - 1)
                    for t in range(GT):
                        n = 0
                        for c in range(HC):
                            for hp, wp in ((0, 0), (0, 1), (1, 0)):
                                last = pe.matmul(ybank[q][:, t, :], (hid_hi, hid_lo)[hp][q][:, c, t * P:(t + 1) * P], w2T[:, e, wp, c, :],
                                                 start=n == 0, stop=n == 3 * HC - 1)
                                n += 1
                    last.then_inc(S["y_full"], 1)

                def step(j, r):
                    turn(j + 1, (r + 1) % 4)
                    up(j, r)
                    if not early(j, 1):
                        down(j - 1, (r - 1) % 4)

                turn(0, 0)
                for j in range(3):
                    step(j, j)
                with pe.Fori(0, (GROUPS - 3) // 4 - 1) as i:
                    for r in range(4):
                        step(i * 4 + (3 + r), (3 + r) % 4)
                for j in range(GROUPS - 4, GROUPS - 1):
                    step(j, j % 4)
                up(GROUPS - 1, (GROUPS - 1) % 4)
                down(GROUPS - 2, (GROUPS - 2) % 4)
                down(GROUPS - 1, (GROUPS - 1) % 4)

            @block.scalar
            def _(act):
                act.wait_ge(S["bias_loaded"], 32)

                def step(j, r):
                    q = r % 2
                    e = act.value_load(expert_of[0:1, bass.ds(j, 1)], min_val=0, max_val=E_N - 1)
                    if not early(j, 2):
                        act.wait_ge(S["lo_done"], j - 1)
                    for c in range(HC):
                        act.wait_ge(S["h_full"], j * (HC // 2) + (c // 2 + 1))
                        act.activation(hid[q][:, c, :], hbank[:, c, :], ACT.Gelu, bias=b1T[:, e, c:c + 1],
                                       scale=1.0 / (GAIN * GAIN)).then_inc(S["gelu_done"], 1)

                all_tiles(act, step)

            @block.vector
            def _(dve):
                dve.wait_ge(S["bias_loaded"], 32)

                def tokens(j, r):
                    q = r % 2
                    dve.wait_ge(S["turned_full"], j + 1)
                    dve.tensor_copy(xT[q][:, :, :, :], turned[:, :, :].rearrange("p (a c) q -> p a c q", a=2)).then_inc(S["xT_done"], 1)
                    if not early(j, 4):
                        dve.wait_ge(S["added"], (j - 3) * (16 * GT))
                    dve.tensor_copy(meta[r][:, :, :], xin[q][:, :, 2 * D:2 * D + 4].bitcast(F32)).then_inc(S["meta_done"], 1)

                def split(j, r):
                    q = r % 2
                    dve.wait_ge(S["gelu_done"], (j + 1) * HC)
                    dve.tensor_scalar(hid_hi[q][:, :, :], hid[q][:, :, :], HID_GAIN, None, ALU.mult).then_inc(S["hi_done"], 1)
                    dve.wait_ge(S["hi_done"], j + 1)
                    dve.scalar_tensor_tensor(hid_lo[q][:, :, :], hid[q][:, :, :], HID_GAIN, hid_hi[q][:, :, :], ALU.mult, ALU.subtract).then_inc(S["lo_done"], 1)

                def out(j, r):
                    q = r % 2
                    e = dve.value_load(expert_of[0:1, bass.ds(j, 1)], min_val=0, max_val=E_N - 1)
                    dve.wait_ge(S["y_full"], j + 1)
                    dve.scalar_tensor_tensor(ysum[q][:, :, :], ybank[q][:, :, :], 1.0 / (GAIN * HID_GAIN),
                                             b2r[:, bass.ds(e, 1), :].to_broadcast((P, GT, D)), ALU.mult, ALU.add).then_inc(S["ysum_done"], 1)
                    dve.wait_ge(S["ysum_done"], j + 1)
                    if not early(j, 2):
                        dve.wait_ge(S["added"], (j - 1) * (16 * GT))
                    for t in range(GT):
                        last = dve.tensor_scalar(y[q][:, t, :], ysum[q][:, t, :], meta[r][:, t, 1:2], None, ALU.mult)
                    last.then_inc(S["y_done"], 1)

                def step(j, r):
                    tokens(j + 1, (r + 1) % 4)
                    if not early(j, 2):
                        out(j - 2, (r - 2) % 4)
                    split(j, r)

                tokens(0, 0)
                for j in range(3):
                    step(j, j)
                with dve.Fori(0, (GROUPS - 3) // 4 - 1) as i:
                    for r in range(4):
                        step(i * 4 + (3 + r), (3 + r) % 4)
                for j in range(GROUPS - 4, GROUPS - 1):
                    step(j, j % 4)
                out(GROUPS - 3, (GROUPS - 3) % 4)
                split(GROUPS - 1, (GROUPS - 1) % 4)
                out(GROUPS - 2, (GROUPS - 2) % 4)
                out(GROUPS - 1, (GROUPS - 1) % 4)
                dve.wait_ge(S["y_done"], GROUPS)


def write_out(nc, acc, out, ident):
    PER = T // P
    with ExitStack() as ctx:
        s = Scope(nc, ctx, "out")
        tok = [s.sb(f"tok{i}", [P, PER, D]) for i in range(2)]
        res = [s.sb(f"res{i}", [P, CC, T]) for i in range(2)]
        bank = [s.ps(f"bank{i}", [P, 512]) for i in range(4)]
        loaded = [s.sem(f"loaded{i}") for i in range(2)]
        stored = [s.sem(f"stored{i}") for i in range(2)]
        full, copied, copied_act = (s.sem(n) for n in ("full", "copied", "copied_act"))
        src = acc[0:B * T, :].rearrange("(b t p) d -> b p t d", p=P, t=PER)
        UN = 2 * CC
        with nc.Block() as block:

            @block.sync
            def _(sp):
                for b in range(B):
                    if b >= 2:
                        sp.wait_ge(full, (b - 1) * UN)
                    sp.dma_start(tok[b % 2][:, :, :], src[b]).then_inc(loaded[b % 2], 16)

            @block.tensor
            def _(pe):
                for b in range(B):
                    pe.wait_ge(loaded[b % 2], 16 * (b // 2 + 1))
                    for n in range(UN):
                        c, h = n // 2, n % 2
                        if b:
                            pe.wait_ge((copied, copied_act)[n % 2], (b - 1) * 2 + n // 2 + 1)
                        for i in range(4):
                            last = pe.transpose(bank[n][:, i * P:(i + 1) * P], tok[b % 2][:, h * 4 + i, c * P:(c + 1) * P], ident[:, :])
                        last.then_inc(full, 1)

            def copies(eng, copy, sem, parity):
                for b in range(B):
                    if b >= 2:
                        eng.wait_ge(stored[b % 2], 16 * CC * (b // 2))
                    for n in range(parity, UN, 2):
                        c, h = n // 2, n % 2
                        eng.wait_ge(full, b * UN + n + 1)
                        copy(res[b % 2][:, c, h * 512:(h + 1) * 512], bank[n][:, :]).then_inc(sem, 1)

            @block.vector
            def _(dve):
                copies(dve, dve.tensor_copy, copied, 0)

            @block.scalar
            def _(act):
                copies(act, lambda o, i: act.activation(o, i, ACT.Copy), copied_act, 1)

            @block.gpsimd
            def _(pool):
                for b in range(B):
                    for c in range(CC):
                        pool.wait_ge(copied, b * CC + c + 1)
                        pool.wait_ge(copied_act, b * CC + c + 1)
                        pool.dma_start(out[b, c * P:(c + 1) * P].rearrange("p h w -> p (h w)"), res[b % 2][:, c, :]).then_inc(stored[b % 2], 16)
                for i in range(2):
                    pool.wait_ge(stored[i], 16 * CC * B // 2)


def fill_rows(nc, rows, blank, filled):
    with ExitStack() as ctx:
        s = Scope(nc, ctx, "fill")
        zeroed, numbered = s.sem("zeroed"), s.sem("numbered")
        with nc.Block() as block:

            @block.gpsimd
            def _(pool):
                pool.memset(blank[:, :, :], 0.0).then_inc(zeroed, 1)
                pool.wait_ge(zeroed, 1)
                pool.iota(blank[:, :, 2 * D:2 * D + 2].bitcast(U32), pattern=[[P, GT], [0, 1]], base=B * T, channel_multiplier=1).then_inc(numbered, 1)

            @block.sync
            def _(sp):
                sp.wait_ge(numbered, 1)
                for t in range(GT):
                    sp.dma_start(rows.rearrange("(n t p) r -> t p n r", p=P, t=GT)[t],
                                 blank[:, t:t + 1, :].bitcast(U32).to_broadcast((P, GROUPS, ROW // 2))).then_inc(filled, 16)
        s.clear()


def build(nc, x, p, out):
    x1 = nc.dram_tensor("x1_scratch", (B, C, T), F32).ap()
    acc = nc.dram_tensor("acc_scratch", (B * T + GT * P, D), F32).ap()
    rows = nc.dram_tensor("rows_scratch", (GROUPS * GS, ROW // 2), U32).ap()
    with ExitStack() as whole:
        s = Scope(nc, whole, "all")
        ident, ident_h = s.sb("ident", [P, P]), s.sb("ident_h", [P, P], F16)
        with ExitStack() as ctx:
            s = Scope(nc, ctx, "l0")
            group_mean = s.sb("group_mean", [P, P])
            filled = s.sem("filled")
            make_constants(nc, ident, ident_h, group_mean)
            fill_rows(nc, rows, s.sb("blank", [P, GT, ROW], F16), filled)
            xs = s.sb("xs", [P, B, CC, T])
            scale, shift = s.sb("scale", [P, B, CC]), s.sb("shift", [P, B, CC])
            w = {n: (s.sb(f"w{n}_hi", [P, CC, C], F32R), s.sb(f"w{n}_lo", [P, CC, C], F32R)) for n in "qkvp"}
            prepare_weights(nc, "w0", [(p[f"L0_conv_w{n}"], *w[n]) for n in "qkvp"], ident)
            group_norm_affine(nc, x, xs, p["L0_conv_norm_gamma"], p["L0_conv_norm_beta"], group_mean, scale, shift)
            conv_attention(nc, xs, x1, scale, shift, ident, w, *(p[f"L0_conv_b{n}"] for n in "qkvp"))
            with nc.Block() as block:

                @block.sync
                def _(sp):
                    sp.wait_ge(filled, 16 * GT)

        with ExitStack() as ctx:
            s = Scope(nc, ctx, "l1")
            qkv = [s.sb(f"qkv{i}", [P, CC, 3 * D], F32R) for i in range(2)]
            units = [(p[f"L1_attn_{n}_w"], *(t[:, :, i * D:(i + 1) * D] for t in qkv)) for i, n in enumerate("qkv")]
            w = {"qkv": qkv}
            for n, k, f in (("o", CC, D), ("gate", CC, FF), ("up", CC, FF), ("down", FC, D)):
                w[n] = [s.sb(f"{n}{i}", [P, k, f], F32R) for i in range(2)]
                units.append((p[f"L1_attn_{n}_w"], *w[n]))
            prepare_weights(nc, "w1", units, ident)
            token_block(nc, x1, acc[0:B * T, :], ident, ident_h, w, p["L1_attn_norm1_w"], p["L1_attn_norm2_w"])

        with ExitStack() as ctx:
            s = Scope(nc, ctx, "l2")
            w1T, w2T = s.sb("w1T", [P, E_N, 2, CC, HID], F16), s.sb("w2T", [P, E_N, 2, HC, D], F16)
            expert_of = s.sb("expert_of", [1, GROUPS], mybir.dt.int32)
            route(nc, acc[0:B * T, :], rows, ident, p["L1_ffn_gate_w"], p["L1_ffn_w1"], p["L1_ffn_w2"], w1T, w2T, expert_of)
            experts(nc, acc, rows, ident_h, p["L1_ffn_b1"], p["L1_ffn_b2"], w1T, w2T, expert_of)
        write_out(nc, acc, out, ident)


_INS = ["x"] + [f"L0_conv_{n}" for n in ("norm_gamma", "norm_beta", "wq", "bq", "wk", "bk", "wv", "bv", "wp", "bp")] \
    + [f"L1_attn_{n}" for n in ("q_w", "k_w", "v_w", "o_w", "gate_w", "up_w", "down_w", "norm1_w", "norm2_w")] \
    + [f"L1_ffn_{n}" for n in ("gate_w", "w1", "b1", "w2", "b2")]


def kernel(**inputs):
    import numpy as np
    from concourse import bacc
    from concourse.bass_utils import run_bass_kernel_spmd

    nc = bacc.Bacc("TRN2", target_bir_lowering=False, num_devices=1)
    arrays, args = {}, {}
    for name in _INS:
        a = np.ascontiguousarray(inputs[name])
        arrays[f"in_{name}"] = a
        args[name] = nc.dram_tensor(f"in_{name}", a.shape, mybir.dt.from_np(a.dtype), kind="ExternalInput").ap()
    out = nc.dram_tensor("out", inputs["x"].shape, F32, kind="ExternalOutput").ap()
    build(nc, args["x"], args, out)
    r = run_bass_kernel_spmd(nc, [arrays], core_ids=[0])
    return r.results[0]["out"]
```

```python
from contextlib import ExitStack

import concourse.bass as bass
from concourse import mybir

F32 = mybir.dt.float32
F32R = mybir.dt.float32r
F16 = mybir.dt.float16
U32 = mybir.dt.uint32
ALU = mybir.AluOpType
ACT = mybir.ActivationFunctionType
AX = mybir.AxisListType

P = 128
B = 4
C = 256
T = 1024
CC = C // P
GROUP = 8
QB = T // P
GQ = 4
NG = QB // GQ
GN_EPS = 1e-6
LN_EPS = 1e-5


class Scope:

    def __init__(self, nc, ctx, tag):
        self.nc, self.ctx, self.tag = nc, ctx, tag
        self.sems = []

    def sb(self, name, shape, dt=F32):
        return self.ctx.enter_context(self.nc.sbuf_tensor(f"{self.tag}_{name}", shape, dt))

    def ps(self, name, shape, dt=F32):
        return self.ctx.enter_context(self.nc.psum_tensor(f"{self.tag}_{name}", shape, dt))

    def sem(self, name):
        sem = self.ctx.enter_context(self.nc.semaphore(f"{self.tag}_{name}"))
        self.sems.append(sem)
        return sem

    def clear(self):
        with self.nc.Block() as block:

            @block.gpsimd
            def _(pool):
                for sem in self.sems:
                    pool.sem_clear(sem)


def make_constants(nc, ident, ident_h, group_mean):
    with ExitStack() as ctx:
        s = Scope(nc, ctx, "const")
        filled, selected = s.sem("filled"), s.sem("selected")
        with nc.Block() as block:

            @block.gpsimd
            def _(pool):
                pool.memset(ident[:, :], 0.0).then_inc(filled, 1)
                pool.memset(group_mean[:, :], 1.0 / GROUP).then_inc(filled, 1)
                pool.wait_ge(filled, 2)
                pool.affine_select(out=ident[:, :], in_=ident[:, :], compare_op=ALU.not_equal, fill=1.0,
                                   base=0, pattern=[[-1, P]], channel_multiplier=1).then_inc(selected, 1)
                gm = group_mean[:, :].rearrange("p (g r) -> p g r", r=GROUP)
                pool.affine_select(out=gm, in_=gm, compare_op=ALU.is_ge, fill=0.0, base=0,
                                   pattern=[[-GROUP, P // GROUP], [0, GROUP]],
                                   channel_multiplier=1).then_inc(selected, 1)
                pool.wait_ge(selected, 2)
                pool.affine_select(out=gm, in_=gm, compare_op=ALU.is_ge, fill=0.0, base=GROUP - 1,
                                   pattern=[[GROUP, P // GROUP], [0, GROUP]],
                                   channel_multiplier=-1).then_inc(selected, 1)
                pool.tensor_copy(ident_h[:, :], ident[:, :]).then_inc(selected, 1)
                pool.wait_ge(selected, 4)
        s.clear()


def prepare_weights(nc, tag, units, ident, further=()):
    with ExitStack() as ctx:
        s = Scope(nc, ctx, tag)
        widest = max(w.shape[0] // P * w.shape[1] for w, _, _ in units)
        natural = [s.sb(f"natural{i}", [P, widest]) for i in range(3)]
        turned = [s.ps(f"turned{i}", [P, 512]) for i in range(3)]
        loaded = [s.sem(f"loaded{i}") for i in range(3)]
        turned_full, unit_read, hi_done, lo_done = (s.sem(n) for n in ("turned_full", "unit_read", "hi_done", "lo_done"))
        strips = [(u, k) for u, (w, _, _) in enumerate(units) for k in range(w.shape[1] // P)]

        def view(u):
            w = units[u][0]
            return natural[u % 3][:, 0:w.shape[0] // P * w.shape[1]].rearrange("p (o i) -> p o i", i=w.shape[1])

        with nc.Block() as block:

            @block.sync
            def _(sp):
                for u, (w, _, _) in enumerate(units):
                    if u >= 3:
                        sp.wait_ge(unit_read, u - 2)
                    sp.dma_start(view(u), w.rearrange("(o p) i -> p o i", p=P)).then_inc(loaded[u % 3], 16)
                for dst, src, sem in further:
                    sp.dma_start(dst, src, allow_slow_non_contiguous=dst.shape[-1] < P).then_inc(sem, 16)

            @block.tensor
            def _(pe):
                for n, (u, k) in enumerate(strips):
                    w = units[u][0]
                    if k == 0:
                        pe.wait_ge(loaded[u % 3], 16 * (u // 3 + 1))
                    if n >= 3:
                        pe.wait_ge(lo_done, n - 2)
                    for o in range(w.shape[0] // P):
                        last = pe.transpose(turned[n % 3][:, o * P:(o + 1) * P], view(u)[:, o, k * P:(k + 1) * P], ident[:, :])
                    last.then_inc(turned_full, 1)
                    if k == w.shape[1] // P - 1:
                        pe.wait_ge(turned_full, n + 1)
                        pe.sem_inc(unit_read, 1)

            @block.scalar
            def _(act):
                for n, (u, k) in enumerate(strips):
                    w, hi, _ = units[u]
                    act.wait_ge(turned_full, n + 1)
                    act.activation(hi[:, k, :], turned[n % 3][:, 0:w.shape[0]], ACT.Copy).then_inc(hi_done, 1)

            @block.vector
            def _(dve):
                for n, (u, k) in enumerate(strips):
                    w, hi, lo = units[u]
                    dve.wait_ge(hi_done, n + 1)
                    dve.tensor_tensor(lo[:, k, :], turned[n % 3][:, 0:w.shape[0]], hi[:, k, :].bitcast(F32),
                                      ALU.subtract).then_inc(lo_done, 1)
                dve.wait_ge(lo_done, len(strips))
        s.clear()


class GroupNorm:

    def __init__(self, s, tag, b0, b1, xs, loaded, gb, gb_loaded, group_mean, scale, shift):
        self.b0, self.bs, self.n = b0, slice(b0, b1), b1 - b0
        self.xs, self.loaded, self.gb, self.gb_loaded, self.group_mean, self.scale, self.shift = xs, loaded, gb, gb_loaded, group_mean, scale, shift
        self.stats = s.sb(f"{tag}_stats", [P, self.n, CC, 2, 6])
        self.moments = s.sb(f"{tag}_moments", [P, self.n, CC, 2])
        self.square, self.var, self.std = (s.sb(f"{tag}_{n}", [P, self.n, CC]) for n in ("square", "var", "std"))
        self.stats_done, self.chain, self.averaged, self.rooted, self.ready = (
            s.sem(f"{tag}_{n}") for n in ("stats_done", "chain", "averaged", "rooted", "ready"))
        self.pieces = [(b, c, h) for b in range(b0, b1) for c in range(CC) for h in range(2)]

    def statistics(self, dve, n):
        b, c, h = self.pieces[n]
        if c == h == 0:
            dve.wait_ge(self.loaded[b], 16 * CC)
        dve.bn_stats(self.stats[:, b - self.b0, c, h, :], self.xs[:, b, c, h * 512:(h + 1) * 512]).then_inc(self.stats_done, 1)

    def channel_moments(self, dve):
        dve.wait_ge(self.stats_done, len(self.pieces))
        for b in range(self.n):
            for c in range(CC):
                dve.bn_aggr(self.moments[:, b, c, :], self.stats[:, b, c, :, :]).then_inc(self.stats_done, 1)
        dve.wait_ge(self.stats_done, len(self.pieces) + self.n * CC)
        dve.tensor_tensor(self.square[:, :, :], self.moments[:, :, :, 0], self.moments[:, :, :, 0], ALU.mult).then_inc(self.chain, 1)
        dve.wait_ge(self.chain, 1)
        dve.tensor_tensor(self.moments[:, :, :, 1], self.moments[:, :, :, 1], self.square[:, :, :], ALU.add).then_inc(self.chain, 1)

    def average(self, pe, out):
        pe.wait_ge(self.chain, 2)
        pe.matmul(out, self.group_mean[:, :], self.moments[:, :, :, :].rearrange("p b c m -> p (b c m)"), start=True, stop=True).then_inc(self.averaged, 1)

    def variance(self, dve, averages):
        dve.wait_ge(self.averaged, 1)
        dve.tensor_copy(self.moments[:, :, :, :].rearrange("p b c m -> p (b c m)"), averages).then_inc(self.chain, 1)
        dve.wait_ge(self.chain, 3)
        dve.tensor_tensor(self.square[:, :, :], self.moments[:, :, :, 0], self.moments[:, :, :, 0], ALU.mult).then_inc(self.chain, 1)
        dve.wait_ge(self.chain, 4)
        dve.scalar_tensor_tensor(self.var[:, :, :], self.moments[:, :, :, 1], GN_EPS, self.square[:, :, :], ALU.add, ALU.subtract).then_inc(self.chain, 1)

    def root(self, act):
        act.wait_ge(self.chain, 5)
        act.activation(self.std[:, :, :], self.var[:, :, :], ACT.Sqrt).then_inc(self.rooted, 1)

    def affine(self, dve):
        dve.wait_ge(self.rooted, 1)
        dve.reciprocal(self.var[:, :, :], self.std[:, :, :]).then_inc(self.chain, 1)
        dve.wait_ge(self.chain, 6)
        dve.wait_ge(self.gb_loaded, 32)
        gamma, beta = (self.gb[:, i, :].rearrange("p (b c) -> p b c", b=1).to_broadcast((P, self.n, CC)) for i in range(2))
        dve.tensor_tensor(self.scale[:, self.bs, :], self.var[:, :, :], gamma, ALU.mult).then_inc(self.chain, 1)
        dve.wait_ge(self.chain, 7)
        dve.tensor_tensor(self.square[:, :, :], self.moments[:, :, :, 0], self.scale[:, self.bs, :], ALU.mult).then_inc(self.chain, 1)
        dve.wait_ge(self.chain, 8)
        dve.tensor_tensor(self.shift[:, self.bs, :], beta, self.square[:, :, :], ALU.subtract).then_inc(self.ready, 1)
        dve.wait_ge(self.ready, 1)


def first_group_norm(nc, norm):
    with ExitStack() as ctx:
        s = Scope(nc, ctx, "gn")
        averages = s.ps("averages", [P, norm.n * CC * 2])
        with nc.Block() as block:

            @block.tensor
            def _(pe):
                norm.average(pe, averages[:, :])

            @block.scalar
            def _(act):
                norm.root(act)

            @block.vector
            def _(dve):
                for n in range(len(norm.pieces)):
                    norm.statistics(dve, n)
                norm.channel_moments(dve)
                norm.variance(dve, averages[:, :])
                norm.affine(dve)


def split_product(pe, out, pairs, start=True, stop=True):
    n = 3 * len(pairs)
    k = 0
    for ah, al, bh, bl in pairs:
        for a, b in ((ah, bh), (ah, bl), (al, bh)):
            last = pe.matmul(out, a, b, start=start and k == 0, stop=stop and k == n - 1)
            k += 1
    return last


def conv_attention(nc, xs, x1, scale, shift, norm, fills, ident, w, bias, bias_loaded):
    SCALE = float(C) ** -0.5
    UNITS = 12 + 4 * NG
    SPLIT = 12 + 2 * NG
    with ExitStack() as ctx:
        s = Scope(nc, ctx, "conv")
        hn = s.sb("hn", [P, CC, T])
        hn_hi, hn_lo = s.sb("hn_hi", [P, CC, T], F32R), s.sb("hn_lo", [P, CC, T], F32R)
        q_hi, q_lo = s.sb("q_hi", [P, CC, T], F32R), s.sb("q_lo", [P, CC, T], F32R)
        k_hi, k_lo = s.sb("k_hi", [P, CC, T], F32R), s.sb("k_lo", [P, CC, T], F32R)
        v_hi, v_lo = s.sb("v_hi", [P, QB, C], F32R), s.sb("v_lo", [P, QB, C], F32R)
        probs = [s.sb(f"probs{i}", [P, T]) for i in range(2)]
        pt_hi, pt_lo = s.sb("pt_hi", [P, NG, QB, GQ * P], F32R), s.sb("pt_lo", [P, NG, QB, GQ * P], F32R)
        ao_hi, ao_lo = s.sb("ao_hi", [P, CC, GQ * P], F32R), s.sb("ao_lo", [P, CC, GQ * P], F32R)
        rowmax, negmax = s.sb("rowmax", [P, QB]), s.sb("negmax", [P, QB])
        rowsum, rowinv = s.sb("rowsum", [P, QB]), s.sb("rowinv", [P, QB])
        score = [s.ps(f"score{i}", [P, T]) for i in range(2)]
        turned = s.ps("turned", [P, QB, P])
        prod = [s.ps(f"prod{i}", [P, 512]) for i in range(2)]
        (hn_ready, hn_act, hn_free, prod_full, unit_hi, unit_done, score_full, max_done, neg_done,
         exp_done, inv_done, probs_ready, turned_full, pt_hi_done, pt_lo_done, av_done, proj_done) = (
            s.sem(n) for n in ("hn_ready", "hn_act", "hn_free", "prod_full", "unit_hi", "unit_done",
                               "score_full", "max_done", "neg_done", "exp_done", "inv_done", "probs_ready",
                               "turned_full", "pt_hi_done", "pt_lo_done", "av_done", "proj_done"))
        stored = s.sem("stored")

        proj_units = [(n, o, h) for n in ("q", "k") for o in range(CC) for h in range(2)]
        bias_of = {"q": 0, "k": 1}
        dest = {"q": (q_hi, q_lo), "k": (k_hi, k_lo)}
        U_V, U_AV = len(proj_units), 12

        averages = turned[:, 0, 0:norm.n * CC * 2]

        def unit_bank(u):
            if u < U_AV and u % 4 >= 2:
                return turned[:, u % 2 * QB // 2:(u % 2 + 1) * QB // 2, :].rearrange("p j q -> p (j q)")
            return prod[u % 2][:, :]

        def av_unit(g, c):
            return U_AV + 4 * g + c

        with nc.Block() as block:

            @block.sync
            def _(sp):
                for dst, src, sem in fills:
                    sp.dma_start(dst, src).then_inc(sem, 16)
                with sp.Fori(0, B) as b:
                    sp.wait_ge(unit_done, (b + 1) * UNITS)
                    sp.dma_start(x1[b].rearrange("(c p) t -> p c t", p=P), xs[:, b, :, :]).then_inc(stored, 16)
                sp.wait_ge(stored, 16 * B)
                for _, _, sem in fills:
                    sp.wait_ge(sem, 16)

            @block.tensor
            def _(pe):
                def free_bank(b, u):
                    pe.wait_ge(unit_done, b * UNITS + max(u - 3 if u < U_AV else u - 1, 0))

                def qkv(b):
                    pe.wait_ge(hn_ready, (b + 1) * CC)
                    for u, (name, o, h) in enumerate(proj_units):
                        free_bank(b, u)
                        wh, wl = w[name]
                        cols, toks = slice(o * P, (o + 1) * P), slice(h * 512, (h + 1) * 512)
                        split_product(pe, unit_bank(u), [(wh[:, k, cols], wl[:, k, cols], hn_hi[:, k, toks], hn_lo[:, k, toks])
                                                              for k in range(CC)]).then_inc(prod_full, 1)
                    wh, wl = w["v"]
                    for n in range(QB // 2):
                        u = U_V + n
                        free_bank(b, u)
                        for t in (2 * n, 2 * n + 1):
                            toks = slice(t * P, (t + 1) * P)
                            last = split_product(pe, unit_bank(u)[:, t % 2 * C:(t % 2 + 1) * C],
                                                 [(hn_hi[:, k, toks], hn_lo[:, k, toks], wh[:, k, :], wl[:, k, :]) for k in range(CC)])
                        last.then_inc(prod_full, 1)
                    pe.wait_ge(prod_full, b * UNITS + U_AV)
                    pe.sem_inc(hn_free, 1)

                def scores(b, i):
                    pe.wait_ge(exp_done, b * QB + max(i - 1, 0))
                    if i == 0:
                        pe.wait_ge(unit_done, b * UNITS + U_AV)
                    qs = slice(i * P, (i + 1) * P)
                    for h in range(2):
                        ks = slice(h * 512, (h + 1) * 512)
                        last = split_product(pe, score[i % 2][:, ks], [(q_hi[:, k, qs], q_lo[:, k, qs], k_hi[:, k, ks], k_lo[:, k, ks])
                                                                       for k in range(CC)])
                    last.then_inc(score_full, 1)

                def turn(b, i):
                    pe.wait_ge(probs_ready, b * QB + i + 1)
                    pe.wait_ge(pt_lo_done, b * QB + i)
                    for j in range(QB):
                        last = pe.transpose(turned[:, j, :], probs[i % 2][:, j * P:(j + 1) * P], ident[:, :])
                    last.then_inc(turned_full, 1)

                def av(b, g, c, half):
                    u = av_unit(g, c)
                    if half == 0:
                        free_bank(b, u)
                        pe.wait_ge(pt_lo_done, b * QB + (g + 1) * GQ)
                    cs = slice(c * P, (c + 1) * P)
                    js = range(half * QB // 2, (half + 1) * QB // 2)
                    last = split_product(pe, unit_bank(u), [(v_hi[:, j, cs], v_lo[:, j, cs], pt_hi[:, g, j, :], pt_lo[:, g, j, :])
                                                                 for j in js], start=half == 0, stop=half == 1)
                    if half == 1:
                        last.then_inc(prod_full, 1)

                def proj(b, g):
                    wh, wl = w["p"]
                    for o in range(CC):
                        u = av_unit(g, CC + o)
                        pe.wait_ge(unit_done, b * UNITS + av_unit(g, CC))
                        free_bank(b, u)
                        cols = slice(o * P, (o + 1) * P)
                        split_product(pe, unit_bank(u), [(wh[:, k, cols], wl[:, k, cols], ao_hi[:, k, :], ao_lo[:, k, :])
                                                              for k in range(CC)]).then_inc(prod_full, 1)

                def batch(b, first=False):
                    qkv(b)
                    scores(b, 0)
                    scores(b, 1)
                    for i in range(QB):
                        if i + 2 < QB:
                            scores(b, i + 2)
                        if i >= GQ:
                            av(b, 0, (i - GQ) // 2, (i - GQ) % 2)
                        turn(b, i)
                    proj(b, 0)
                    if first:
                        pe.wait_ge(pt_lo_done, QB)
                        norm.average(pe, averages)
                    for q in range(4):
                        av(b, 1, q // 2, q % 2)
                    proj(b, 1)

                pe.wait_ge(bias_loaded, 64)
                batch(0, True)
                with pe.Fori(1, B) as b:
                    batch(b)

            def normalise(act, b):
                for c in range(CC):
                    act.activation(hn[:, c, :], xs[:, b, c, :], ACT.Identity, bias=shift[:, b, c:c + 1],
                                   scale=scale[:, b, c:c + 1]).then_inc(hn_act, 1)
                    act.wait_ge(hn_act, (2 * b * CC) + 2 * c + 1)
                    act.activation(hn_hi[:, c, :], hn[:, c, :], ACT.Copy).then_inc(hn_act, 1)

            @block.scalar
            def _(act):
                def hi(b, u, dst, bias_ap):
                    act.wait_ge(prod_full, b * UNITS + u + 1)
                    if bias_ap is None:
                        act.activation(dst, unit_bank(u), ACT.Copy).then_inc(unit_hi, 1)
                    else:
                        act.activation(dst, unit_bank(u), ACT.Identity, bias=bias_ap).then_inc(unit_hi, 1)

                def exps(b, i):
                    act.wait_ge(neg_done, b * QB + i + 1)
                    act.wait_ge(turned_full, b * QB + max(i - 1, 0))
                    act.activation(probs[i % 2][:, :], score[i % 2][:, :], ACT.Exp, bias=negmax[:, i:i + 1], scale=SCALE,
                                   accum_out=rowsum[:, i:i + 1]).then_inc(exp_done, 1)

                def pt(b, i):
                    act.wait_ge(turned_full, b * QB + i + 1)
                    act.wait_ge(av_done, b * NG)
                    act.activation(pt_hi[:, i // GQ, :, i % GQ * P:(i % GQ + 1) * P], turned[:, :, :], ACT.Copy).then_inc(pt_hi_done, 1)

                def ao(b, g, c):
                    act.wait_ge(proj_done, b * NG + g)
                    hi(b, av_unit(g, c), ao_hi[:, c, :], bias[:, 2, c:c + 1])

                def batch(b, last, first=False):
                    for u, (name, o, h) in enumerate(proj_units):
                        hi(b, u, dest[name][0][:, o, h * 512:(h + 1) * 512], bias[:, bias_of[name], o:o + 1])
                    for n in range(QB // 2):
                        hi(b, U_V + n, v_hi[:, 2 * n:2 * n + 2, :], None)
                    exps(b, 0)
                    exps(b, 1)
                    for i in range(QB):
                        pt(b, i)
                        if i + 2 < QB:
                            exps(b, i + 2)
                        if i == GQ + 1:
                            ao(b, 0, 0)
                    ao(b, 0, 1)
                    if first:
                        norm.root(act)
                        act.wait_ge(norm.ready, 1)
                    if not last:
                        act.wait_ge(hn_free, b + 1)
                        act.wait_ge(hn_ready, (b + 1) * CC)
                        normalise(act, b + 1)
                    ao(b, 1, 0)
                    ao(b, 1, 1)

                act.wait_ge(bias_loaded, 64)
                normalise(act, 0)
                batch(0, False, True)
                with act.Fori(1, B - 1) as b:
                    batch(b, False)
                batch(B - 1, True)

            @block.vector
            def _(dve):
                def normalise_lo(b):
                    for c in range(CC):
                        dve.wait_ge(hn_act, 2 * b * CC + 2 * c + 2)
                        dve.tensor_tensor(hn_lo[:, c, :], hn[:, c, :], hn_hi[:, c, :].bitcast(F32), ALU.subtract).then_inc(hn_ready, 1)

                def lo(b, u, n, dst, hi, bias_ap):
                    dve.wait_ge(unit_hi, b * SPLIT + n + 1)
                    if bias_ap is None:
                        dve.tensor_tensor(dst, unit_bank(u), hi.bitcast(F32), ALU.subtract).then_inc(unit_done, 1)
                    else:
                        dve.scalar_tensor_tensor(dst, unit_bank(u), bias_ap, hi.bitcast(F32), ALU.add, ALU.subtract).then_inc(unit_done, 1)

                def row_max(b, i):
                    dve.wait_ge(score_full, b * QB + i + 1)
                    dve.tensor_reduce(rowmax[:, i:i + 1], score[i % 2][:, :], AX.X, ALU.max).then_inc(max_done, 1)
                    dve.wait_ge(max_done, b * QB + i + 1)
                    dve.tensor_scalar(negmax[:, i:i + 1], rowmax[:, i:i + 1], -SCALE, None, ALU.mult).then_inc(neg_done, 1)

                def weigh(b, i):
                    dve.wait_ge(exp_done, b * QB + i + 1)
                    dve.reciprocal(rowinv[:, i:i + 1], rowsum[:, i:i + 1]).then_inc(inv_done, 1)
                    dve.wait_ge(inv_done, b * QB + i + 1)
                    dve.tensor_scalar(probs[i % 2][:, :], probs[i % 2][:, :], rowinv[:, i:i + 1], None, ALU.mult).then_inc(probs_ready, 1)

                def pt(b, i):
                    dve.wait_ge(pt_hi_done, b * QB + i + 1)
                    qs = slice(i % GQ * P, (i % GQ + 1) * P)
                    dve.tensor_tensor(pt_lo[:, i // GQ, :, qs], turned[:, :, :], pt_hi[:, i // GQ, :, qs].bitcast(F32), ALU.subtract).then_inc(pt_lo_done, 1)

                def ao(b, g, c):
                    lo(b, av_unit(g, c), 12 + 2 * g + c, ao_lo[:, c, :], ao_hi[:, c, :], bias[:, 2, c:c + 1])
                    if c == CC - 1:
                        dve.sem_inc(av_done, 1)

                def residual(b, g):
                    for o in range(CC):
                        u = av_unit(g, CC + o)
                        dve.wait_ge(prod_full, b * UNITS + u + 1)
                        xt = xs[:, b, o, g * 512:(g + 1) * 512]
                        dve.scalar_tensor_tensor(xt, unit_bank(u), bias[:, 3, o:o + 1], xt, ALU.add, ALU.add).then_inc(unit_done, 1)
                    dve.sem_inc(proj_done, 1)

                def batch(b, last, first=False):
                    for u, (name, o, h) in enumerate(proj_units):
                        hs = slice(h * 512, (h + 1) * 512)
                        lo(b, u, u, dest[name][1][:, o, hs], dest[name][0][:, o, hs], bias[:, bias_of[name], o:o + 1])
                        if first:
                            norm.statistics(dve, u)
                    for n in range(QB // 2):
                        lo(b, U_V + n, U_V + n, v_lo[:, 2 * n:2 * n + 2, :], v_hi[:, 2 * n:2 * n + 2, :], None)
                        if first:
                            norm.statistics(dve, U_V + n)
                    row_max(b, 0)
                    row_max(b, 1)
                    weigh(b, 0)
                    if first:
                        norm.channel_moments(dve)
                    for i in range(QB):
                        if i + 2 < QB:
                            row_max(b, i + 2)
                        if i + 1 < QB:
                            weigh(b, i + 1)
                        pt(b, i)
                        if i == GQ + 1:
                            ao(b, 0, 0)
                    ao(b, 0, 1)
                    residual(b, 0)
                    if first:
                        norm.variance(dve, averages)
                        norm.affine(dve)
                    if not last:
                        normalise_lo(b + 1)
                    ao(b, 1, 0)
                    ao(b, 1, 1)
                    residual(b, 1)

                dve.wait_ge(bias_loaded, 64)
                normalise_lo(0)
                batch(0, False, True)
                with dve.Fori(1, B - 1) as b:
                    batch(b, False)
                batch(B - 1, True)
                dve.wait_ge(unit_done, B * UNITS)
        s.clear()


D = C
H = 8
HD = D // H
FF = 512
FC = FF // P
NT = T // P
PAIRS = NT // 2
MAX_NORM = 1.0 - 1e-5
F32_EPS = 2.0 ** -23
QK_GAIN = 64.0


def token_block(nc, x1, t2, ident, ident_h, weights, norm1_w, norm2_w):
    SCALE = 2.0 / (float(HD) ** 0.5 * QK_GAIN ** 2)
    rounds = [(hg, qh) for qh in range(2) for hg in range(H // 4)]
    steps = [(r, kb) for r, (_, qh) in enumerate(rounds) for kb in range(4 * (qh + 1))]
    diagonal = [kb >= 4 * rounds[r][1] for r, kb in steps]
    NR, NS, ND = len(rounds), len(steps), sum(diagonal)
    O_STEP, X_STEP, ROOT_STEP = steps.index((NR - 2, 4)), steps.index((NR - 1, 2)), NS - 2

    def first_query(m):
        r, kb = steps[m]
        return max(kb * P - rounds[r][1] * 512, 0)

    with ExitStack() as ctx:
        s = Scope(nc, ctx, "block")
        w = {n: [s.sb(f"{n}{i}", [P, k, f], F32R) for i in range(2)]
             for n, k, f in (("qkv", CC, 3 * D), ("gate", CC, FF), ("up", CC, FF), ("down", FC, D), ("o", CC, D))}
        xin = [s.sb(f"xin{i}", [P, CC, 2 * P]) for i in range(2)]
        t1, u, h = s.sb("t1", [P, NT, D]), s.sb("u", [P, NT, D]), s.sb("h", [P, NT, D])
        res = s.sb("res", [P, NT, D])
        hT = [s.sb(f"hT{i}", [P, CC, 2 * P], F32R) for i in range(2)]
        turned_hi, turned_lo = s.sb("turned_hi", [P, CC, T], F32R), s.sb("turned_lo", [P, CC, T], F32R)
        qk = s.sb("qk", [P, NT, 2, D])
        x2, h2 = qk[:, :, 0, :], qk[:, :, 1, :]
        v = s.sb("v", [P, NT, D])
        stack = s.sb("stack", [P, 2, 2, 2, H, 4, HD], F16)
        qkT = s.sb("qkT", [P, 2, H, T], F16)
        probs = s.sb("probs", [P, 2, 4, 512])
        ff_hi, ff_lo = s.sb("ff_hi", [P, FC, 512], F32R), s.sb("ff_lo", [P, FC, 512], F32R)
        n1, n2 = s.sb("n1", [P, D]), s.sb("n2", [P, D])
        mask = s.sb("mask", [P, P])
        ones = s.sb("ones", [P, HD])
        stats, mv = s.sb("stats", [P, NT, 6]), s.sb("mv", [P, NT, 2])
        roots = s.sb("roots", [P, 2, NT])
        mean_sq, late_root = s.sb("mean_sq", [P, NT]), s.sb("late_root", [P, NT])
        rstd, rr = roots[:, 0, :], roots[:, 1, :]
        hsq, alpha, hsq2 = (s.sb(n, [P, NT]) for n in ("hsq", "alpha", "hsq2"))
        ta, tb, tc, td = (s.sb(n, [P, 2 * NT]) for n in ("ta", "tb", "tc", "td"))
        gsq, fac = s.sb("gsq", [P, NT, 2]), s.sb("fac", [P, NT, 2])
        sq2 = s.sb("sq2", [P, 2, 2, 2, H])
        rr2, ball = s.sb("rr2", [P, NT]), s.sb("ball", [P, NT])
        junk, junk_qk = s.sb("junk", [P, D]), s.sb("junk_qk", [P, D])
        squares = [probs[:, i, 2:4, :] for i in range(2)]
        bank = s.ps("bank", [P, 8, 512])
        staged = [a.rearrange("p a b -> p (a b)") for a in (qk[:, 0, :, :], qk[:, 1, :, :], qk[:, 2, :, :],
                                                            res[:, 0:4, :], res[:, 4:8, :], probs[:, 0, 0:2, :], probs[:, 1, 0:1, :])]
        staged = [a.rearrange("p (o i) -> p o i", i=wt.shape[1]) for a, wt in zip(staged, weights)]
        strips = [(n, k) for n, wt in enumerate(weights) for k in range(wt.shape[1] // P)]
        QKV_STRIPS = 3 * CC
        last_strips = range(QKV_STRIPS + 2 * PAIRS, len(strips))

        def strips_with(pr):
            return range(QKV_STRIPS + 2 * pr, QKV_STRIPS + 2 * pr + 2)


        names = tuple(f"w{n}_loaded" for n in range(len(weights))) + (
                 "w_full", "w_hi", "w_lo", "half_inv", "half_attn", "half_hi", "half_lo", "consts", "xin0", "xin1", "norm_loaded", "x_full", "x_copied", "stats_done", "front_scal", "front_act", "late_scal", "late_act", "res_done", "u_done", "h_done",
                 "hsq_done", "h_full", "hT_hi", "hT_lo", "qkv_full", "qk_copied", "v_copied", "gsq_done", "fac_done",
                 "scaled", "squared", "summed", "stack_hi", "stack_dup", "stack_lo", "stack_x", "stack_full", "qT_done", "kT_done",
                 "score_full", "exp_done", "masked", "av_step", "inv_done", "attn_done", "aT_hi", "aT_lo",
                 "o_full", "x2_done", "x2sq_done", "h2_done", "h2_full", "h2T_hi", "h2T_lo", "gate_full", "silu_done", "ffprod_done",
                 "ff_hi_done", "ff_lo_done", "down_full", "o_added", "t2_done", "t2_stored", "log_done", "alpha_done", "passed")
        S = {n: s.sem(n) for n in names}

        FRONT_DVE, FRONT_ACT, LATE_DVE = 19, 6, 4

        def stack_bank(n):
            return (6, 7, 4, 5)[n % 4] if n < 8 else n % 4

        def split_of(n):
            unit, k = strips[n]
            if unit < 3:
                return *(part[:, k, unit * D:(unit + 1) * D] for part in w["qkv"]), D
            return *(part[:, k, :] for part in w[("gate", "up", "down", "o")[unit - 3]]), weights[unit].shape[0]

        def o_bank(pr):
            return 6 + pr if pr < 2 else 2 + pr

        def h2_bank(pr):
            return 2 + pr

        def attn_buf(r):
            return h[:, 2 * (r % 2):2 * (r % 2) + 2, :].rearrange("p a b -> p (a b)")

        with nc.Block() as block:

            @block.gpsimd
            def _(pool):
                pool.memset(ones[:, :], 1.0).then_inc(S["consts"], 1)
                pool.memset(mask[:, :], 1.0).then_inc(S["consts"], 1)
                for slot in range(2):
                    pool.memset(stack[:, slot, :, :, :, 3, :], 0.0).then_inc(S["consts"], 1)
                pool.wait_ge(S["consts"], 4)
                pool.affine_select(out=mask[:, :], in_=mask[:, :], compare_op=ALU.is_ge, fill=0.0, base=0,
                                   pattern=[[1, P]], channel_multiplier=-1).then_inc(S["consts"], 1)
                for slot in range(2):
                    pool.memset(stack[:, slot, 0, :, :, 3, 2:4], 1.0).then_inc(S["consts"], 1)
                    pool.memset(stack[:, slot, 1, :, :, 3, 0:2], 1.0).then_inc(S["consts"], 1)

                def second_high(b):
                    for pr in range(PAIRS):
                        pool.wait_ge(S["stack_hi"], b * 3 * PAIRS + (3 * pr + 1))
                        pool.sem_inc(S["passed"], 1)
                        st = stack[:, pr % 2, 0, :, :, :, :]
                        pool.tensor_copy(st[:, :, :, 2, :], st[:, :, :, 0, :]).then_inc(S["stack_dup"], 1)

                second_high(0)
                with pool.Fori(1, B) as b:
                    second_high(b)

            CONSTS = 9

            @block.sync
            def _(sp):
                def load(b, pr):
                    if not isinstance(b, int) or b or pr > 1:
                        sp.wait_ge(S["x_full"], b * PAIRS + (pr - 1))
                    sp.dma_start(xin[pr % 2][:, :, :], x1[b].rearrange("(c p) (n q) -> n p c q", p=P, q=2 * P)[pr]).then_inc(S[f"xin{pr % 2}"], 16)

                def store(b):
                    for pr in range(PAIRS):
                        sp.wait_ge(S["t2_done"], b * PAIRS + (pr + 1))
                        sp.dma_start(t2.rearrange("(b n t p) d -> b n p t d", p=P, t=2, n=PAIRS)[b, pr],
                                     res[:, 2 * pr:2 * pr + 2, :]).then_inc(S["t2_stored"], 16)

                def load_weight(n):
                    sp.dma_start(staged[n], weights[n].rearrange("(o p) i -> p o i", p=P)).then_inc(S[f"w{n}_loaded"], 16)

                load(0, 0)
                load(0, 1)
                for n in range(3):
                    load_weight(n)
                load(0, 2)
                load(0, 3)
                for dst, src in ((n1, norm1_w), (n2, norm2_w)):
                    sp.dma_start(dst[:, :], src.rearrange("(a d) -> a d", a=1).to_broadcast((P, D))).then_inc(S["norm_loaded"], 16)
                for n in range(3, len(weights)):
                    load_weight(n)
                with sp.Fori(1, B) as b:
                    for pr in range(PAIRS):
                        load(b, pr)
                    store(b - 1)
                store(B - 1)
                sp.wait_ge(S["t2_stored"], 16 * PAIRS * B)

            @block.tensor
            def _(pe):
                def x_turned(b, pr):
                    pe.wait_ge(S[f"xin{pr % 2}"], 16 * (b * (PAIRS // 2) + (pr // 2 + 1)))
                    if not isinstance(b, int) or b > 0:
                        pe.wait_ge(S["attn_done"], (b - 1) * NR + (NR - 1))
                    if pr >= 2:
                        pe.wait_ge(S["x_copied"], b * PAIRS + (pr - 1))
                    for t in range(2):
                        for c in range(CC):
                            last = pe.transpose(bank[:, 4 + pr % 2, (t * CC + c) * P:(t * CC + c + 1) * P],
                                                xin[pr % 2][:, c, t * P:(t + 1) * P], ident[:, :])
                    last.then_inc(S["x_full"], 1)

                def h_turned(b, pr):
                    pe.wait_ge(S["h_done"], b * NT + (2 * pr + 2))
                    if pr == 0:
                        pe.wait_ge(S["attn_done"], b * NR)
                    else:
                        pe.wait_ge(S["v_copied"], b * NT + 2 * pr)
                    for c in range(CC):
                        for t in range(2):
                            last = pe.transpose(bank[:, 7, (c * 2 + t) * P:(c * 2 + t + 1) * P],
                                                h[:, 2 * pr + t, c * P:(c + 1) * P], ident[:, :])
                    last.then_inc(S["h_full"], 1)

                def qkv(b, t):
                    wh, wl = w["qkv"]
                    pe.wait_ge(S["hT_lo"], b * PAIRS + (t // 2 + 1))
                    pe.wait_ge(S["qk_copied"], b * NT + t)
                    toks = slice(t % 2 * P, (t % 2 + 1) * P)
                    for i, cols in ((0, slice(0, 512)), (1, slice(512, 768))):
                        if i == 1:
                            pe.wait_ge(S["v_copied"], b * NT + t)
                        last = split_product(pe, bank[:, 6 + i, 0:cols.stop - cols.start],
                                             [(hT[0][:, k, toks], hT[1][:, k, toks], wh[:, k, cols], wl[:, k, cols])
                                              for k in range(CC)])
                        last.then_inc(S["qkv_full"], 1)

                def stacks(b, pr):
                    for n in range(4 * pr, 4 * pr + 4):
                        t, side = n // 2, n % 2
                        pe.wait_ge(S["stack_x"], b * PAIRS + (pr + 1))
                        pe.wait_ge(S["stack_dup"], b * PAIRS + (pr + 1))
                        if n == 8:
                            pe.wait_ge(S["ffprod_done"], b * 2 * FC)
                        if n < 2:
                            pe.wait_ge(S["qk_copied"], (b + 1) * NT)
                            pe.wait_ge(S["v_copied"], (b + 1) * NT)
                        elif n == 2 and (not isinstance(b, int) or b > 0):
                            pe.wait_ge(S["t2_done"], (b - 1) * PAIRS + 2)
                        elif n >= 4 and n // 4 != 2:
                            pe.wait_ge(S[("qT_done", "kT_done")[side]], b * NT + (t - 1))
                        out = bank[:, stack_bank(n), :].bitcast(F16)
                        for hh in range(H):
                            last = pe.transpose(out[:, hh * P:(hh + 1) * P],
                                                stack[:, pr % 2, side, t % 2, hh, :, :], ident_h[:, :])
                        last.then_inc(S["stack_full"], 1)

                def attention(b, nb):
                    pe.wait_ge(S["qT_done"], b * NT + NT)
                    pe.wait_ge(S["kT_done"], b * NT + NT)

                    def scores(m):
                        r, kb = steps[m]
                        hg, qh = rounds[r]
                        q0 = first_query(m)
                        for p in range(2):
                            n = 2 * m + p
                            if n >= 2:
                                pe.wait_ge(S["exp_done"], b * 2 * NS + n - 1)
                            for i in range(2):
                                hh = 4 * hg + 2 * p + i
                                last = pe.matmul(bank[:, 2 * (n % 2) + i, q0:512], qkT[:, 1, hh, kb * P:(kb + 1) * P],
                                                 qkT[:, 0, hh, qh * 512 + q0:(qh + 1) * 512], start=True, stop=True)
                            last.then_inc(S["score_full"], 1)

                    def weigh(m):
                        r, kb = steps[m]
                        hg, qh = rounds[r]
                        q0 = first_query(m)
                        last_kb = 4 * (qh + 1) - 1
                        pe.wait_ge(S["exp_done"], b * 2 * NS + 2 * m + 2)
                        pe.wait_ge(S["masked"], b * ND + sum(diagonal[:m + 1]))
                        if m == 0:
                            pe.wait_ge(S["t2_done"], b * PAIRS)
                        if kb == 0 and r >= 2:
                            pe.wait_ge(S["attn_done"], b * NR + (r - 1))
                        if kb == 0 and r == NR - 1:
                            pe.wait_ge(S["o_added"], b * PAIRS + 2)
                        num, den = bank[:, 4 + 2 * (r % 2), :], bank[:, 5 + 2 * (r % 2), :]
                        for out, own in ((num, True), (den, False)):
                            for i in range(4):
                                hh = 4 * hg + i
                                lhs = v[:, kb, hh * HD:(hh + 1) * HD] if own else ones[:, :]
                                last = pe.matmul(out[i * HD:(i + 1) * HD, q0:512], lhs, probs[:, m % 2, i, q0:512],
                                                 start=kb == 0, stop=kb == last_kb)
                        last.then_inc(S["av_step"], 1)

                    scores(0)
                    for m in range(NS):
                        if m + 1 < NS:
                            scores(m + 1)
                        if m == X_STEP and nb is not None:
                            x_turned(nb, 0)
                            x_turned(nb, 1)
                        weigh(m)
                        if m == O_STEP:
                            output(b, 0)
                            output(b, 1)
                        if m == X_STEP + 1 and nb is not None:
                            x_turned(nb, 2)
                            x_turned(nb, 3)

                def output(b, pr, nb=None):
                    wh, wl = w["o"]
                    pe.wait_ge(S["aT_lo"], b * NR + (2, 2, NR - 1, NR)[pr])
                    if pr == 2:
                        pe.wait_ge(S["half_lo"], b + 1)
                    if pr < 2:
                        pe.wait_ge(S["attn_done"], b * NR + 2)
                    elif nb is not None:
                        pe.wait_ge(S["x_copied"], (nb + 1) * PAIRS)
                    for t in range(2):
                        toks = slice((2 * pr + t) * P, (2 * pr + t + 1) * P)
                        last = split_product(pe, bank[:, o_bank(pr), t * D:(t + 1) * D],
                                             [(turned_hi[:, k, toks], turned_lo[:, k, toks], wh[:, k, :], wl[:, k, :]) for k in range(CC)])
                    last.then_inc(S["o_full"], 1)

                def h2_turned(b, pr):
                    pe.wait_ge(S["h2_done"], b * NT + (2 * pr + 2))
                    for c in range(CC):
                        for t in range(2):
                            last = pe.transpose(bank[:, h2_bank(pr), (c * 2 + t) * P:(c * 2 + t + 1) * P],
                                                h2[:, 2 * pr + t, c * P:(c + 1) * P], ident[:, :])
                    last.then_inc(S["h2_full"], 1)

                def gate(b, n):
                    toks, cols = slice(n // FC * 512, (n // FC + 1) * 512), slice(n % FC * P, (n % FC + 1) * P)
                    pe.wait_ge(S["h2T_lo"], b * PAIRS + (2 if n < FC else PAIRS))
                    if n >= 2:
                        pe.wait_ge(S["ffprod_done"], b * 2 * FC + (n - 1))
                    for i in range(2):
                        wh, wl = w[("gate", "up")[i]]
                        last = split_product(pe, bank[:, 2 * (n % 2) + i, :],
                                             [(wh[:, k, cols], wl[:, k, cols], turned_hi[:, k, toks], turned_lo[:, k, toks])
                                              for k in range(CC)])
                    last.then_inc(S["gate_full"], 1)

                def down(b, pr, nb=None):
                    wh, wl = w["down"]
                    g = pr // 2
                    pe.wait_ge(S["ff_lo_done"], b * 2 * FC + (g + 1) * FC)
                    if g == 1:
                        pe.wait_ge(S["t2_done"], b * PAIRS + (pr - 1))
                        if nb is not None:
                            pe.wait_ge(S[("qT_done", "kT_done")[pr % 2]], nb * NT + 4)
                    else:
                        pe.wait_ge(S["h2T_lo"], (b + 1) * PAIRS)
                    for t in range(2):
                        own = slice((2 * pr + t) % 4 * P, ((2 * pr + t) % 4 + 1) * P)
                        last = split_product(pe, bank[:, 4 + pr % 2, t * D:(t + 1) * D],
                                             [(ff_hi[:, f, own], ff_lo[:, f, own], wh[:, f, :], wl[:, f, :]) for f in range(FC)])
                    last.then_inc(S["down_full"], 1)

                def weight_strip(n):
                    unit, k = strips[n]
                    pe.wait_ge(S[f"w{unit}_loaded"], 16)
                    if n >= 4:
                        pe.wait_ge(S["w_lo"], n - 3)
                    for o in range(weights[unit].shape[0] // P):
                        last = pe.transpose(bank[:, n % 4, o * P:(o + 1) * P], staged[unit][:, o, k * P:(k + 1) * P], ident[:, :])
                    last.then_inc(S["w_full"], 1)

                def first_front():
                    for pr in range(PAIRS):
                        x_turned(0, pr)
                    for n in range(QKV_STRIPS):
                        weight_strip(n)
                    for pr in range(PAIRS):
                        h_turned(0, pr)
                        if pr == 0:
                            pe.wait_ge(S["w_lo"], QKV_STRIPS)
                        qkv(0, 2 * pr)
                        qkv(0, 2 * pr + 1)
                        for n in strips_with(pr):
                            weight_strip(n)
                    for n in last_strips:
                        weight_strip(n)
                    for pr in range(PAIRS):
                        if pr == 2:
                            pe.wait_ge(S["w_lo"], len(strips))
                        stacks(0, pr)

                def late(b, nb):
                    h2_turned(b, 0)
                    h2_turned(b, 1)
                    gate(b, 0)
                    output(b, 2, nb)
                    output(b, 3, nb)
                    gate(b, 1)
                    h_turned(nb, 0)
                    gate(b, 2)
                    qkv(nb, 0)
                    qkv(nb, 1)
                    h_turned(nb, 1)
                    h2_turned(b, 2)
                    h2_turned(b, 3)
                    qkv(nb, 2)
                    qkv(nb, 3)
                    h_turned(nb, 2)
                    gate(b, 3)
                    qkv(nb, 4)
                    qkv(nb, 5)
                    h_turned(nb, 3)
                    down(b, 0)
                    qkv(nb, 6)
                    qkv(nb, 7)
                    down(b, 1)
                    gate(b, 4)
                    gate(b, 5)
                    gate(b, 6)
                    stacks(nb, 0)
                    gate(b, 7)
                    stacks(nb, 1)
                    down(b, 2, nb)
                    stacks(nb, 2)
                    down(b, 3, nb)
                    stacks(nb, 3)

                def last_late(b):
                    h2_turned(b, 0)
                    h2_turned(b, 1)
                    gate(b, 0)
                    output(b, 2)
                    output(b, 3)
                    gate(b, 1)
                    gate(b, 2)
                    h2_turned(b, 2)
                    h2_turned(b, 3)
                    gate(b, 3)
                    gate(b, 4)
                    down(b, 0)
                    down(b, 1)
                    for n in range(5, 8):
                        gate(b, n)
                    down(b, 2)
                    down(b, 3)

                pe.wait_ge(S["consts"], CONSTS)
                first_front()
                attention(0, 1)
                late(0, 1)
                with pe.Fori(1, B - 1) as b:
                    attention(b, b + 1)
                    late(b, b + 1)
                attention(B - 1, None)
                last_late(B - 1)

            @block.scalar
            def _(act):
                def x_copy(b, pr):
                    act.wait_ge(S["x_full"], b * PAIRS + (pr + 1))
                    act.wait_ge(S["res_done"], b * PAIRS)
                    act.activation(t1[:, 2 * pr:2 * pr + 2, :], bank[:, 4 + pr % 2, :], ACT.Copy).then_inc(S["x_copied"], 1)

                def norm_roots(b):
                    act.wait_ge(S["front_scal"], b * FRONT_DVE + 4)
                    act.activation(tb[:, :], ta[:, :], ACT.Sqrt).then_inc(S["front_act"], 1)

                def lengths(b, ts):
                    for t in ts:
                        act.wait_ge(S["h_done"], b * NT + (t + 1))
                        act.wait_ge(S["hsq_done"], b * NT + t)
                        act.activation(junk[:, :], h[:, t, :], ACT.Square, accum_out=hsq[:, t:t + 1]).then_inc(S["hsq_done"], 1)

                def length_roots(b):
                    act.wait_ge(S["hsq_done"], (b + 1) * NT)
                    act.activation(ta[:, 0:NT], hsq[:, :], ACT.Sqrt, scale=0.25).then_inc(S["front_act"], 1)

                def h_high(b, pr):
                    act.wait_ge(S["h_full"], b * PAIRS + (pr + 1))
                    act.wait_ge(S["qkv_full"], b * 2 * NT + 4 * pr)
                    act.activation(hT[0][:, :, :], bank[:, 7, :].rearrange("p (c q) -> p c q", c=CC), ACT.Copy).then_inc(S["hT_hi"], 1)

                def logs(b):
                    act.wait_ge(S["front_scal"], b * FRONT_DVE + 11)
                    act.activation(ta[:, 0:NT], tc[:, 0:NT], ACT.Ln).then_inc(S["front_act"], 1)
                    act.activation(tb[:, 0:NT], td[:, 0:NT], ACT.Ln).then_inc(S["front_act"], 1)

                def qk_copy(b, t):
                    act.wait_ge(S["qkv_full"], b * 2 * NT + (2 * t + 1))
                    act.activation(qk[:, t, :, :], bank[:, 6, :], ACT.Copy).then_inc(S["qk_copied"], 1)
                    act.wait_ge(S["qk_copied"], b * NT + (t + 1))
                    for side in range(2):
                        act.wait_ge(S["gsq_done"], b * 2 * NT + (2 * t + side))
                        act.activation(junk_qk[:, :], qk[:, t, side, :], ACT.Square,
                                       accum_out=gsq[:, t, side:side + 1]).then_inc(S["gsq_done"], 1)

                def qk_roots(b):
                    act.wait_ge(S["gsq_done"], (b + 1) * 2 * NT)
                    act.wait_ge(S["alpha_done"], b + 1)
                    act.activation(ta[:, :], gsq[:, :, :], ACT.Sqrt).then_inc(S["front_act"], 1)

                def tanhs(b):
                    act.wait_ge(S["front_scal"], b * FRONT_DVE + 16)
                    act.activation(tc[:, :], tb[:, :], ACT.Tanh).then_inc(S["front_act"], 1)

                def stack_high(b, pr):
                    act.wait_ge(S["scaled"], b * PAIRS + (pr + 1))
                    act.wait_ge(S["stack_full"], b * 2 * NT + max(pr - 1, 0) * 4)
                    act.wait_ge(S["summed"], b * PAIRS + max(pr - 1, 0))
                    act.activation(squares[pr % 2].rearrange("p a b -> p (a b)"), qk[:, 2 * pr:2 * pr + 2, :, :].rearrange("p a b c -> p (a b c)"),
                                   ACT.Square).then_inc(S["squared"], 1)
                    act.activation(stack[:, pr % 2, 0, :, :, 0, :],
                                   qk[:, 2 * pr:2 * pr + 2, 0, :].rearrange("p t (h d) -> p t h d", h=H), ACT.Copy).then_inc(S["stack_hi"], 1)
                    for t in range(2):
                        act.activation(stack[:, pr % 2, 1, t, :, 0:2, :],
                                       qk[:, 2 * pr + t, 1, :].rearrange("p (h g d) -> p h g d", h=H, g=1).to_broadcast((P, H, 2, HD)),
                                       ACT.Copy).then_inc(S["stack_hi"], 1)

                def attention(b, nb):
                    for m in range(NS):
                        q0 = first_query(m)
                        act.wait_ge(S["av_step"], b * NS + max(m - 1, 0))
                        for p in range(2):
                            n = 2 * m + p
                            act.wait_ge(S["score_full"], b * 2 * NS + n + 1)
                            src = bank[:, 2 * (n % 2):2 * (n % 2) + 2, q0:512]
                            act.activation(probs[:, m % 2, 2 * p:2 * p + 2, q0:512], src, ACT.Exp, scale=SCALE).then_inc(S["exp_done"], 1)
                        if steps[m][1] == 2 and steps[m][0] > 0:
                            aT(b, steps[m][0] - 1)
                        if nb is not None and m in (X_STEP + 1, X_STEP + 2):
                            for pr in (2 * (m - X_STEP) - 2, 2 * (m - X_STEP) - 1):
                                x_copy(nb, pr)
                        if m in (O_STEP + 3, O_STEP + 4):
                            late_squares(b, m - O_STEP - 3)
                        if m == ROOT_STEP:
                            late_roots(b, 0)
                            if nb is not None:
                                norm_roots(nb)

                def late_squares(b, pr):
                    for t in (2 * pr, 2 * pr + 1):
                        act.wait_ge(S["x2_done"], b * PAIRS + (pr + 1))
                        act.wait_ge(S["x2sq_done"], b * NT + t)
                        act.activation(junk[:, :], x2[:, t, :], ACT.Square, accum_out=hsq2[:, t:t + 1]).then_inc(S["x2sq_done"], 1)

                def late_roots(b, half):
                    act.wait_ge(S["late_scal"], b * LATE_DVE + (2 * half + 1))
                    ts = slice(half * NT // 2, (half + 1) * NT // 2)
                    act.activation(late_root[:, ts], mean_sq[:, ts], ACT.Sqrt).then_inc(S["late_act"], 1)

                def h2_high(b, pr):
                    act.wait_ge(S["h2_full"], b * PAIRS + (pr + 1))
                    act.activation(turned_hi[:, :, pr * 256:(pr + 1) * 256],
                                   bank[:, h2_bank(pr), :].rearrange("p (c q) -> p c q", c=CC), ACT.Copy).then_inc(S["h2T_hi"], 1)

                def silu(b, n):
                    act.wait_ge(S["gate_full"], b * 2 * FC + (n + 1))
                    if n >= 2:
                        act.wait_ge(S["ffprod_done"], b * 2 * FC + (n - 1))
                    act.activation(probs[:, 0, n % 2, :], bank[:, 2 * (n % 2), :], ACT.Silu).then_inc(S["silu_done"], 1)

                def ff_high(b, n):
                    act.wait_ge(S["ffprod_done"], b * 2 * FC + (n + 1))
                    act.wait_ge(S["down_full"], b * PAIRS + n // FC * 2)
                    act.activation(ff_hi[:, n % FC, :], probs[:, 1, n % 2, :], ACT.Copy).then_inc(S["ff_hi_done"], 1)

                def q_turned(b, pr):
                    for t in (2 * pr, 2 * pr + 1):
                        act.wait_ge(S["stack_full"], b * 2 * NT + 2 * t + 1)
                        act.activation(qkT[:, 0, :, t * P:(t + 1) * P],
                                       bank[:, stack_bank(2 * t), :].bitcast(F16).rearrange("p (h q) -> p h q", h=H), ACT.Copy).then_inc(S["qT_done"], 1)

                def last_aT(b):
                    hg, qh = rounds[NR - 1]
                    for half, (attn_sem, hi_sem) in enumerate((("half_attn", "half_hi"), ("attn_done", "aT_hi"))):
                        act.wait_ge(S[attn_sem], b + 1 if half == 0 else b * NR + NR)
                        ts = slice(qh * 512 + half * 256, qh * 512 + (half + 1) * 256)
                        act.activation(turned_hi[:, hg, ts], attn_buf(NR - 1)[:, half * 256:(half + 1) * 256], ACT.Copy).then_inc(S[hi_sem], 1)

                def aT(b, r):
                    hg, qh = rounds[r]
                    act.wait_ge(S["attn_done"], b * NR + r + 1)
                    act.activation(turned_hi[:, hg, qh * 512:(qh + 1) * 512], attn_buf(r), ACT.Copy).then_inc(S["aT_hi"], 1)

                def weight_high(n):
                    hi, _, rows = split_of(n)
                    act.wait_ge(S["w_full"], n + 1)
                    act.activation(hi, bank[:, n % 4, 0:rows], ACT.Copy).then_inc(S["w_hi"], 1)

                def first_front():
                    for pr in range(PAIRS):
                        x_copy(0, pr)
                    for n in range(QKV_STRIPS // 2):
                        weight_high(n)
                    norm_roots(0)
                    for n in range(QKV_STRIPS // 2, QKV_STRIPS):
                        weight_high(n)
                    h_high(0, 0)
                    lengths(0, range(NT))
                    length_roots(0)
                    logs(0)
                    for pr in range(PAIRS):
                        qk_copy(0, 2 * pr)
                        qk_copy(0, 2 * pr + 1)
                        if pr < PAIRS - 1:
                            h_high(0, pr + 1)
                        for n in strips_with(pr):
                            weight_high(n)
                    qk_roots(0)
                    for n in last_strips:
                        weight_high(n)
                    tanhs(0)
                    for pr in range(PAIRS):
                        stack_high(0, pr)
                        if pr > 0:
                            q_turned(0, pr - 1)
                    q_turned(0, PAIRS - 1)

                def late(b, nb):
                    h2_high(b, 0)
                    h2_high(b, 1)
                    last_aT(b)
                    silu(b, 0)
                    late_squares(b, 2)
                    late_squares(b, 3)
                    late_roots(b, 1)
                    h_high(nb, 0)
                    silu(b, 1)
                    ff_high(b, 0)
                    qk_copy(nb, 0)
                    qk_copy(nb, 1)
                    h_high(nb, 1)
                    h2_high(b, 2)
                    h2_high(b, 3)
                    ff_high(b, 1)
                    silu(b, 2)
                    lengths(nb, range(0, 4))
                    qk_copy(nb, 2)
                    qk_copy(nb, 3)
                    ff_high(b, 2)
                    h_high(nb, 2)
                    lengths(nb, range(4, NT))
                    silu(b, 3)
                    length_roots(nb)
                    qk_copy(nb, 4)
                    qk_copy(nb, 5)
                    ff_high(b, 3)
                    h_high(nb, 3)
                    logs(nb)
                    qk_copy(nb, 6)
                    qk_copy(nb, 7)
                    qk_roots(nb)
                    tanhs(nb)
                    silu(b, 4)
                    stack_high(nb, 0)
                    ff_high(b, 4)
                    silu(b, 5)
                    ff_high(b, 5)
                    silu(b, 6)
                    stack_high(nb, 1)
                    ff_high(b, 6)
                    q_turned(nb, 0)
                    silu(b, 7)
                    ff_high(b, 7)
                    stack_high(nb, 2)
                    q_turned(nb, 1)
                    stack_high(nb, 3)
                    q_turned(nb, 2)
                    q_turned(nb, 3)

                def last_late(b):
                    h2_high(b, 0)
                    h2_high(b, 1)
                    last_aT(b)
                    silu(b, 0)
                    late_squares(b, 2)
                    late_squares(b, 3)
                    late_roots(b, 1)
                    for n in range(2 * FC):
                        if n < 2 * FC - 1:
                            silu(b, n + 1)
                        ff_high(b, n)
                        if n == 1:
                            h2_high(b, 2)
                            h2_high(b, 3)

                act.wait_ge(S["consts"], CONSTS)
                first_front()
                attention(0, 1)
                late(0, 1)
                with act.Fori(1, B - 1) as b:
                    attention(b, b + 1)
                    late(b, b + 1)
                attention(B - 1, None)
                last_late(B - 1)

            @block.vector
            def _(dve):
                FS, LS = S["front_scal"], S["late_scal"]
                count = [0]

                def chain(b):
                    count[0] += 1
                    dve.wait_ge(FS, b * FRONT_DVE + count[0])

                def statistics(b):
                    count[0] = 0
                    for pr in range(PAIRS):
                        dve.wait_ge(S["x_copied"], b * PAIRS + (pr + 1))
                        for t in (2 * pr, 2 * pr + 1):
                            dve.bn_stats(stats[:, t, :], t1[:, t, :]).then_inc(S["stats_done"], 1)
                    dve.wait_ge(S["stats_done"], b * 2 * NT + NT)
                    dve.sem_inc(S["passed"], 1)
                    for t in range(NT):
                        dve.bn_aggr(mv[:, t, :], stats[:, t, :]).then_inc(S["stats_done"], 1)
                    dve.wait_ge(S["stats_done"], (b + 1) * 2 * NT)
                    var = mv[:, :, 1]
                    dve.tensor_scalar(ta[:, 0:NT], var, LN_EPS, None, ALU.add).then_inc(FS, 1)
                    chain(b)
                    dve.reciprocal(tc[:, 0:NT], ta[:, 0:NT]).then_inc(FS, 1)
                    chain(b)
                    dve.tensor_tensor(td[:, 0:NT], tc[:, 0:NT], var, ALU.mult).then_inc(FS, 1)
                    chain(b)
                    dve.tensor_scalar(ta[:, NT:2 * NT], td[:, 0:NT], F32_EPS, None, ALU.add).then_inc(FS, 1)
                    chain(b)

                def norm_factors(b):
                    dve.wait_ge(S["front_act"], b * FRONT_ACT + 1)
                    dve.reciprocal(roots[:, :, :], tb[:, :].rearrange("p (a t) -> p a t", a=2)).then_inc(FS, 1)
                    chain(b)

                def normalised(b, ts):
                    for t in ts:
                        dve.tensor_scalar(u[:, t, :], t1[:, t, :], mv[:, t, 0:1], rstd[:, t:t + 1], ALU.subtract, ALU.mult).then_inc(S["u_done"], 1)
                    for t in ts:
                        h_tile(b, t)

                def h_tile(b, t):
                    dve.wait_ge(S["u_done"], b * NT + (t + 1))
                    dve.scalar_tensor_tensor(h[:, t, :], u[:, t, :], rr[:, t:t + 1], n1[:, :], ALU.mult, ALU.mult).then_inc(S["h_done"], 1)

                def h_low(b, pr):
                    dve.wait_ge(S["hT_hi"], b * PAIRS + (pr + 1))
                    dve.tensor_tensor(hT[1][:, :, :], bank[:, 7, :].rearrange("p (c q) -> p c q", c=CC),
                                      hT[0][:, :, :].bitcast(F32), ALU.subtract).then_inc(S["hT_lo"], 1)

                def v_copy(b, t):
                    dve.wait_ge(S["qkv_full"], b * 2 * NT + (2 * t + 2))
                    dve.tensor_copy(v[:, t, :], bank[:, 7, 0:D]).then_inc(S["v_copied"], 1)

                def onto_ball(b):
                    dve.wait_ge(S["front_act"], b * FRONT_ACT + 2)
                    dve.tensor_scalar(tb[:, 0:NT], ta[:, 0:NT], MAX_NORM, None, ALU.max).then_inc(FS, 1)
                    chain(b)
                    dve.reciprocal(tc[:, 0:NT], tb[:, 0:NT]).then_inc(FS, 1)
                    chain(b)
                    dve.scalar_tensor_tensor(tb[:, 0:NT], tc[:, 0:NT], MAX_NORM, ta[:, 0:NT], ALU.mult, ALU.mult).then_inc(FS, 1)
                    dve.tensor_scalar(alpha[:, :], tc[:, 0:NT], 0.5 * MAX_NORM, None, ALU.mult).then_inc(FS, 1)
                    chain(b)
                    chain(b)
                    dve.tensor_scalar(ball[:, :], tb[:, 0:NT], 1e-6, MAX_NORM, ALU.max, ALU.min).then_inc(FS, 1)
                    chain(b)
                    dve.tensor_scalar(tc[:, 0:NT], ball[:, :], 1.0, None, ALU.add).then_inc(S["log_done"], 1)
                    dve.wait_ge(S["log_done"], b + 1)
                    dve.tensor_scalar(td[:, 0:NT], ball[:, :], -1.0, 1.0, ALU.mult, ALU.add).then_inc(FS, 1)
                    chain(b)

                def log_factor(b):
                    dve.wait_ge(S["front_act"], b * FRONT_ACT + 4)
                    dve.tensor_tensor(tc[:, 0:NT], ta[:, 0:NT], tb[:, 0:NT], ALU.subtract).then_inc(FS, 1)
                    chain(b)
                    dve.reciprocal(td[:, 0:NT], ball[:, :]).then_inc(FS, 1)
                    chain(b)
                    dve.scalar_tensor_tensor(td[:, 0:NT], tc[:, 0:NT], 0.5, td[:, 0:NT], ALU.mult, ALU.mult).then_inc(FS, 1)
                    chain(b)
                    dve.tensor_tensor(alpha[:, :], alpha[:, :], td[:, 0:NT], ALU.mult).then_inc(S["alpha_done"], 1)
                    dve.wait_ge(S["alpha_done"], b + 1)

                alphas = alpha[:, :].rearrange("p (t a) -> p t a", a=1).to_broadcast((P, NT, 2))

                def tangent_length(b):
                    dve.wait_ge(S["front_act"], b * FRONT_ACT + 5)
                    dve.tensor_tensor(td[:, :].rearrange("p (t a) -> p t a", a=2), ta[:, :].rearrange("p (t a) -> p t a", a=2), alphas, ALU.mult).then_inc(FS, 1)
                    chain(b)
                    dve.tensor_scalar(tb[:, :], td[:, :], 1e-6, None, ALU.max).then_inc(FS, 1)
                    chain(b)

                def factors(b):
                    dve.wait_ge(S["front_act"], b * FRONT_ACT + 6)
                    dve.reciprocal(ta[:, :], tb[:, :]).then_inc(FS, 1)
                    chain(b)
                    dve.tensor_tensor(tb[:, :], ta[:, :], tc[:, :], ALU.mult).then_inc(FS, 1)
                    chain(b)
                    dve.tensor_tensor(tc[:, :], tb[:, :], td[:, :], ALU.mult).then_inc(FS, 1)
                    chain(b)
                    assert count[0] == FRONT_DVE
                    dve.tensor_scalar(td[:, :], tc[:, :], MAX_NORM, 1.0 / (MAX_NORM * QK_GAIN), ALU.max, ALU.mult).then_inc(S["fac_done"], 1)
                    dve.wait_ge(S["fac_done"], b * 4 + 1)
                    dve.reciprocal(tc[:, :], td[:, :]).then_inc(S["fac_done"], 1)
                    dve.wait_ge(S["fac_done"], b * 4 + 2)
                    dve.tensor_tensor(td[:, :], tc[:, :], tb[:, :], ALU.mult).then_inc(S["fac_done"], 1)
                    dve.wait_ge(S["fac_done"], b * 4 + 3)
                    dve.tensor_tensor(fac[:, :, :], td[:, :].rearrange("p (t a) -> p t a", a=2), alphas, ALU.mult).then_inc(S["fac_done"], 1)
                    dve.wait_ge(S["fac_done"], b * 4 + 4)
                    dve.wait_ge(S["gsq_done"], (b + 1) * 2 * NT)

                def scale_qk(b, pr):
                    ts = slice(2 * pr, 2 * pr + 2)
                    dve.tensor_tensor(qk[:, ts, :, :].rearrange("p t s d -> p (t s) d"), qk[:, ts, :, :].rearrange("p t s d -> p (t s) d"),
                                      fac[:, ts, :].rearrange("p t s -> p (t s)").rearrange("p (n a) -> p n a", a=1).to_broadcast((P, 4, D)), ALU.mult).then_inc(S["scaled"], 1)

                def stack_low(b, pr):
                    ts = slice(2 * pr, 2 * pr + 2)
                    dve.wait_ge(S["squared"], b * PAIRS + (pr + 1))
                    dve.tensor_reduce(sq2[:, pr % 2, :, :, :].rearrange("p t s h -> p (t s h)"),
                                      squares[pr % 2].rearrange("p a (n d) -> p (a n) d", d=HD), AX.X, ALU.add).then_inc(S["summed"], 1)
                    for side in range(2):
                        dve.wait_ge(S["stack_hi"], b * 3 * PAIRS + (3 * pr + 1 + 2 * side))
                        st = stack[:, pr % 2, side, :, :, :, :]
                        src = qk[:, ts, side, :].rearrange("p t (h d) -> p t h d", h=H)
                        dve.tensor_tensor(st[:, :, :, 1 + side, :], src, st[:, :, :, 0, :], ALU.subtract).then_inc(S["stack_lo"], 1)
                    dve.wait_ge(S["summed"], b * PAIRS + (pr + 1))
                    for side in range(2):
                        row = 2 * side
                        x = stack[:, pr % 2, side, :, :, 3, row:row + 2]
                        sq = sq2[:, pr % 2, :, side, :]
                        dve.tensor_scalar(x[:, :, :, 0], sq, -0.5, None, ALU.mult).then_inc(S["inv_done"], 1)
                    dve.wait_ge(S["inv_done"], b * INV + (2 * pr + 2))
                    dve.wait_ge(S["stack_lo"], b * 2 * PAIRS + 2 * (pr + 1))
                    for side in range(2):
                        row = 2 * side
                        x = stack[:, pr % 2, side, :, :, 3, row:row + 2]
                        sq = sq2[:, pr % 2, :, side, :]
                        last = dve.scalar_tensor_tensor(x[:, :, :, 1], sq, -0.5, x[:, :, :, 0], ALU.mult, ALU.subtract)
                        if side == 1:
                            last.then_inc(S["stack_x"], 1)

                def attention(b, nb):
                    for m in range(NS):
                        r, kb = steps[m]
                        q0 = first_query(m)
                        if diagonal[m]:
                            dve.wait_ge(S["exp_done"], b * 2 * NS + 2 * m + 2)
                            pm = probs[:, m % 2, :, q0:q0 + P]
                            dve.tensor_tensor(pm, pm, mask[:, :].rearrange("p (a q) -> p a q", a=1).to_broadcast((P, 4, P)), ALU.mult).then_inc(S["masked"], 1)
                        if kb == 1 and r > 0:
                            normalise(b, r - 1)
                        if kb == 3 and r > 0:
                            low_part(b, r - 1)
                        if (r, kb) == (2, 0):
                            input_sum(b)
                        if m in (O_STEP + 1, O_STEP + 2):
                            output_sum(b, m - O_STEP - 1)
                        if m == X_STEP - 1:
                            mean_square(b, 0)
                        if nb is not None and m == X_STEP + 3:
                            statistics(nb)
                        if m == ROOT_STEP + 1:
                            if nb is not None:
                                norm_factors(nb)
                            second_norm(b, 0)

                def last_round(b):
                    hg, qh = rounds[NR - 1]
                    r = NR - 1
                    dve.wait_ge(S["av_step"], b * NS + NS)
                    for half, (inv_sem, attn_sem) in enumerate((("half_inv", "half_attn"), ("inv_done", "attn_done"))):
                        cols = slice(half * 256, (half + 1) * 256)
                        inv = h[:, 4 + 2 * (r % 2) + half, :]
                        num, den = bank[:, 4 + 2 * (r % 2), cols], bank[:, 5 + 2 * (r % 2), cols]
                        dve.reciprocal(inv, den).then_inc(S[inv_sem], 1)
                        dve.wait_ge(S[inv_sem], b + 1 if half == 0 else b * INV + (2 * PAIRS + r + 1))
                        dve.tensor_tensor(attn_buf(r)[:, cols], num, inv, ALU.mult).then_inc(S[attn_sem], 1)
                    for half, (hi_sem, lo_sem) in enumerate((("half_hi", "half_lo"), ("aT_hi", "aT_lo"))):
                        dve.wait_ge(S[hi_sem], b + 1 if half == 0 else b * NR + (r + 1))
                        ts = slice(qh * 512 + half * 256, qh * 512 + (half + 1) * 256)
                        dve.tensor_tensor(turned_lo[:, hg, ts], attn_buf(r)[:, half * 256:(half + 1) * 256],
                                          turned_hi[:, hg, ts].bitcast(F32), ALU.subtract).then_inc(S[lo_sem], 1)

                def input_sum(b):
                    dve.wait_ge(S["t2_stored"], b * (16 * PAIRS))
                    for pr in range(PAIRS):
                        ts = slice(2 * pr, 2 * pr + 2)
                        dve.tensor_tensor(res[:, ts, :], t1[:, ts, :], u[:, ts, :], ALU.add).then_inc(S["res_done"], 1)

                def output_sum(b, pr):
                    dve.wait_ge(S["o_full"], b * PAIRS + (pr + 1))
                    dve.wait_ge(S["res_done"], (b + 1) * PAIRS)
                    ts = slice(2 * pr, 2 * pr + 2)
                    out = bank[:, o_bank(pr), :].rearrange("p (t d) -> p t d", t=2)
                    dve.tensor_tensor(x2[:, ts, :], out, u[:, ts, :], ALU.add).then_inc(S["x2_done"], 1)
                    dve.tensor_tensor(res[:, ts, :], res[:, ts, :], out, ALU.add).then_inc(S["o_added"], 1)

                def mean_square(b, half):
                    dve.wait_ge(S["x2sq_done"], b * NT + (half + 1) * NT // 2)
                    ts = slice(half * NT // 2, (half + 1) * NT // 2)
                    dve.tensor_scalar(mean_sq[:, ts], hsq2[:, ts], 1.0 / D, F32_EPS, ALU.mult, ALU.add).then_inc(LS, 1)

                def second_norm(b, half):
                    dve.wait_ge(S["late_act"], b * 2 + (half + 1))
                    ts = slice(half * NT // 2, (half + 1) * NT // 2)
                    dve.reciprocal(rr2[:, ts], late_root[:, ts]).then_inc(LS, 1)
                    dve.wait_ge(LS, b * LATE_DVE + (2 * half + 2))
                    for t in range(half * NT // 2, (half + 1) * NT // 2):
                        dve.scalar_tensor_tensor(h2[:, t, :], x2[:, t, :], rr2[:, t:t + 1], n2[:, :], ALU.mult, ALU.mult).then_inc(S["h2_done"], 1)

                def h2_low(b, pr):
                    dve.wait_ge(S["h2T_hi"], b * PAIRS + (pr + 1))
                    ts = slice(pr * 256, (pr + 1) * 256)
                    dve.tensor_tensor(turned_lo[:, :, ts], bank[:, h2_bank(pr), :].rearrange("p (c q) -> p c q", c=CC),
                                      turned_hi[:, :, ts].bitcast(F32), ALU.subtract).then_inc(S["h2T_lo"], 1)

                def ff_product(b, n):
                    dve.wait_ge(S["silu_done"], b * 2 * FC + (n + 1))
                    if n >= 2:
                        dve.wait_ge(S["ff_lo_done"], b * 2 * FC + (n - 1))
                    dve.tensor_tensor(probs[:, 1, n % 2, :], probs[:, 0, n % 2, :], bank[:, 2 * (n % 2) + 1, :], ALU.mult).then_inc(S["ffprod_done"], 1)

                def ff_low(b, n):
                    dve.wait_ge(S["ff_hi_done"], b * 2 * FC + (n + 1))
                    dve.tensor_tensor(ff_lo[:, n % FC, :], probs[:, 1, n % 2, :], ff_hi[:, n % FC, :].bitcast(F32), ALU.subtract).then_inc(S["ff_lo_done"], 1)

                def add(b, pr):
                    dve.wait_ge(S["down_full"], b * PAIRS + (pr + 1))
                    dve.wait_ge(S["o_added"], b * PAIRS + (pr + 1))
                    ts = slice(2 * pr, 2 * pr + 2)
                    dve.tensor_tensor(res[:, ts, :], res[:, ts, :], bank[:, 4 + pr % 2, :].rearrange("p (t d) -> p t d", t=2), ALU.add).then_inc(S["t2_done"], 1)

                INV = 2 * PAIRS + NR

                def k_turned(b, n):
                    if n < 0:
                        return
                    dve.wait_ge(S["stack_full"], b * 2 * NT + n + 1)
                    dve.tensor_copy(qkT[:, 1, :, n // 2 * P:(n // 2 + 1) * P],
                                    bank[:, stack_bank(n), :].bitcast(F16).rearrange("p (h q) -> p h q", h=H)).then_inc(S["kT_done"], 1)

                def normalise(b, r):
                    hg, qh = rounds[r]
                    m = max(i for i in range(NS) if steps[i][0] == r)
                    dve.wait_ge(S["av_step"], b * NS + m + 1)
                    inv = h[:, 4 + 2 * (r % 2):6 + 2 * (r % 2), :].rearrange("p a b -> p (a b)")
                    num, den = bank[:, 4 + 2 * (r % 2), :], bank[:, 5 + 2 * (r % 2), :]
                    dve.reciprocal(inv, den).then_inc(S["inv_done"], 1)
                    dve.wait_ge(S["inv_done"], b * INV + 2 * PAIRS + r + 1)
                    dve.tensor_tensor(attn_buf(r), num, inv, ALU.mult).then_inc(S["attn_done"], 1)

                def low_part(b, r):
                    hg, qh = rounds[r]
                    dve.wait_ge(S["aT_hi"], b * NR + r + 1)
                    ts = slice(qh * 512, (qh + 1) * 512)
                    dve.tensor_tensor(turned_lo[:, hg, ts], attn_buf(r), turned_hi[:, hg, ts].bitcast(F32), ALU.subtract).then_inc(S["aT_lo"], 1)

                def weight_low(n):
                    hi, lo, rows = split_of(n)
                    dve.wait_ge(S["w_hi"], n + 1)
                    dve.tensor_tensor(lo, bank[:, n % 4, 0:rows], hi.bitcast(F32), ALU.subtract).then_inc(S["w_lo"], 1)

                def first_front():
                    statistics(0)
                    for n in range(QKV_STRIPS // 2):
                        weight_low(n)
                    norm_factors(0)
                    normalised(0, range(0, 4))
                    for n in range(QKV_STRIPS // 2, QKV_STRIPS):
                        weight_low(n)
                    normalised(0, range(4, NT))
                    h_low(0, 0)
                    onto_ball(0)
                    for pr in range(PAIRS):
                        v_copy(0, 2 * pr)
                        v_copy(0, 2 * pr + 1)
                        if pr < PAIRS - 1:
                            h_low(0, pr + 1)
                        for n in strips_with(pr):
                            weight_low(n)
                    log_factor(0)
                    tangent_length(0)
                    for n in last_strips:
                        weight_low(n)
                    factors(0)
                    scale_qk(0, 0)
                    for pr in range(PAIRS):
                        if pr < PAIRS - 1:
                            scale_qk(0, pr + 1)
                        stack_low(0, pr)
                        k_turned(0, 4 * pr + 1 - 4)
                        k_turned(0, 4 * pr + 3 - 4)
                    k_turned(0, 13)
                    k_turned(0, 15)

                def late(b, nb):
                    h2_low(b, 0)
                    h2_low(b, 1)
                    last_round(b)
                    normalised(nb, range(0, 4))
                    output_sum(b, 2)
                    output_sum(b, 3)
                    mean_square(b, 1)
                    ff_product(b, 0)
                    second_norm(b, 1)
                    h_low(nb, 0)
                    ff_low(b, 0)
                    ff_product(b, 1)
                    v_copy(nb, 0)
                    v_copy(nb, 1)
                    h_low(nb, 1)
                    h2_low(b, 2)
                    h2_low(b, 3)
                    normalised(nb, range(4, NT))
                    ff_low(b, 1)
                    ff_product(b, 2)
                    v_copy(nb, 2)
                    v_copy(nb, 3)
                    h_low(nb, 2)
                    ff_low(b, 2)
                    ff_product(b, 3)
                    v_copy(nb, 4)
                    v_copy(nb, 5)
                    onto_ball(nb)
                    ff_low(b, 3)
                    h_low(nb, 3)
                    add(b, 0)
                    v_copy(nb, 6)
                    v_copy(nb, 7)
                    log_factor(nb)
                    add(b, 1)
                    tangent_length(nb)
                    factors(nb)
                    scale_qk(nb, 0)
                    ff_product(b, 4)
                    scale_qk(nb, 1)
                    ff_low(b, 4)
                    stack_low(nb, 0)
                    ff_product(b, 5)
                    ff_low(b, 5)
                    ff_product(b, 6)
                    scale_qk(nb, 2)
                    ff_low(b, 6)
                    stack_low(nb, 1)
                    k_turned(nb, 1)
                    k_turned(nb, 3)
                    ff_product(b, 7)
                    scale_qk(nb, 3)
                    ff_low(b, 7)
                    stack_low(nb, 2)
                    k_turned(nb, 5)
                    k_turned(nb, 7)
                    add(b, 2)
                    stack_low(nb, 3)
                    k_turned(nb, 9)
                    k_turned(nb, 11)
                    add(b, 3)
                    k_turned(nb, 13)
                    k_turned(nb, 15)

                def last_late(b):
                    h2_low(b, 0)
                    h2_low(b, 1)
                    last_round(b)
                    output_sum(b, 2)
                    output_sum(b, 3)
                    mean_square(b, 1)
                    ff_product(b, 0)
                    second_norm(b, 1)
                    for n in range(2 * FC):
                        if n < 2 * FC - 1:
                            if n == FC:
                                add(b, 0)
                                add(b, 1)
                            ff_product(b, n + 1)
                        ff_low(b, n)
                        if n == 1:
                            h2_low(b, 2)
                            h2_low(b, 3)
                    add(b, 2)
                    add(b, 3)

                dve.wait_ge(S["norm_loaded"], 32)
                dve.wait_ge(S["consts"], CONSTS)
                first_front()
                attention(0, 1)
                late(0, 1)
                with dve.Fori(1, B - 1) as b:
                    attention(b, b + 1)
                    late(b, b + 1)
                attention(B - 1, None)
                last_late(B - 1)
                dve.wait_ge(S["t2_done"], B * PAIRS)


E_N = 8
HID = 1024
HC = HID // P
TILES = B * T // P
TOPK = 2
GT = 2
GS = GT * P
GROUPS = TILES * TOPK // GT + E_N - 1
ROW = 2 * D + 4
GAIN = 64.0
HID_GAIN = 16.0
TURNS = 4
AHEAD = 1


def route(nc, t2, rows, ident, gate_w, w1, w2, w1T, w2T, expert_of):
    PER = TILES // TURNS
    CH = 4
    BANKS = 8
    each = AHEAD * BANKS // TURNS
    own = {i * PER // each: [divmod(a * each + i, BANKS) for a in range(TURNS)] for i in range(each)}
    with ExitStack() as ctx:
        s = Scope(nc, ctx, "route")
        xrow = s.sb("xrow", [P, TILES, ROW], F16)
        tok = [s.sb(f"tok{i}", [P, PER, D]) for i in range(2)]
        natural = s.sb("natural", [P, CH, 4 * D])
        gT = s.sb("gT", [P, CC, E_N])
        xT = s.sb("xT", [P, 2, CC, P])
        stats, mv = s.sb("stats", [P, PER, 6]), s.sb("mv", [P, PER, 2])
        va, vb = s.sb("va", [P, PER]), s.sb("vb", [P, PER])
        top, idx = s.sb("top", [P, PER, 8]), s.sb("idx", [P, PER, 8], U32)
        logit = s.sb("logit", [P, PER, E_N])
        idxf = s.sb("idxf", [P, TILES, TOPK])
        oh = s.sb("oh", [P, TOPK, TILES, E_N])
        member = s.sb("member", [P, TILES, E_N])
        before = s.sb("before", [P, P])
        all_ones = s.sb("all_ones", [P, P])
        iota_e = s.sb("iota_e", [P, E_N])
        iota_t = s.sb("iota_t", [P, TILES // GT])
        iota_s = s.sb("iota_s", [1, GROUPS])
        within, total = s.sb("within", [P, TILES, E_N]), s.sb("total", [P, TILES, E_N])
        scan = s.sb("scan", [P, 2, TILES, E_N])
        cmp = s.sb("cmp", [P, E_N, TILES // GT])
        groups_e = s.sb("groups_e", [P, E_N])
        esc = s.sb("esc", [P, 2, E_N])
        posf, pos = s.sb("posf", [P, TILES]), s.sb("pos", [P, TOPK, TILES], U32)
        diff, wt = s.sb("diff", [P, TILES]), s.sb("wt", [P, TOPK, TILES])
        cmp_s, sum_s = s.sb("cmp_s", [1, GROUPS, E_N - 1]), s.sb("sum_s", [1, GROUPS])

        wbank = [s.ps(f"wbank{i}", [P, 512]) for i in range(4)]
        xbank = [s.ps(f"xbank{i}", [P, 512]) for i in range(2)]
        lbank = s.ps("lbank", [P, PER, E_N])
        pbank = s.ps("pbank", [P, 2, TILES * E_N])
        names = ("consts", "gate_loaded", "tok0", "tok1", "chunk0", "chunk1", "chunk2", "chunk3", "w_full", "w_hi", "w_lo",
                 "stats_done", "var_done", "root_done", "rstd_done", "x_done", "x_hi", "x_lo", "xT_full", "xT_copied",
                 "logit_full", "logit_copied", "top_done", "idx_done", "plan", "counted", "exp_done", "choice_kept", "weights_set",
                 "pos_done", "scattered0", "scattered1", "map_done")
        S = {n: s.sem(n) for n in names}
        w1_v = w1.rearrange("e (a o p) d -> e a p o d", a=2, p=P)
        w2_v = w2.rearrange("e (a p) h -> e a p h", p=P)
        t2_v = t2.rearrange("(a t p) d -> a p t d", p=P, t=PER)

        def wdest(e, n):
            c, half = n // 2, n % 2
            if c < 2:
                return tuple(w1T[:, e, part, half, c * 512:(c + 1) * 512] for part in range(2))
            return tuple(w2T[:, e, part, half * 4:(half + 1) * 4, (c - 2) * P:(c - 1) * P] for part in range(2))

        def bank_ap(n):
            b = wbank[n % 4][:, :]
            return b if n // 2 < 2 else b.rearrange("p (h q) -> p h q", h=4)

        with nc.Block() as block:

            @block.gpsimd
            def _(pool):
                def load(a):
                    pool.dma_start(tok[a % 2][:, :, :], t2_v[a]).then_inc(S[f"tok{a % 2}"], 16)

                load(0)
                load(1)
                pool.memset(before[:, :], 1.0).then_inc(S["consts"], 1)
                pool.memset(all_ones[:, :], 1.0).then_inc(S["consts"], 1)
                pool.iota(iota_e[:, :], pattern=[[1, E_N]], base=0, channel_multiplier=0, allow_small_or_imprecise_dtypes=True).then_inc(S["consts"], 1)
                pool.iota(iota_t[:, :], pattern=[[GS, TILES // GT]], base=0, channel_multiplier=0, allow_small_or_imprecise_dtypes=True).then_inc(S["consts"], 1)
                pool.iota(iota_s[:, :], pattern=[[1, GROUPS]], base=0, channel_multiplier=0, allow_small_or_imprecise_dtypes=True).then_inc(S["consts"], 1)
                pool.iota(xrow[:, :, 2 * D:2 * D + 2].bitcast(U32).rearrange("p t a -> p (t a)"), pattern=[[P, TILES]], base=0, channel_multiplier=1).then_inc(S["consts"], 1)
                pool.wait_ge(S["consts"], 6)
                pool.affine_select(out=before[:, :], in_=before[:, :], compare_op=ALU.is_gt, fill=0.0, base=0,
                                   pattern=[[1, P]], channel_multiplier=-1).then_inc(S["consts"], 1)
                for a in range(2, TURNS):
                    pool.wait_ge(S["x_lo"], a - 1)
                    pool.wait_ge(S["xT_full"], (a - 1) * PER)
                    load(a)
                for k in range(TOPK):
                    pool.wait_ge(S["pos_done"], k + 1)
                    pool.wait_ge(S["weights_set"], 1)
                    for half in range(2):
                        ts = range(half * TILES // 2, (half + 1) * TILES // 2)
                        if k:
                            pool.wait_ge(S[f"scattered{half}"], k * len(ts) * 16)
                            own = slice(ts.start, ts.stop)
                            pool.tensor_copy(xrow[:, own, 2 * D + 2:2 * D + 4].bitcast(F32)[:, :, 0], wt[:, k, own]).then_inc(S["weights_set"], 1)
                            pool.wait_ge(S["weights_set"], 2 + half)
                        for t in ts:
                            pool.indirect_dma_start(rows, bass.IndirectOffsetOnAxis(ap=pos[:, k, t:t + 1], axis=0),
                                                    xrow[:, t, :].bitcast(U32), None).then_inc(S[f"scattered{half}"], 16)
                for half in range(2):
                    pool.wait_ge(S[f"scattered{half}"], TOPK * TILES // 2 * 16)

            CONSTS = 7

            @block.sync
            def _(sp):
                def chunk(e, c):
                    src = w1_v[e, c] if c < 2 else w2_v[e, c - 2]
                    dst = natural[:, c, :].rearrange("p (o d) -> p o d", d=D) if c < 2 else natural[:, c, :]
                    sp.dma_start(dst, src).then_inc(S[f"chunk{c}"], 16)

                for k in range(CC):
                    sp.dma_start(gT[:, k, :], gate_w[:, k * P:(k + 1) * P].rearrange("e p -> p e"), allow_slow_non_contiguous=True).then_inc(S["gate_loaded"], 16)
                for c in range(CH):
                    chunk(0, c)
                with sp.Fori(0, E_N - 1) as e:
                    for c in range(CH):
                        sp.wait_ge(S["w_full"], e * BANKS + (2 * c + 2))
                        chunk(e + 1, c)

            @block.scalar
            def _(act):
                def weight(e, n):
                    act.wait_ge(S["w_full"], e * BANKS + n + 1)
                    act.activation(wdest(e, n)[0], bank_ap(n), ACT.Copy, scale=GAIN).then_inc(S["w_hi"], 1)

                def root(a):
                    act.wait_ge(S["var_done"], a + 1)
                    act.activation(vb[:, :], va[:, :], ACT.Sqrt).then_inc(S["root_done"], 1)

                root(0)
                for a in range(TURNS):
                    for i in range(PER):
                        act.wait_ge(S["xT_full"], a * PER + i + 1)
                        if a or i > 1:
                            act.wait_ge(S["logit_full"], a * PER + i - 1)
                        act.activation(xT[:, i % 2, :, :], xbank[i % 2][:, 0:CC * P].rearrange("p (c q) -> p c q", c=CC), ACT.Copy).then_inc(S["xT_copied"], 1)
                        if i == 0:
                            act.wait_ge(S["x_done"], (a + 1) * PER)
                            act.activation(xrow[:, a * PER:(a + 1) * PER, 0:D], tok[a % 2][:, :, :], ACT.Copy, scale=GAIN).then_inc(S["x_hi"], 1)
                        if i in own:
                            weight(*own[i][a])
                        if i == 4 and a + 1 < TURNS:
                            root(a + 1)
                act.wait_ge(S["choice_kept"], 2 * TURNS)
                act.activation(wt[:, 1, :], diff[:, :], ACT.Exp).then_inc(S["exp_done"], 1)
                with act.Fori(AHEAD, E_N) as e:
                    for n in range(BANKS):
                        weight(e, n)

            @block.tensor
            def _(pe):
                def weight(e, n):
                    c, half = n // 2, n % 2
                    if half == 0:
                        pe.wait_ge(S[f"chunk{c}"], 16 * (e + 1))
                    if n > 3 or not isinstance(e, int) or e > 0:
                        pe.wait_ge(S["w_lo"], e * BANKS + (n - 3))
                    for i in range(4):
                        src = natural[:, c, i * D + half * P:i * D + (half + 1) * P] if c < 2 else natural[:, c, (half * 4 + i) * P:(half * 4 + i + 1) * P]
                        last = pe.transpose(wbank[n % 4][:, i * P:(i + 1) * P], src, ident[:, :])
                    last.then_inc(S["w_full"], 1)

                def logits(a, i):
                    pe.wait_ge(S["xT_copied"], a * PER + i + 1)
                    if i == 0 and a:
                        pe.wait_ge(S["logit_copied"], a)
                    for k in range(CC):
                        last = pe.matmul(lbank[:, i, :], xT[:, i % 2, k, :], gT[:, k, :], start=k == 0, stop=k == CC - 1)
                    last.then_inc(S["logit_full"], 1)

                pe.wait_ge(S["gate_loaded"], 16 * CC)
                for a in range(TURNS):
                    for i in range(PER):
                        pe.wait_ge(S["x_done"], a * PER + i + 1)
                        if a or i > 1:
                            pe.wait_ge(S["xT_copied"], a * PER + i - 1)
                        for k in range(CC):
                            last = pe.transpose(xbank[i % 2][:, k * P:(k + 1) * P], tok[a % 2][:, i, k * P:(k + 1) * P], ident[:, :])
                        last.then_inc(S["xT_full"], 1)
                        if i in own:
                            weight(*own[i][a])
                        if i:
                            logits(a, i - 1)
                    logits(a, PER - 1)
                pe.wait_ge(S["consts"], CONSTS)
                pe.wait_ge(S["plan"], 3)
                flat = member[:, :, :].rearrange("p t e -> p (t e)")
                pe.matmul(pbank[:, 0, :], before[:, :], flat, start=True, stop=True).then_inc(S["counted"], 1)
                pe.matmul(pbank[:, 1, :], all_ones[:, :], flat, start=True, stop=True).then_inc(S["counted"], 1)
                with pe.Fori(AHEAD, E_N) as e:
                    for n in range(BANKS):
                        weight(e, n)

            @block.vector
            def _(dve):
                def weight(e, n):
                    dve.wait_ge(S["w_hi"], e * BANKS + n + 1)
                    hi, lo = wdest(e, n)
                    dve.scalar_tensor_tensor(lo, bank_ap(n), GAIN, hi, ALU.mult, ALU.subtract).then_inc(S["w_lo"], 1)

                def variance(a):
                    dve.wait_ge(S[f"tok{a % 2}"], 16 * (a // 2 + 1))
                    for i in range(PER):
                        dve.bn_stats(stats[:, i, :], tok[a % 2][:, i, :]).then_inc(S["stats_done"], 1)
                    dve.wait_ge(S["stats_done"], a * 2 * PER + PER)
                    for i in range(PER):
                        dve.bn_aggr(mv[:, i, :], stats[:, i, :]).then_inc(S["stats_done"], 1)
                    dve.wait_ge(S["stats_done"], (a + 1) * 2 * PER)
                    dve.tensor_scalar(va[:, :], mv[:, :, 1], LN_EPS, None, ALU.add).then_inc(S["var_done"], 1)

                def normalise(a):
                    dve.wait_ge(S["root_done"], a + 1)
                    dve.reciprocal(va[:, :], vb[:, :]).then_inc(S["rstd_done"], 1)
                    dve.wait_ge(S["rstd_done"], a + 1)
                    for i in range(PER):
                        dve.tensor_scalar(tok[a % 2][:, i, :], tok[a % 2][:, i, :], mv[:, i, 0:1], va[:, i:i + 1], ALU.subtract, ALU.mult).then_inc(S["x_done"], 1)

                def low_parts(a):
                    dve.wait_ge(S["x_hi"], a + 1)
                    rs = slice(a * PER, (a + 1) * PER)
                    dve.scalar_tensor_tensor(xrow[:, rs, D:2 * D], tok[a % 2][:, :, :], GAIN, xrow[:, rs, 0:D], ALU.mult, ALU.subtract).then_inc(S["x_lo"], 1)

                def choose(a):
                    dve.wait_ge(S["logit_full"], (a + 1) * PER)
                    dve.tensor_copy(logit[:, :, :], lbank[:, :, :]).then_inc(S["logit_copied"], 1)
                    dve.wait_ge(S["logit_copied"], a + 1)
                    for i in range(PER):
                        dve.max(top[:, i, :], logit[:, i, :]).then_inc(S["top_done"], 1)
                    dve.wait_ge(S["top_done"], (a + 1) * PER)
                    for i in range(PER):
                        dve.max_index(idx[:, i, :], top[:, i, :], logit[:, i, :]).then_inc(S["idx_done"], 1)
                    dve.wait_ge(S["idx_done"], (a + 1) * PER)
                    rs = slice(a * PER, (a + 1) * PER)
                    dve.tensor_copy(idxf[:, rs, :], idx[:, :, 0:TOPK]).then_inc(S["choice_kept"], 1)
                    dve.tensor_tensor(diff[:, rs], top[:, :, 1], top[:, :, 0], ALU.subtract).then_inc(S["choice_kept"], 1)
                    dve.wait_ge(S["choice_kept"], 2 * (a + 1))

                variance(0)
                normalise(0)
                for a in range(TURNS):
                    for i in range(PER):
                        if i in own:
                            weight(*own[i][a])
                        if i == 0:
                            low_parts(a)
                        if i == 3 and a + 1 < TURNS:
                            variance(a + 1)
                    if a + 1 < TURNS:
                        normalise(a + 1)
                    choose(a)

                plan = S["plan"]
                dve.wait_ge(S["consts"], CONSTS)
                for k in range(TOPK):
                    dve.tensor_tensor(oh[:, k, :, :], idxf[:, :, k:k + 1].to_broadcast((P, TILES, E_N)),
                                      iota_e[:, :].rearrange("p (a e) -> p a e", a=1).to_broadcast((P, TILES, E_N)), ALU.is_equal).then_inc(S["map_done"], 1)
                dve.wait_ge(S["map_done"], 2)
                dve.tensor_tensor(member[:, :, :], oh[:, 0, :, :], oh[:, 1, :, :], ALU.add).then_inc(plan, 3)
                dve.wait_ge(S["exp_done"], 1)
                dve.tensor_scalar(diff[:, :], wt[:, 1, :], 1.0, None, ALU.add).then_inc(plan, 1)
                dve.wait_ge(plan, 4)
                dve.reciprocal(wt[:, 0, :], diff[:, :]).then_inc(plan, 1)
                dve.wait_ge(plan, 5)
                dve.tensor_tensor(wt[:, 1, :], wt[:, 1, :], wt[:, 0, :], ALU.mult).then_inc(plan, 1)
                wfield = xrow[:, :, 2 * D + 2:2 * D + 4].bitcast(F32)
                dve.tensor_copy(wfield[:, :, 0], wt[:, 0, :]).then_inc(S["weights_set"], 1)
                dve.wait_ge(S["counted"], 2)
                dve.tensor_copy(within[:, :, :], pbank[:, 0, :].rearrange("p (t e) -> p t e", e=E_N)).then_inc(plan, 1)
                dve.tensor_copy(total[:, :, :], pbank[:, 1, :].rearrange("p (t e) -> p t e", e=E_N)).then_inc(plan, 1)
                dve.wait_ge(plan, 8)
                dve.tensor_copy(scan[:, 0, :, :], total[:, :, :]).then_inc(plan, 1)
                n, step, at = 9, 1, 0
                while step < TILES:
                    dve.wait_ge(plan, n)
                    dve.tensor_copy(scan[:, 1 - at, 0:step, :], scan[:, at, 0:step, :]).then_inc(plan, 1)
                    dve.tensor_tensor(scan[:, 1 - at, step:TILES, :], scan[:, at, step:TILES, :], scan[:, at, 0:TILES - step, :], ALU.add).then_inc(plan, 1)
                    n, step, at = n + 2, step * 2, 1 - at
                dve.wait_ge(plan, n)
                dve.tensor_tensor(cmp[:, :, :], scan[:, at, TILES - 1, :].rearrange("p (e a) -> p e a", a=1).to_broadcast((P, E_N, TILES // GT)),
                                  iota_t[:, :].rearrange("p (a t) -> p a t", a=1).to_broadcast((P, E_N, TILES // GT)), ALU.is_gt).then_inc(plan, 1)
                dve.tensor_tensor(scan[:, 1 - at, :, :], scan[:, at, :, :], total[:, :, :], ALU.subtract).then_inc(plan, 1)
                at = 1 - at
                n += 2
                dve.wait_ge(plan, n)
                dve.tensor_reduce(groups_e[:, :], cmp[:, :, :], AX.X, ALU.add).then_inc(plan, 1)
                dve.tensor_tensor(within[:, :, :], within[:, :, :], scan[:, at, :, :], ALU.add).then_inc(plan, 1)
                n += 2
                dve.wait_ge(plan, n)
                dve.tensor_copy(esc[:, 0, :], groups_e[:, :]).then_inc(plan, 1)
                n, step, ea = n + 1, 1, 0
                while step < E_N:
                    dve.wait_ge(plan, n)
                    dve.tensor_copy(esc[:, 1 - ea, 0:step], esc[:, ea, 0:step]).then_inc(plan, 1)
                    dve.tensor_tensor(esc[:, 1 - ea, step:E_N], esc[:, ea, step:E_N], esc[:, ea, 0:E_N - step], ALU.add).then_inc(plan, 1)
                    n, step, ea = n + 2, step * 2, 1 - ea
                dve.wait_ge(plan, n)
                ends = esc[0:1, ea, 0:E_N - 1]
                dve.tensor_tensor(cmp_s[:, :, :], iota_s[:, :].rearrange("p (s a) -> p s a", a=1).to_broadcast((1, GROUPS, E_N - 1)),
                                  ends.rearrange("p (a e) -> p a e", a=1).to_broadcast((1, GROUPS, E_N - 1)), ALU.is_ge).then_inc(plan, 1)
                dve.tensor_tensor(esc[:, 1 - ea, :], esc[:, ea, :], groups_e[:, :], ALU.subtract).then_inc(plan, 1)
                n += 2
                dve.wait_ge(plan, n)
                dve.tensor_reduce(sum_s[:, :], cmp_s[:, :, :], AX.X, ALU.add).then_inc(plan, 1)
                dve.scalar_tensor_tensor(within[:, :, :], esc[:, 1 - ea, :].rearrange("p (a e) -> p a e", a=1).to_broadcast((P, TILES, E_N)), float(GS),
                                         within[:, :, :], ALU.mult, ALU.add).then_inc(plan, 1)
                n += 2
                dve.wait_ge(plan, n)
                dve.tensor_copy(expert_of[:, :], sum_s[:, :]).then_inc(plan, 1)
                n += 1
                for k in range(TOPK):
                    dve.tensor_tensor(oh[:, k, :, :], oh[:, k, :, :], within[:, :, :], ALU.mult).then_inc(plan, 1)
                    n += 1
                    dve.wait_ge(plan, n)
                    dve.tensor_reduce(posf[:, :], oh[:, k, :, :], AX.X, ALU.add).then_inc(plan, 1)
                    n += 1
                    dve.wait_ge(plan, n)
                    dve.tensor_copy(pos[:, k, :], posf[:, :]).then_inc(S["pos_done"], 1)
                    dve.wait_ge(S["pos_done"], k + 1)
                with dve.Fori(AHEAD, E_N) as e:
                    for n in range(BANKS):
                        weight(e, n)


def experts(nc, acc, rows, ident_h, b1, b2, w1T, w2T, expert_of):
    with ExitStack() as ctx:
        s = Scope(nc, ctx, "moe")
        b1T, b2r = s.sb("b1T", [P, E_N, HC]), s.sb("b2r", [P, E_N, D])
        xin = [s.sb(f"xin{i}", [P, GT, ROW], F16) for i in range(2)]
        meta = [s.sb(f"meta{i}", [P, GT, 2]) for i in range(4)]
        xT = [s.sb(f"xT{i}", [P, 2, CC, GS], F16) for i in range(2)]
        hid = [s.sb(f"hid{i}", [P, HC, GS]) for i in range(2)]
        hid_hi = [s.sb(f"hid_hi{i}", [P, HC, GS], F16) for i in range(2)]
        hid_lo = [s.sb(f"hid_lo{i}", [P, HC, GS], F16) for i in range(2)]
        y = [s.sb(f"y{i}", [P, GT, D]) for i in range(2)]
        ysum = [s.sb(f"ysum{i}", [P, GT, D]) for i in range(2)]
        turned = s.ps("turned", [P, 2 * CC, GS], F16)
        hbank = s.ps("hbank", [P, HC, GS])
        ybank = [s.ps(f"ybank{i}", [P, GT, D]) for i in range(2)]
        names = ("bias_loaded", "in0", "in1", "turned_full", "xT_done", "h_full", "gelu_done", "hi_done", "lo_done", "y_full",
                 "meta_done", "ysum_done", "y_done", "added", "passed")
        S = {n: s.sem(n) for n in names}
        rows_v = rows.rearrange("(n t p) r -> n p t r", p=P, t=GT)

        def all_tiles(eng, step):
            for j in range(3):
                step(j, j)
            with eng.Fori(0, (GROUPS - 3) // 4) as i:
                for r in range(4):
                    step(i * 4 + (3 + r), (3 + r) % 4)

        assert (GROUPS - 3) % 4 == 0

        def early(j, n):
            return isinstance(j, int) and j < n

        with nc.Block() as block:

            @block.sync
            def _(sp):
                sp.dma_start(b1T[:, :, :], b1.rearrange("e (c p) -> p e c", p=P), allow_slow_non_contiguous=True).then_inc(S["bias_loaded"], 16)
                sp.dma_start(b2r[:, :, :], b2.rearrange("(a e) d -> a e d", a=1).to_broadcast((P, E_N, D))).then_inc(S["bias_loaded"], 16)

                def step(j, r):
                    if not early(j, 2):
                        sp.wait_ge(S["turned_full"], j - 1)
                        sp.wait_ge(S["meta_done"], j - 1)
                    sp.dma_start(xin[r % 2][:, :, :].bitcast(U32), rows_v[j]).then_inc(S[f"in{r % 2}"], 16)

                all_tiles(sp, step)

            @block.gpsimd
            def _(pool):
                def step(j, r):
                    pool.wait_ge(S["y_done"], j + 1)
                    if not early(j, 1):
                        pool.wait_ge(S["added"], j * (16 * GT))
                    pool.sem_inc(S["passed"], 1)
                    for t in range(GT):
                        pool.indirect_dma_start(acc, bass.IndirectOffsetOnAxis(ap=meta[r][:, t, 0:1].bitcast(U32), axis=0),
                                                y[r % 2][:, t, :], None, compute_op=ALU.add).then_inc(S["added"], 16)

                all_tiles(pool, step)
                pool.wait_ge(S["added"], GROUPS * 16 * GT)

            @block.tensor
            def _(pe):
                def expert(j):
                    return pe.value_load(expert_of[0:1, bass.ds(j, 1)], min_val=0, max_val=E_N - 1)

                def turn(j, r):
                    q = r % 2
                    pe.wait_ge(S[f"in{q}"], (j - q) * 8 + 16)
                    if not early(j, 1):
                        pe.wait_ge(S["xT_done"], j)
                    for part in range(2):
                        for k in range(CC):
                            for t in range(GT):
                                last = pe.transpose(turned[:, part * CC + k, t * P:(t + 1) * P],
                                                    xin[q][:, t, part * D + k * P:part * D + (k + 1) * P], ident_h[:, :])
                    last.then_inc(S["turned_full"], 1)

                def up(j, r):
                    q, e = r % 2, expert(j)
                    pe.wait_ge(S["xT_done"], j + 1)
                    for c in range(HC):
                        if c % 2 == 0 and not early(j, 1):
                            pe.wait_ge(S["gelu_done"], j * HC - (HC - 2 - c))
                        n = 0
                        for wp, xp in ((0, 0), (0, 1), (1, 0)):
                            for k in range(CC):
                                last = pe.matmul(hbank[:, c, :], w1T[:, e, wp, k, c * P:(c + 1) * P], xT[q][:, xp, k, :],
                                                 start=n == 0, stop=n == 5)
                                n += 1
                        if c % 2 == 1:
                            last.then_inc(S["h_full"], 1)

                def down(j, r):
                    q, e = r % 2, expert(j)
                    pe.wait_ge(S["lo_done"], j + 1)
                    if not early(j, 2):
                        pe.wait_ge(S["ysum_done"], j - 1)
                    for t in range(GT):
                        n = 0
                        for c in range(HC):
                            for hp, wp in ((0, 0), (0, 1), (1, 0)):
                                last = pe.matmul(ybank[q][:, t, :], (hid_hi, hid_lo)[hp][q][:, c, t * P:(t + 1) * P], w2T[:, e, wp, c, :],
                                                 start=n == 0, stop=n == 3 * HC - 1)
                                n += 1
                    last.then_inc(S["y_full"], 1)

                def step(j, r):
                    turn(j + 1, (r + 1) % 4)
                    up(j, r)
                    if not early(j, 1):
                        down(j - 1, (r - 1) % 4)

                turn(0, 0)
                for j in range(3):
                    step(j, j)
                with pe.Fori(0, (GROUPS - 3) // 4 - 1) as i:
                    for r in range(4):
                        step(i * 4 + (3 + r), (3 + r) % 4)
                for j in range(GROUPS - 4, GROUPS - 1):
                    step(j, j % 4)
                up(GROUPS - 1, (GROUPS - 1) % 4)
                down(GROUPS - 2, (GROUPS - 2) % 4)
                down(GROUPS - 1, (GROUPS - 1) % 4)

            @block.scalar
            def _(act):
                act.wait_ge(S["bias_loaded"], 32)

                def step(j, r):
                    q = r % 2
                    e = act.value_load(expert_of[0:1, bass.ds(j, 1)], min_val=0, max_val=E_N - 1)
                    if not early(j, 2):
                        act.wait_ge(S["lo_done"], j - 1)
                    for c in range(HC):
                        act.wait_ge(S["h_full"], j * (HC // 2) + (c // 2 + 1))
                        act.activation(hid[q][:, c, :], hbank[:, c, :], ACT.Gelu, bias=b1T[:, e, c:c + 1],
                                       scale=1.0 / (GAIN * GAIN)).then_inc(S["gelu_done"], 1)

                all_tiles(act, step)

            @block.vector
            def _(dve):
                dve.wait_ge(S["bias_loaded"], 32)

                def tokens(j, r):
                    q = r % 2
                    dve.wait_ge(S["turned_full"], j + 1)
                    dve.tensor_copy(xT[q][:, :, :, :], turned[:, :, :].rearrange("p (a c) q -> p a c q", a=2)).then_inc(S["xT_done"], 1)
                    if not early(j, 4):
                        dve.wait_ge(S["added"], (j - 3) * (16 * GT))
                    dve.tensor_copy(meta[r][:, :, :], xin[q][:, :, 2 * D:2 * D + 4].bitcast(F32)).then_inc(S["meta_done"], 1)

                def split(j, r):
                    q = r % 2
                    dve.wait_ge(S["gelu_done"], (j + 1) * HC)
                    dve.tensor_scalar(hid_hi[q][:, :, :], hid[q][:, :, :], HID_GAIN, None, ALU.mult).then_inc(S["hi_done"], 1)
                    dve.wait_ge(S["hi_done"], j + 1)
                    dve.scalar_tensor_tensor(hid_lo[q][:, :, :], hid[q][:, :, :], HID_GAIN, hid_hi[q][:, :, :], ALU.mult, ALU.subtract).then_inc(S["lo_done"], 1)

                def out(j, r):
                    q = r % 2
                    e = dve.value_load(expert_of[0:1, bass.ds(j, 1)], min_val=0, max_val=E_N - 1)
                    dve.wait_ge(S["y_full"], j + 1)
                    dve.scalar_tensor_tensor(ysum[q][:, :, :], ybank[q][:, :, :], 1.0 / (GAIN * HID_GAIN),
                                             b2r[:, bass.ds(e, 1), :].to_broadcast((P, GT, D)), ALU.mult, ALU.add).then_inc(S["ysum_done"], 1)
                    dve.wait_ge(S["ysum_done"], j + 1)
                    if not early(j, 2):
                        dve.wait_ge(S["added"], (j - 1) * (16 * GT))
                    for t in range(GT):
                        last = dve.tensor_scalar(y[q][:, t, :], ysum[q][:, t, :], meta[r][:, t, 1:2], None, ALU.mult)
                    last.then_inc(S["y_done"], 1)

                def step(j, r):
                    tokens(j + 1, (r + 1) % 4)
                    if not early(j, 2):
                        out(j - 2, (r - 2) % 4)
                    split(j, r)

                tokens(0, 0)
                for j in range(3):
                    step(j, j)
                with dve.Fori(0, (GROUPS - 3) // 4 - 1) as i:
                    for r in range(4):
                        step(i * 4 + (3 + r), (3 + r) % 4)
                for j in range(GROUPS - 4, GROUPS - 1):
                    step(j, j % 4)
                out(GROUPS - 3, (GROUPS - 3) % 4)
                split(GROUPS - 1, (GROUPS - 1) % 4)
                out(GROUPS - 2, (GROUPS - 2) % 4)
                out(GROUPS - 1, (GROUPS - 1) % 4)
                dve.wait_ge(S["y_done"], GROUPS)


def write_out(nc, acc, out, ident):
    PER = T // P
    with ExitStack() as ctx:
        s = Scope(nc, ctx, "out")
        tok = [s.sb(f"tok{i}", [P, PER, D]) for i in range(B)]
        res = [s.sb(f"res{i}", [P, CC, T]) for i in range(2)]
        bank = [s.ps(f"bank{i}", [P, 512]) for i in range(4)]
        loaded = [s.sem(f"loaded{i}") for i in range(2 * B)]
        stored = [s.sem(f"stored{i}") for i in range(2)]
        full, copied, copied_act = (s.sem(n) for n in ("full", "copied", "copied_act"))
        src = acc[0:B * T, :].rearrange("(b t p) d -> b p t d", p=P, t=PER)
        UN = 2 * CC
        with nc.Block() as block:

            @block.sync
            def _(sp):
                for b in range(B):
                    for h in range(2):
                        ts = slice(h * PER // 2, (h + 1) * PER // 2)
                        sp.dma_start(tok[b][:, ts, :], src[b][:, ts, :]).then_inc(loaded[2 * b + h], 16)

            @block.tensor
            def _(pe):
                for b in range(B):
                    for n in range(UN):
                        c, h = n // 2, n % 2
                        pe.wait_ge(loaded[2 * b + h], 16)
                        if b:
                            pe.wait_ge((copied, copied_act)[n % 2], (b - 1) * 2 + n // 2 + 1)
                        for i in range(4):
                            last = pe.transpose(bank[n][:, i * P:(i + 1) * P], tok[b][:, h * 4 + i, c * P:(c + 1) * P], ident[:, :])
                        last.then_inc(full, 1)

            def copies(eng, copy, sem, parity):
                for b in range(B):
                    if b >= 2:
                        eng.wait_ge(stored[b % 2], 16 * CC * (b // 2))
                    for n in range(parity, UN, 2):
                        c, h = n // 2, n % 2
                        eng.wait_ge(full, b * UN + n + 1)
                        copy(res[b % 2][:, c, h * 512:(h + 1) * 512], bank[n][:, :]).then_inc(sem, 1)

            @block.vector
            def _(dve):
                copies(dve, dve.tensor_copy, copied, 0)

            @block.scalar
            def _(act):
                copies(act, lambda o, i: act.activation(o, i, ACT.Copy), copied_act, 1)

            @block.gpsimd
            def _(pool):
                for b in range(B):
                    for c in range(CC):
                        pool.wait_ge(copied, b * CC + c + 1)
                        pool.wait_ge(copied_act, b * CC + c + 1)
                        pool.dma_start(out[b, c * P:(c + 1) * P].rearrange("p h w -> p (h w)"), res[b % 2][:, c, :]).then_inc(stored[b % 2], 16)
                for i in range(2):
                    pool.wait_ge(stored[i], 16 * CC * B // 2)


def make_blank_rows(nc, blank):
    with ExitStack() as ctx:
        s = Scope(nc, ctx, "fill")
        zeroed, numbered = s.sem("zeroed"), s.sem("numbered")
        with nc.Block() as block:

            @block.gpsimd
            def _(pool):
                pool.memset(blank[:, :, :], 0.0).then_inc(zeroed, 1)
                pool.wait_ge(zeroed, 1)
                pool.iota(blank[:, :, 2 * D:2 * D + 2].bitcast(U32), pattern=[[P, GT], [0, 1]], base=B * T, channel_multiplier=1).then_inc(numbered, 1)
                pool.wait_ge(numbered, 1)
        s.clear()


def build(nc, x, p, out):
    x1 = nc.dram_tensor("x1_scratch", (B, C, T), F32).ap()
    acc = nc.dram_tensor("acc_scratch", (B * T + GT * P, D), F32).ap()
    rows = nc.dram_tensor("rows_scratch", (GROUPS * GS, ROW // 2), U32).ap()
    with ExitStack() as whole:
        s = Scope(nc, whole, "all")
        ident, ident_h = s.sb("ident", [P, P]), s.sb("ident_h", [P, P], F16)
        with ExitStack() as ctx:
            s = Scope(nc, ctx, "l0")
            group_mean = s.sb("group_mean", [P, P])
            make_constants(nc, ident, ident_h, group_mean)
            blank = s.sb("blank", [P, GT, ROW], F16)
            make_blank_rows(nc, blank)
            filled = [s.sem(f"filled{t}") for t in range(GT)]
            fills = [(rows.rearrange("(n t p) r -> t p n r", p=P, t=GT)[t],
                      blank[:, t:t + 1, :].bitcast(U32).to_broadcast((P, GROUPS, ROW // 2)), filled[t]) for t in range(GT)]
            xs, gb = s.sb("xs", [P, B, CC, T]), s.sb("gb", [P, 2, CC])
            scale, shift = s.sb("scale", [P, B, CC]), s.sb("shift", [P, B, CC])
            w = {n: (s.sb(f"w{n}_hi", [P, CC, C], F32R), s.sb(f"w{n}_lo", [P, CC, C], F32R)) for n in "qkvp"}
            x_loaded, gb_loaded = [s.sem(f"x_loaded{b}") for b in range(B)], s.sem("gb_loaded")
            loads = [(xs[:, b, c, :], x[b, c * P:(c + 1) * P].rearrange("p h w -> p (h w)"), x_loaded[b]) for b in range(B) for c in range(CC)]
            loads[CC:CC] = [(gb[:, i, :], p[f"L0_conv_norm_{n}"].rearrange("(c p) -> p c", p=P), gb_loaded) for i, n in enumerate(("gamma", "beta"))]
            bias, bias_loaded = s.sb("bias", [P, 4, CC]), s.sem("bias_loaded")
            loads[CC:CC] = [(bias[:, i, :], p[f"L0_conv_b{n}"].rearrange("(c p) -> p c", p=P), bias_loaded) for i, n in enumerate("qkvp")]
            norms = [GroupNorm(s, f"gn{i}", b0, b1, xs, x_loaded, gb, gb_loaded, group_mean, scale, shift) for i, (b0, b1) in enumerate(((0, 1), (1, B)))]
            prepare_weights(nc, "w0", [(p[f"L0_conv_w{n}"], *w[n]) for n in "qkvp"], ident, loads)
            first_group_norm(nc, norms[0])
            conv_attention(nc, xs, x1, scale, shift, norms[1], fills, ident, w, bias, bias_loaded)
            s.clear()

        token_block(nc, x1, acc[0:B * T, :], ident, ident_h, [p[f"L1_attn_{n}_w"] for n in ("q", "k", "v", "gate", "up", "down", "o")],
                    p["L1_attn_norm1_w"], p["L1_attn_norm2_w"])

        with ExitStack() as ctx:
            s = Scope(nc, ctx, "l2")
            w1T, w2T = s.sb("w1T", [P, E_N, 2, CC, HID], F16), s.sb("w2T", [P, E_N, 2, HC, D], F16)
            expert_of = s.sb("expert_of", [1, GROUPS], mybir.dt.int32)
            route(nc, acc[0:B * T, :], rows, ident, p["L1_ffn_gate_w"], p["L1_ffn_w1"], p["L1_ffn_w2"], w1T, w2T, expert_of)
            experts(nc, acc, rows, ident_h, p["L1_ffn_b1"], p["L1_ffn_b2"], w1T, w2T, expert_of)
        write_out(nc, acc, out, ident)


_INS = ["x"] + [f"L0_conv_{n}" for n in ("norm_gamma", "norm_beta", "wq", "bq", "wk", "bk", "wv", "bv", "wp", "bp")] \
    + [f"L1_attn_{n}" for n in ("q_w", "k_w", "v_w", "o_w", "gate_w", "up_w", "down_w", "norm1_w", "norm2_w")] \
    + [f"L1_ffn_{n}" for n in ("gate_w", "w1", "b1", "w2", "b2")]


def kernel(**inputs):
    import numpy as np
    from concourse import bacc
    from concourse.bass_utils import run_bass_kernel_spmd

    nc = bacc.Bacc("TRN2", target_bir_lowering=False, num_devices=1)
    arrays, args = {}, {}
    for name in _INS:
        a = np.ascontiguousarray(inputs[name])
        arrays[f"in_{name}"] = a
        args[name] = nc.dram_tensor(f"in_{name}", a.shape, mybir.dt.from_np(a.dtype), kind="ExternalInput").ap()
    out = nc.dram_tensor("out", inputs["x"].shape, F32, kind="ExternalOutput").ap()
    build(nc, args["x"], args, out)
    r = run_bass_kernel_spmd(nc, [arrays], core_ids=[0])
    return r.results[0]["out"]
```
